# Optimizing a Trainium2 kernel written in Bass

```python
import numpy as np
import jax
import jax.numpy as jnp

def _softmax(x, axis=-1):
    return jax.nn.softmax(x, axis=axis)

def _gelu(x):
    return jax.nn.gelu(x, approximate=True)

def _silu(x):
    return jax.nn.silu(x)

def _sigmoid(x):
    return jax.nn.sigmoid(x)

def _layernorm(x, axis=-1, eps=1e-05):
    m = jnp.mean(x, axis=axis, keepdims=True)
    v = jnp.var(x, axis=axis, keepdims=True)
    return (x - m) / jnp.sqrt(v + eps)

def _scatter_add(tgt, idx, src, axis=0):
    return tgt.at[idx].add(src)

def _segment_sum(src, seg, n):
    return jax.ops.segment_sum(src, seg, n)
kernel_name = 'mk_gnn_resnorm_d2_gnn_r8_d2e7c8'

def setup_inputs(seed: int=0):
    np.random.seed(seed)
    _w = jnp.asarray

    def _rec_inputs():
        import jax
        import jax.numpy as jnp
        _gk = jax.random.key(seed)
        x = -0.0005121 + 1.001 * jax.random.normal(jax.random.fold_in(_gk, 1), (6250, 64), jnp.float32)
        _s = jax.random.randint(jax.random.fold_in(_gk, 2), (100000,), 0, 6250, jnp.int32)
        _d = jax.random.randint(jax.random.fold_in(_gk, 3), (100000,), 0, 6250, jnp.int32)
        _loop = jnp.arange(6250, dtype=jnp.int32)
        src = jnp.concatenate([_s, _d, _loop])
        dst = jnp.concatenate([_d, _s, _loop])
        _o = jnp.argsort(dst, stable=True)
        src = src[_o]
        dst = dst[_o]
        edge_attr_64 = -5.16925e-05 + 1.00005 * jax.random.normal(jax.random.fold_in(_gk, 12), (206250, 64), jnp.float32)
        return (x, src, dst, edge_attr_64)
    x, src, dst, edge_attr_64 = _rec_inputs()

    def _L0_gnn_setup():
        import jax, jax.numpy as jnp
        import numpy as np
        N_NODES = 6250

        def _sage_conv(x, src, dst, W_l, b_l, W_r):
            msgs = x[src]
            agg = jax.ops.segment_sum(msgs, dst, num_segments=N_NODES)
            ones = jnp.ones((src.shape[0],), dtype=x.dtype)
            cnt = jax.ops.segment_sum(ones, dst, num_segments=N_NODES)
            agg = agg / jnp.maximum(cnt, 1.0)[:, None]
            return agg @ W_l + b_l + x @ W_r
        key = jax.random.key(seed)
        ks = jax.random.split(key, 8)
        d_in, hid, out = (64, 128, 64)
        x = jax.random.normal(ks[0], (N_NODES, d_in), dtype=jnp.float32)
        edge_index = jax.random.randint(ks[1], (2, 200000), 0, N_NODES, dtype=jnp.int64)

        def w(k, a, b):
            return jax.random.normal(k, (a, b), dtype=jnp.float32) / np.sqrt(a)
        return {'x': x, 'edge_index': edge_index, 'W_l1': w(ks[2], d_in, hid), 'b_l1': jnp.zeros((hid,), jnp.float32), 'W_r1': w(ks[3], d_in, hid), 'W_l2': w(ks[4], hid, hid), 'b_l2': jnp.zeros((hid,), jnp.float32), 'W_r2': w(ks[5], hid, hid), 'W_out': w(ks[6], hid, out), 'b_out': jnp.zeros((out,), jnp.float32)}
    _L0_gnn_all = _L0_gnn_setup()
    _L0_gnn_in = {k: v for k, v in _L0_gnn_all.items() if k in ('W_l1', 'b_l1', 'W_r1', 'W_l2', 'b_l2', 'W_r2', 'W_out', 'b_out')}
    del _L0_gnn_all

    def _L1_gnn_setup():
        import jax, jax.numpy as jnp
        import numpy as np
        N_NODES = 12500
        N_EDGES = 200000
        N_GRAPHS = 256
        NODE = 64
        EDGE = 64
        GLOB = 64
        HID = 64

        def _lin_init(key, fan_in, fan_out):
            kw, kb = jax.random.split(key)
            bound = 1.0 / np.sqrt(fan_in)
            W = jax.random.uniform(kw, (fan_in, fan_out), minval=-bound, maxval=bound, dtype=jnp.float32)
            b = jax.random.uniform(kb, (fan_out,), minval=-bound, maxval=bound, dtype=jnp.float32)
            return (W, b)
        key = jax.random.key(seed)
        ks = jax.random.split(key, 9)
        x = jax.random.normal(ks[0], (N_NODES, NODE), dtype=jnp.float32)
        edge_index = jax.random.randint(ks[1], (2, N_EDGES), 0, N_NODES, dtype=jnp.int32)
        edge_attr = jax.random.normal(ks[2], (N_EDGES, EDGE), dtype=jnp.float32)
        u = jax.random.normal(ks[3], (N_GRAPHS, GLOB), dtype=jnp.float32)
        batch = jnp.sort(jax.random.randint(ks[4], (N_NODES,), 0, N_GRAPHS, dtype=jnp.int32))
        W1a, b1a = _lin_init(ks[5], NODE + EDGE, HID)
        W1b, b1b = _lin_init(ks[6], HID, HID)
        W2a, b2a = _lin_init(ks[7], NODE + HID + GLOB, HID)
        W2b, b2b = _lin_init(ks[8], HID, NODE)
        return {'x': x, 'edge_index': edge_index, 'edge_attr': edge_attr, 'u': u, 'batch': batch, 'W1a': W1a, 'b1a': b1a, 'W1b': W1b, 'b1b': b1b, 'W2a': W2a, 'b2a': b2a, 'W2b': W2b, 'b2b': b2b}
    _L1_gnn_all = _L1_gnn_setup()
    _L1_gnn_in = {k: v for k, v in _L1_gnn_all.items() if k in ('u', 'W1a', 'b1a', 'W1b', 'b1b', 'W2a', 'b2a', 'W2b', 'b2b')}
    del _L1_gnn_all
    return {'x': x, 'src': src, 'dst': dst, 'edge_attr_64': edge_attr_64, 'L0_gnn_W_l1': _L0_gnn_in['W_l1'], 'L0_gnn_b_l1': _L0_gnn_in['b_l1'], 'L0_gnn_W_r1': _L0_gnn_in['W_r1'], 'L0_gnn_W_l2': _L0_gnn_in['W_l2'], 'L0_gnn_b_l2': _L0_gnn_in['b_l2'], 'L0_gnn_W_r2': _L0_gnn_in['W_r2'], 'L0_gnn_W_out': _L0_gnn_in['W_out'], 'L0_gnn_b_out': _L0_gnn_in['b_out'], 'L1_gnn_u': _L1_gnn_in['u'], 'L1_gnn_W1a': _L1_gnn_in['W1a'], 'L1_gnn_b1a': _L1_gnn_in['b1a'], 'L1_gnn_W1b': _L1_gnn_in['W1b'], 'L1_gnn_b1b': _L1_gnn_in['b1b'], 'L1_gnn_W2a': _L1_gnn_in['W2a'], 'L1_gnn_b2a': _L1_gnn_in['b2a'], 'L1_gnn_W2b': _L1_gnn_in['W2b'], 'L1_gnn_b2b': _L1_gnn_in['b2b']}

def reference(x, src, dst, edge_attr_64, L0_gnn_W_l1, L0_gnn_b_l1, L0_gnn_W_r1, L0_gnn_W_l2, L0_gnn_b_l2, L0_gnn_W_r2, L0_gnn_W_out, L0_gnn_b_out, L1_gnn_u, L1_gnn_W1a, L1_gnn_b1a, L1_gnn_W1b, L1_gnn_b1b, L1_gnn_W2a, L1_gnn_b2a, L1_gnn_W2b, L1_gnn_b2b):
    import jax
    import jax.numpy as jnp

    def _L0_gnn_ref(x, edge_index, W_l1, b_l1, W_r1, W_l2, b_l2, W_r2, W_out, b_out):
        import jax, jax.numpy as jnp
        import numpy as np
        N_NODES = 6250

        def _sage_conv(x, src, dst, W_l, b_l, W_r):
            msgs = x[src]
            agg = jax.ops.segment_sum(msgs, dst, num_segments=N_NODES)
            ones = jnp.ones((src.shape[0],), dtype=x.dtype)
            cnt = jax.ops.segment_sum(ones, dst, num_segments=N_NODES)
            agg = agg / jnp.maximum(cnt, 1.0)[:, None]
            return agg @ W_l + b_l + x @ W_r
        src, dst = (edge_index[0], edge_index[1])
        h = jax.nn.relu(_sage_conv(x, src, dst, W_l1, b_l1, W_r1))
        h = jax.nn.relu(_sage_conv(h, src, dst, W_l2, b_l2, W_r2))
        return h @ W_out + b_out

    def _L1_gnn_ref(x, edge_index, edge_attr, u, batch, W1a, b1a, W1b, b1b, W2a, b2a, W2b, b2b):
        import jax, jax.numpy as jnp
        import numpy as np
        N_NODES = 12500
        N_EDGES = 200000
        N_GRAPHS = 256
        NODE = 64
        EDGE = 64
        GLOB = 64
        HID = 64

        def _lin_init(key, fan_in, fan_out):
            kw, kb = jax.random.split(key)
            bound = 1.0 / np.sqrt(fan_in)
            W = jax.random.uniform(kw, (fan_in, fan_out), minval=-bound, maxval=bound, dtype=jnp.float32)
            b = jax.random.uniform(kb, (fan_out,), minval=-bound, maxval=bound, dtype=jnp.float32)
            return (W, b)
        row, col = (edge_index[0], edge_index[1])
        out = jnp.concatenate([x[row], edge_attr], axis=1)
        out = jax.nn.selu(out @ W1a + b1a) @ W1b + b1b
        summed = jax.ops.segment_sum(out, col, num_segments=x.shape[0])
        counts = jax.ops.segment_sum(jnp.ones((out.shape[0],), out.dtype), col, num_segments=x.shape[0])
        mean = summed / jnp.maximum(counts, 1.0)[:, None]
        h = jnp.concatenate([x, mean, u[batch]], axis=1)
        return jax.nn.selu(h @ W2a + b2a) @ W2b + b2b
    edge_index = jnp.stack([src, dst])
    batch0 = jnp.zeros((6250,), jnp.int32)
    x = _layernorm(x + _L0_gnn_ref(x, edge_index, L0_gnn_W_l1, L0_gnn_b_l1, L0_gnn_W_r1, L0_gnn_W_l2, L0_gnn_b_l2, L0_gnn_W_r2, L0_gnn_W_out, L0_gnn_b_out), axis=-1)
    x = _layernorm(x + _L1_gnn_ref(x, edge_index, edge_attr_64, L1_gnn_u, batch0, L1_gnn_W1a, L1_gnn_b1a, L1_gnn_W1b, L1_gnn_b1b, L1_gnn_W2a, L1_gnn_b2a, L1_gnn_W2b, L1_gnn_b2b), axis=-1)
    return x

_drawn_inputs = setup_inputs


def setup_inputs(seed=0):
    import zlib

    import numpy as np

    out = dict(_drawn_inputs(seed))
    spreads = {'L0_gnn_b_l1': (0.0, 0.1), 'L0_gnn_b_l2': (0.0, 0.1), 'L0_gnn_b_out': (0.0, 0.1)}
    factors = {'edge_attr_64': 5.861, 'L1_gnn_b1a': 8.0, 'L1_gnn_b1b': 4.547}
    for name, (base, spread) in spreads.items():
        noise = np.random.default_rng([zlib.crc32(name.encode()), seed]).standard_normal(out[name].shape)
        drawn = base * np.exp(spread * noise) if base else spread * noise
        out[name] = jnp.asarray(drawn.astype(out[name].dtype))
    for name, factor in factors.items():
        out[name] = (out[name] * factor).astype(out[name].dtype)
    return out
```

```python
from contextlib import ExitStack

import math

import concourse.bass as bass
from concourse import mybir

F32 = mybir.dt.float32
BF16 = mybir.dt.bfloat16
FP16 = mybir.dt.float16
I32 = mybir.dt.int32
I16 = mybir.dt.int16
ALU = mybir.AluOpType
ACT = mybir.ActivationFunctionType
AX_X = mybir.AxisListType.X

P = 128
N = 6250
E = 206250
F = 64
H = 128
EPS = 1e-5
ALPHA = 1.6732632423543772848170429916717
SCALE = 1.0507009873554804934193349852946
LN_ALPHA = math.log(ALPHA)

SRC_BLOCKS = -(-N // P)
GROUP = 8
CODES = SRC_BLOCKS * GROUP
CHUNKS = 3
ROW = 32
WROWS = CHUNKS * P // ROW
EPP = 51 * ROW
TROWS = P * EPP // ROW
NO_NODE = 20000

SB_GROUPS = 56
SBN = SB_GROUPS * GROUP
NSB = 14
PAIRS = NSB // 2
BODIES = 7
BG = SB_GROUPS // BODIES
BH = SRC_BLOCKS // BODIES
SLOTS = 4
CH = 112
NCH = SBN // CH
NPAD = NSB * SBN

EG = 1024
EJ = EG // P
NEG = -(-E // EG)
ETAIL = E - (NEG - 1) * EG
WIN = 64

assert NPAD >= N and SRC_BLOCKS == BODIES * BH and NCH * CH == SBN


def build(nc, x, src, dst, edge_attr, Wl1, bl1, Wr1, Wl2, bl2, Wr2, Wout, bout,
          u, W1a, b1a, W1b, b1b, W2a, b2a, W2b, b2b, out, PH=9):
    def dram(name, shape, dt):
        return nc.dram_tensor(name, shape, dt, kind="Internal").ap()

    table = dram("edge_table", [TROWS, 2 * ROW], F32)
    firsts_d = dram("first_dst", [TROWS], I16)
    A_d = dram("counts_matrix", [NSB, P, SRC_BLOCKS * SBN], FP16)
    hp_d = dram("h1_parts", [3, NPAD, H], BF16)
    h1_d = dram("h1_rows", [NPAD, H], F32)
    p_d = dram("source_terms", [NPAD, F], F32)

    with ExitStack() as ctx:
        def sb(name, shape, dt):
            return ctx.enter_context(nc.sbuf_tensor(name, shape, dt))

        def sem(name):
            return ctx.enter_context(nc.semaphore(name))

        def bank(name, shape, dt=F32):
            return ctx.enter_context(nc.psum_tensor(name, shape, dt))

        A_sb = sb("A_sb", [P, 2, SRC_BLOCKS * SBN], FP16)
        wT = CHUNKS * 8 * P // 2
        ar1 = sb("arena1", [P, 3 * SRC_BLOCKS * H // 2 + 2 * NCH * H + NCH * F], F32)
        w1 = SRC_BLOCKS * 2 * F // 2
        w2 = w1 + SRC_BLOCKS * (F + 2) // 2
        X12 = ar1[:, 0:w1].bitcast(BF16).rearrange("p (b f) -> p b f", f=2 * F)
        X3 = ar1[:, w1:w2].bitcast(BF16).rearrange("p (b f) -> p b f", f=F + 2)[:, :, 0:F + 1]
        laneT = ar1[:, w2:w2 + wT].bitcast(FP16).rearrange("p (g k) -> p g k", k=CHUNKS)
        codeT = ar1[:, w2 + wT:w2 + 2 * wT].bitcast(FP16).rearrange("p (g k) -> p g k", k=CHUNKS)
        Hsb = ar1[:, 0:3 * SRC_BLOCKS * H // 2].bitcast(BF16).rearrange("p (a b f) -> p a b f", a=3, f=H)
        wl = SLOTS * CHUNKS * P // 2
        wc = wl + SLOTS * CHUNKS * CODES // 2
        ww = wc + WROWS * 2 * ROW
        wr = ww + 2 * WROWS * ROW
        ar2 = sb("arena2", [P, max(wr + TROWS // 4, 2 * NSB * NCH * F)], F32)
        lane_hot = ar2[:, 0:wl].bitcast(FP16).rearrange("p (s n c) -> p s n c", s=SLOTS, c=CHUNKS)
        code_hot = ar2[:, wl:wc].bitcast(FP16).rearrange("p (s n c) -> p s n c", s=SLOTS, c=CHUNKS)
        win = ar2[:, wc:ww].rearrange("p (r c) -> p r c", c=2 * ROW)
        rel = ar2[:, ww:wr].rearrange("p (a n) -> p a n", a=2)
        junk = ar2[:, wr:wr + TROWS // 4].bitcast(mybir.dt.uint8)
        x2all = ar2[0:CH, 0:NSB * NCH * F].rearrange("p (m c f) -> p m c f", c=NCH, f=F)
        q2all = ar2[0:CH, NSB * NCH * F:2 * NSB * NCH * F].rearrange("p (m c f) -> p m c f", c=NCH, f=F)
        ar3 = sb("arena3", [P, max(TROWS // 2, 2 * NEG * EJ)], F32)
        firsts = ar3[:, 0:TROWS // 2].bitcast(I16)
        src_e = ar3[:, 0:NEG * EJ].bitcast(I32).rearrange("p (g j) -> p g j", j=EJ)
        dst_e = ar3[:, NEG * EJ:2 * NEG * EJ].bitcast(I32).rearrange("p (g j) -> p g j", j=EJ)
        drel = ar3[:, NEG * EJ:2 * NEG * EJ].rearrange("p (g j) -> p g j", j=EJ)
        rows12 = sb("rows12", [P, 1, WROWS], I32)
        below = sb("below", [P, 8], F32)
        start = sb("start", [P, 8], F32)
        iota_code = sb("iota_code", [P, CODES, CHUNKS], FP16)
        iota_i = sb("iota_i", [P, 512], I32)
        iota_w = sb("iota_w", [P, WIN], F32)
        thr = sb("thr", [P, 8], F32)
        code0 = sb("code0", [P, 8], F32)
        ident = sb("ident", [P, P], F32)
        zrow = sb("zrow", [P, 512], BF16)
        aggS = sb("aggS", [P, 2, SBN], F32)
        agg3S = sb("agg3S", [F + 1, 2, SBN], F32)
        xm = sb("xm", [CH, 2, NCH, F], F32)
        xTs = sb("xTs", [P, SBN], F32)
        Wl1s = sb("Wl1s", [P, H], F32)
        Wr1s = sb("Wr1s", [F, H], F32)
        cnt_sel = sb("cnt_sel", [F + 1, 1], F32)
        bl1s = sb("bl1s", [CH, H], F32)
        ctmp = sb("ctmp", [CH, NCH], F32)
        inv_c = sb("inv_c", [CH, NCH], F32)
        inv = sb("inv", [CH, NSB, NCH], F32)
        hs = sb("hs", [CH, NCH, H], F32)
        ht = sb("ht", [CH, NCH, H], F32)
        hv = sb("hv", [CH, NCH, H], F32)
        hpart = sb("hpart", [CH, 3, NCH, H], BF16)
        Wl2s, Wr2s = sb("Wl2s", [H, H], F32), sb("Wr2s", [H, H], F32)
        Wouts = sb("Wouts", [H, F], F32)
        bl2s, bouts = sb("bl2s", [CH, H], F32), sb("bouts", [CH, F], F32)
        Wxx = sb("Wxx", [F, 2 * F], F32)
        Wedge = sb("Wedge", [P, 2 * F], F32)
        W1bs, W2am, W2au, W2bs = (sb(n, [F, F], F32) for n in ("W1bs", "W2am", "W2au", "W2bs"))
        b1as, b2as, b2bs = (sb(n, [CH, F], F32) for n in ("b1as", "b2as", "b2bs"))
        b1bcol, u0 = sb("b1bcol", [F, 1], F32), sb("u0", [F, 1], F32)
        u0b = sb("u0b", [F, CH], F32)
        shift_b = sb("shift_b", [F, CH], F32)
        WbT = sb("WbT", [F, F + 1], F32)
        Wc = sb("Wc", [F + 1, F], F32)
        c2 = sb("c2", [CH, F], F32)
        ln_alpha = sb("ln_alpha", [P, 1], F32)
        eps_t = sb("eps_t", [P, 1], F32)
        base_i = sb("base_i", [1, NEG], I32)
        base_f = sb("base_f", [1, NEG], F32)
        ones_r = sb("ones_r", [1, P], F32)

        A_raw = A_sb[:, :, :].rearrange("p a b -> p (a b)")

        def over(at, n, dt):
            return A_raw[:, at // 2:(at + n * 4) // 2].bitcast(dt)

        src_i = over(0, EPP, I32)
        dst_i = over(4 * EPP, EPP, I32)
        lane_i = over(8 * EPP, EPP, I32)
        blk_i = over(12 * EPP, EPP, I32)
        grp_i = over(16 * EPP, EPP, I32)
        pos_i = over(20 * EPP, EPP, I32)
        comb = over(24 * EPP, 2 * EPP, F32).rearrange("p (r c) -> p r c", c=2 * ROW)
        code_a = over(32 * EPP, EPP, F32)
        x_rows = over(36 * EPP, SRC_BLOCKS * F, F32)
        x_rest = over(36 * EPP + 4 * SRC_BLOCKS * F, SRC_BLOCKS * F, F32)
        at = [0]

        def edge_buf(n, parts=P):
            w = A_raw[0:parts, 2 * at[0]:2 * (at[0] + n)].bitcast(F32)
            at[0] += n
            return w

        NB = 3
        acc = edge_buf(N + WIN, F + 1)
        attr = [edge_buf(EJ * F) for _ in range(NB)]
        gath = [edge_buf(EJ * F) for _ in range(NB)]
        attrT = [edge_buf(EJ * F) for _ in range(NB)]
        zs = edge_buf(EJ * F)
        ex = edge_buf(EJ * F)
        rl = edge_buf(EJ * F)
        msg = [edge_buf(EJ * (F + 1)).rearrange("p (j f) -> p j f", j=EJ) for _ in range(NB)]
        hot = [edge_buf(EJ * WIN).rearrange("p (j n) -> p j n", j=EJ) for _ in range(NB)]
        accS = [edge_buf(SBN, F + 1) for _ in range(2)]
        assert at[0] * 4 <= 4 * SRC_BLOCKS * SBN
        f16 = over(36 * EPP + 8 * SRC_BLOCKS * F, TROWS // P, I32).bitcast(I16)[:, 0:TROWS // P]

        hw = 3 * SRC_BLOCKS * H // 2
        h1m = [ar1[0:CH, hw + i * NCH * H:hw + (i + 1) * NCH * H].rearrange("p (c f) -> p c f", f=H) for i in range(2)]
        g2S = aggS[:, 0, :]
        h2T = aggS[:, 1, :]
        x2T = agg3S[0:F, 0, :]
        hTs = xTs
        yv = sb("yv", [CH, NCH, F], F32)
        yd = sb("yd", [CH, NCH, F], F32)
        x2c = ar1[0:CH, hw + 2 * NCH * H:hw + 2 * NCH * H + NCH * F].rearrange("p (c f) -> p c f", f=F)
        pc = iota_i[0:CH, 0:NCH * F].bitcast(F32).rearrange("p (c f) -> p c f", f=F)
        st = sb("st", [CH, 4, NCH], F32)
        hr = iota_i[0:CH, :].bitcast(F32).rearrange("p (c f) -> p c f", f=H)
        zero_c = sb("zero_c", [CH, NCH], F32)
        src_cur = [sb(f"src_cur{i}", [P, EJ], I32) for i in range(NB)]
        ex4, rl4, yv4, zm4, msg4 = (b[0:CH, 0:NCH * F] for b in (ex, rl, gath[0], gath[1], gath[2]))
        cnt_ps = [bank(f"cnt_ps{i}", [P, 512]) for i in range(2)]
        agg_ps = bank("agg_ps", [P, 512])
        agg3_ps = bank("agg3_ps", [P, 512])
        u_ps = bank("u_ps", [P, 512])
        v_ps = bank("v_ps", [P, 512])
        t_ps = bank("t_ps", [P, 512])
        t2_ps = bank("t2_ps", [P, 512])

        pads_set = sem("pads_set")
        dst_in, src_in, x_in, w_in, w2_in = sem("dst_in"), sem("src_in"), sem("x_in"), sem("w_in"), sem("w2_in")
        iota_set = sem("iota_set")
        consts = sem("consts")
        firsts_made, firsts_out, firsts_in = sem("firsts_made"), sem("firsts_out"), sem("firsts_in")
        table_made, table_out = sem("table_made"), sem("table_out")
        x1_made = sem("x1_made")
        dve0 = sem("dve0")
        rows_ready, win_in, rel_ready, win_turned, win_moved = (sem(n) for n in (
            "rows_ready", "win_in", "rel_ready", "win_turned", "win_moved"))
        win_dve = sem("win_dve")
        hot_ready = sem("hot_ready")
        groups_summed = sem("groups_summed")
        counts_moved = sem("counts_moved")
        agg_ready, agg_moved = sem("agg_ready"), sem("agg_moved")
        A_stored = [sem("A_stored0"), sem("A_stored1")]
        xm_in = [sem("xm_in0"), sem("xm_in1")]
        xT_ready, xT_moved, uv_ready, layer_dve, h_ready, h_split, h_stored = (sem(n) for n in (
            "xT_ready", "xT_moved", "uv_ready", "layer_dve", "h_ready", "h_split", "h_stored"))
        pool_at, act_at, pe_at, dve_at = sem("pool_at"), sem("act_at"), sem("pe_at"), sem("dve_at")
        pool_dep, idx_made, zm_made = sem("pool_dep"), sem("idx_made"), sem("zm_made")
        parts_in = sem("parts_in")
        A_in = [sem("A_in0"), sem("A_in1")]
        hx_in = [sem("hx_in0"), sem("hx_in1")]
        (agg2_ready, agg2_moved, hT_turned, hT_moved, u2_ready, v2_ready, h2_ready, h2_turned, h2_moved, o_ready,
         var_ready, std_ready, x2_ready, x2_kept, x2_turned, x2_moved, pq_ready, p_ready, p_stored, dve2) = (
            sem(n) for n in ("agg2_ready", "agg2_moved", "hT_turned", "hT_moved", "u2_ready", "v2_ready", "h2_ready",
                             "h2_turned", "h2_moved", "o_ready", "var_ready", "std_ready", "x2_ready", "x2_kept",
                             "x2_turned", "x2_moved", "pq_ready", "p_ready", "p_stored", "dve2"))
        edges_in, base_in, base_made, bases_ready = sem("edges_in"), sem("base_in"), sem("base_made"), sem("bases_ready")
        drel_made, acc_zero, ones_set = sem("drel_made"), sem("acc_zero"), sem("ones_set")
        wt_turned, wt_moved, wts_ready, wts_made = sem("wt_turned"), sem("wt_moved"), sem("wts_ready"), sem("wts_made")
        attr_in = [sem(f"attr_in{i}") for i in range(3)]
        gath_in = [sem(f"gath_in{i}") for i in range(3)]
        (attr_turned, attr_moved, z_ready, z_made, selu_act, hot_made, msg_made, seg_ready, acc_added) = (sem(n) for n in (
            "attr_turned", "attr_moved", "z_ready", "z_made", "selu_act", "hot_made", "msg_made", "seg_ready",
            "acc_added"))
        (accS_moved, m_ready, dve4, zq_made, selu4, msg4_made, msg4_turned, msg4_moved, y_ready, var4, std4, row_made,
         row_stored) = (sem(n) for n in (
            "accS_moved", "m_ready", "dve4", "zq_made", "selu4", "msg4_made", "msg4_turned", "msg4_moved", "y_ready",
            "var4", "std4", "row_made", "row_stored"))

        block = ctx.enter_context(nc.Block())
        full = E // EPP
        tail = E - full * EPP
        whole = N // P

        def Asb(half):
            return A_sb[:, half, :].rearrange("p (b n) -> p b n", n=SBN)

        def by_node(t, m):
            return t[bass.ds(m * SBN, SBN), :].rearrange("(c q) f -> q c f", q=CH)

        LAST = (NSB - 1) * SBN
        LCH = (N - LAST) // CH
        LREST = N - LAST - LCH * CH

        @block.sync
        def _(sp):
            sp.wait_ge(pads_set, 2)
            sp.dma_start(dst_i[0:full, :], dst[0:full * EPP].rearrange("(p j) -> p j", j=EPP)).then_inc(dst_in, 16)
            sp.dma_start(dst_i[full:full + 1, 0:tail], dst[full * EPP:E].rearrange("(p j) -> p j", p=1)).then_inc(dst_in, 16)
            sp.dma_start(src_i[0:full, :], src[0:full * EPP].rearrange("(p j) -> p j", j=EPP)).then_inc(src_in, 16)
            sp.dma_start(src_i[full:full + 1, 0:tail], src[full * EPP:E].rearrange("(p j) -> p j", p=1)).then_inc(src_in, 16)
            xr3 = x_rows.rearrange("p (b f) -> p b f", f=F)
            sp.wait_ge(pads_set, 3)
            sp.dma_start(xr3[:, 0:whole, :], x[0:whole * P, :].rearrange("(b p) f -> p b f", p=P)).then_inc(x_in, 16)
            sp.dma_start(xr3[0:N - whole * P, whole, :], x[whole * P:N, :]).then_inc(x_in, 16)
            for half in range(2):
                sp.dma_start(Wl1s[half * F:(half + 1) * F, :], Wl1).then_inc(w_in, 16)
            sp.dma_start(Wr1s[:, :], Wr1).then_inc(w_in, 16)
            sp.dma_start(bl1s[:, :], bl1.partition_broadcast(CH)).then_inc(w_in, 16)
            sp.wait_ge(firsts_made, 1)
            sp.dma_start(firsts_d.rearrange("(p r) -> p r", p=P), f16).then_inc(firsts_out, 16)
            sp.wait_ge(firsts_out, 16)
            sp.dma_start(firsts, firsts_d.partition_broadcast(P)).then_inc(firsts_in, 16)
            sp.wait_ge(table_made, 1)
            sp.dma_start(table.rearrange("(p r) c -> p (r c)", p=P), comb.rearrange("p r c -> p (r c)")).then_inc(table_out, 16)
            for to, frm in ((Wl2s, Wl2), (Wr2s, Wr2), (Wouts, Wout), (bl2s, bl2.partition_broadcast(CH)),
                            (bouts, bout.partition_broadcast(CH)), (Wxx[:, 0:F], W1a[0:F, :]), (Wxx[:, F:2 * F], W2a[0:F, :]),
                            (W1bs, W1b), (W2am, W2a[F:2 * F, :]), (W2au, W2a[2 * F:3 * F, :]), (W2bs, W2b),
                            (b1as, b1a.partition_broadcast(CH)), (b2as, b2a.partition_broadcast(CH)),
                            (b2bs, b2b.partition_broadcast(CH)), (b1bcol, b1b.rearrange("(f a) -> f a", a=1)),
                            (u0, u[0:1, :].rearrange("a f -> f a"))):
                sp.dma_start(to if isinstance(to, bass.AP) else to[:, :], frm).then_inc(w2_in, 16)
            sp.wait_ge(pads_set, 4)
            for half in range(2):
                sp.dma_start(Wedge[half * F:(half + 1) * F, half * F:(half + 1) * F], W1a[F:2 * F, :]).then_inc(w2_in, 16)

            def store_h(m, half):
                sp.wait_ge(h_split, m + 1)
                sp.dma_start(by_node(h1_d, m), hs[:, :, :]).then_inc(h_stored, 16)
                for part in range(3):
                    sp.dma_start(by_node(hp_d[part], m), hpart[:, part, :, :]).then_inc(h_stored, 16)

            def superblock(s, half, layer):
                if layer:
                    if not isinstance(s, int):
                        sp.wait_ge(xT_ready, s - 3)
                    sp.dma_start(xm[:, half, :, :], by_node(x, s - 2)).then_inc(xm_in[half], 16)
                sp.wait_ge(counts_moved, (s + 1) * SB_GROUPS + 2)
                sp.dma_start(A_d[bass.ds(s, 1), :, :].rearrange("a p n -> (a p) n"), A_sb[:, half, :]).then_inc(A_stored[half], 16)
                if layer:
                    store_h(s - 2, half)

            superblock(0, 0, False)
            superblock(1, 1, False)
            superblock(2, 0, True)
            superblock(3, 1, True)
            with sp.Fori(2, PAIRS) as pair:
                superblock(pair * 2, 0, True)
                superblock(pair * 2 + 1, 1, True)
            sp.wait_ge(xT_ready, NSB - 3)
            sp.dma_start(xm[:, 0, :, :], by_node(x, NSB - 2)).then_inc(xm_in[0], 16)
            sp.wait_ge(xT_ready, NSB - 2)

            def last_rows(rows, done):
                sp.dma_start(rows[:, 0:LCH, :], x[LAST:LAST + LCH * CH, :].rearrange("(c q) f -> q c f", q=CH)).then_inc(done, 16)
                sp.dma_start(rows[0:LREST, LCH, :], x[LAST + LCH * CH:N, :]).then_inc(done, 16)
            last_rows(xm[:, 1], xm_in[1])
            store_h(NSB - 2, 0)
            sp.wait_ge(firsts_in, 16)
            sp.wait_ge(rows_ready, PAIRS + 1)
            sp.wait_ge(pads_set, 6)
            gE = NEG - 1
            for to, frm in ((src_e, src), (dst_e, dst)):
                sp.dma_start(to[:, 0:gE, :], frm[0:gE * EG].rearrange("(g p j) -> p g j", p=P, j=EJ)).then_inc(edges_in, 16)
                sp.dma_start(to[0:ETAIL // EJ, gE, :], frm[gE * EG:gE * EG + ETAIL // EJ * EJ].rearrange("(p j) -> p j", j=EJ)).then_inc(edges_in, 16)
                sp.dma_start(to[ETAIL // EJ:ETAIL // EJ + 1, gE, 0:ETAIL % EJ], frm[gE * EG + ETAIL // EJ * EJ:E].rearrange("(p j) -> p j", p=1)).then_inc(edges_in, 16)
            with nc.allow_non_contiguous_dma(reason="one destination of every 1024"):
                sp.dma_start(base_i[0:1, 0:gE], dst[0:gE * EG].rearrange("(a g q) -> a g q", a=1, q=EG)[:, :, 0]).then_inc(base_in, 16)
            sp.dma_start(base_i[0:1, gE:NEG], dst[gE * EG:gE * EG + 1].rearrange("(a g) -> a g", a=1)).then_inc(base_in, 16)
            store_h(NSB - 1, 1)

            sp.wait_ge(A_stored[0], 16 * PAIRS)
            sp.wait_ge(A_stored[1], 16 * PAIRS)
            sp.wait_ge(h_stored, 64 * NSB)
            sp.wait_ge(agg_ready, NSB)
            sp.dma_start(A_sb[:, 0, :], A_d[0]).then_inc(A_in[0], 16)
            for part in range(3):
                sp.dma_start(Hsb[:, part], hp_d[part, 0:SRC_BLOCKS * P, :].rearrange("(b p) f -> p b f", p=P)).then_inc(parts_in, 16)
            sp.dma_start(A_sb[:, 1, :], A_d[1]).then_inc(A_in[1], 16)

            def load_hx(m, half):
                sp.dma_start(h1m[half][:, :, :], by_node(h1_d, m)).then_inc(hx_in[half], 16)
                sp.dma_start(xm[:, half, :, :], by_node(x, m)).then_inc(hx_in[half], 16)

            load_hx(0, 0)

            def superblock2(s, half):
                sp.wait_ge(agg2_ready, s)
                if not (isinstance(s, int) and s == NSB - 1):
                    sp.dma_start(A_sb[:, 1 - half, :], A_d[bass.ds(s + 1, 1), :, :].rearrange("a p n -> (a p) n")).then_inc(A_in[1 - half], 16)
                    sp.wait_ge(x2_ready, s + 1)
                    load_hx(s, half)
                else:
                    sp.wait_ge(x2_ready, NSB)
                    sp.dma_start(h1m[1][:, :, :], by_node(h1_d, NSB - 1)).then_inc(hx_in[1], 16)
                    last_rows(xm[:, 1], hx_in[1])
                sp.wait_ge(p_ready, s)
                sp.dma_start(by_node(p_d, s - 1), pc[:, :, :]).then_inc(p_stored, 16)

            with sp.Fori(0, PAIRS - 1) as j:
                superblock2(j * 2 + 1, 1)
                superblock2(j * 2 + 2, 0)
            superblock2(NSB - 1, 1)
            sp.wait_ge(p_ready, NSB)
            sp.dma_start(by_node(p_d, NSB - 1), pc[:, :, :]).then_inc(p_stored, 16)

            sp.wait_ge(agg2_ready, NSB)

            def load_attr(g, k):
                sp.dma_start(attr[k], edge_attr[bass.ds(g * EG, EG), :].rearrange("(p j) f -> p (j f)", p=P)).then_inc(attr_in[k], 16)
            for k in range(NB):
                load_attr(k, k)
            with sp.Fori(1, gE // NB) as r:
                for k in range(NB):
                    sp.wait_ge(attr_turned, r * NB + (k - NB + 1))
                    load_attr(r * NB + k, k)
            sp.wait_ge(attr_turned, gE - NB + 1)
            te = gE * EG
            sp.dma_start(attr[0][0:ETAIL // EJ, :], edge_attr[te:te + ETAIL // EJ * EJ, :].rearrange("(p j) f -> p (j f)", j=EJ)).then_inc(attr_in[0], 16)
            sp.dma_start(attr[0][ETAIL // EJ:ETAIL // EJ + 1, 0:ETAIL % EJ * F], edge_attr[te + ETAIL // EJ * EJ:E, :].rearrange("(p j) f -> p (j f)", p=1)).then_inc(attr_in[0], 16)

            with sp.Fori(0, NSB - 1) as m:
                sp.wait_ge(row_made, m + 1)
                sp.dma_start(by_node(out, m), yv[:, :, :]).then_inc(row_stored, 16)
            sp.wait_ge(row_made, NSB)
            sp.dma_start(out[LAST:LAST + LCH * CH, :].rearrange("(c q) f -> q c f", q=CH), yv[:, 0:LCH, :]).then_inc(row_stored, 16)
            sp.dma_start(out[LAST + LCH * CH:N, :], yv[0:LREST, LCH, :]).then_inc(row_stored, 16)
            sp.wait_ge(row_stored, 16 * (NSB + 1))

        @block.gpsimd
        def _(pool):
            pool.memset(src_i, 0).then_inc(pads_set, 1)
            pool.memset(dst_i, NO_NODE).then_inc(pads_set, 1)
            pool.memset(x_rows, 0.0).then_inc(pads_set, 1)
            pool.memset(Wedge[:, :], 0.0).then_inc(pads_set, 1)
            pool.iota(iota_i[:, :], [[1, 512]], 0, 0).then_inc(iota_set, 1)
            pool.memset(ident[:, :], 0.0).then_inc(iota_set, 1)
            pool.memset(zrow[:, :], 0.0).then_inc(iota_set, 1)
            pool.memset(X3[:, :, F:F + 1], 1.0).then_inc(iota_set, 1)
            pool.memset(cnt_sel[:, :], 0.0).then_inc(iota_set, 1)
            pool.wait_ge(iota_set, 5)
            pool.affine_select(out=ident[:, :], in_=ident[:, :], compare_op=ALU.not_equal, fill=1.0,
                               base=0, pattern=[[-1, P]], channel_multiplier=1).then_inc(iota_set, 1)
            pool.affine_select(out=cnt_sel[:, :], in_=cnt_sel[:, :], compare_op=ALU.not_equal, fill=1.0,
                               base=-F, pattern=[[0, 1]], channel_multiplier=1).then_inc(iota_set, 1)
            pool.iota(thr[:, :], [[GROUP * P, 8]], 0, GROUP, allow_small_or_imprecise_dtypes=True).then_inc(iota_set, 1)
            pool.iota(code0[:, :], [[P, 8]], 0, 1, allow_small_or_imprecise_dtypes=True).then_inc(iota_set, 1)
            pool.memset(shift_b[:, :], -SCALE * ALPHA).then_inc(ones_set, 1)
            pool.memset(ln_alpha[:, :], LN_ALPHA).then_inc(ones_set, 1)
            pool.memset(eps_t[:, :], EPS).then_inc(ones_set, 1)
            pool.memset(ones_r[:, :], 1.0).then_inc(ones_set, 1)
            pool.wait_ge(table_out, 16)

            def gather_windows(n):
                pool.wait_ge(rows_ready, n + 1)
                pool.sem_inc(pool_at, 1)
                for j in range(WROWS):
                    pool.indirect_dma_start(
                        out=win[:, j, :], out_offset=None, in_=table,
                        in_offset=bass.IndirectOffsetOnAxis(ap=rows12[:, 0, j:j + 1], axis=0)).then_inc(win_in, 16)

            def split_h(m):
                pool.wait_ge(h_ready, m + 1)
                pool.wait_ge(h_stored, m * 64)
                pool.sem_inc(pool_at, 1)
                seq = [lambda: pool.tensor_copy(hpart[:, 0], hs[:, :, :]),
                       lambda: pool.tensor_tensor(hr[:, :, :], hs[:, :, :], hpart[:, 0], ALU.subtract),
                       lambda: pool.tensor_copy(hpart[:, 1], hr[:, :, :]),
                       lambda: pool.tensor_tensor(hr[:, :, :], hr[:, :, :], hpart[:, 1], ALU.subtract),
                       lambda: pool.tensor_copy(hpart[:, 2], hr[:, :, :])]
                for i, op in enumerate(seq):
                    if i < 4:
                        op().then_inc(pool_dep, 1)
                        pool.wait_ge(pool_dep, m * 4 + (i + 1))
                        pool.sem_inc(pool_at, 1)
                    else:
                        op().then_inc(h_split, 1)

            gather_windows(0)
            pool.wait_ge(win_turned, 1)
            gather_windows(1)
            pool.wait_ge(win_turned, 2)
            gather_windows(2)
            split_h(0)
            split_h(1)
            with pool.Fori(2, PAIRS) as pair:
                pool.wait_ge(win_turned, pair + 1)
                pool.sem_inc(pool_at, 1)
                gather_windows(pair + 1)
                split_h(pair * 2 - 2)
                split_h(pair * 2 - 1)
            pool.wait_ge(rows_ready, PAIRS + 1)
            pool.memset(src_e[:, NEG - 1, :], 0).then_inc(pads_set, 1)
            pool.memset(dst_e[:, NEG - 1, :], NO_NODE).then_inc(pads_set, 1)
            split_h(NSB - 2)
            split_h(NSB - 1)

            pool.wait_ge(hot_ready, NSB * SB_GROUPS)
            pool.wait_ge(groups_summed, NSB * SB_GROUPS + SLOTS)
            pool.wait_ge(win_turned, PAIRS + 1)
            with pool.Fori(0, NSB) as m:
                pool.wait_ge(x2_ready, m + 3)
                pool.sem_inc(pool_at, 1)
                pool.tensor_copy(x2all[:, bass.ds(m, 1), :, :].rearrange("p a c f -> p (a c) f"), x2c[:, :, :]).then_inc(x2_kept, 1)

            pool.wait_ge(agg2_ready, NSB)
            pool.memset(acc[:, :], 0.0).then_inc(acc_zero, 1)
            for k in range(NB):
                pool.memset(msg[k][:, :, F:F + 1], 1.0).then_inc(acc_zero, 1)
            pool.wait_ge(edges_in, 96)
            pool.wait_ge(p_stored, 16 * NSB)

            def gather(g, k):
                for j in range(EJ):
                    pool.indirect_dma_start(
                        out=gath[k][:, j * F:(j + 1) * F], out_offset=None, in_=p_d,
                        in_offset=bass.IndirectOffsetOnAxis(ap=src_cur[k][:, j:j + 1], axis=0)).then_inc(gath_in[k], 16)

            for k in range(NB):
                pool.wait_ge(idx_made, k + 1)
                gather(k, k)
            with pool.Fori(1, (NEG - 1) // NB) as r:
                for k in range(NB):
                    pool.wait_ge(z_made, r * NB + (k - NB + 1))
                    pool.wait_ge(idx_made, r * NB + (k + 1))
                    pool.sem_inc(pool_at, 1)
                    gather(r * NB + k, k)
            pool.wait_ge(z_made, NEG - NB)
            pool.wait_ge(idx_made, NEG)
            gather(NEG - 1, 0)

        @block.scalar
        def _(act):
            act.wait_ge(iota_set, 9)
            act.activation(iota_code[:, :, :], iota_i[:, 0:CODES].unsqueeze(2).to_broadcast([P, CODES, CHUNKS]), ACT.Copy, bias=1.0).then_inc(consts, 1)
            act.activation(iota_w[:, :], iota_i[:, 0:WIN], ACT.Copy).then_inc(consts, 1)
            act.wait_ge(x_in, 32)
            act.activation(X12[:, :, 0:F], x_rows.rearrange("p (b f) -> p b f", f=F), ACT.Copy).then_inc(x1_made, 1)

            def move_windows(n):
                act.wait_ge(win_turned, n + 1)
                act.sem_inc(act_at, 1)
                cols = bass.ds(n * P, P)
                act.activation(laneT[:, cols, :], t_ps[:, 0:CHUNKS * P].rearrange("p (k g) -> p g k", g=P), ACT.Copy).then_inc(win_moved, 1)
                act.activation(codeT[:, cols, :], t2_ps[:, 0:CHUNKS * P].rearrange("p (k g) -> p g k", g=P), ACT.Relu).then_inc(win_moved, 1)

            def move_xT(m):
                act.wait_ge(xT_ready, m + 1)
                act.activation(xTs[0:F, :], t_ps[0:F, 0:SBN], ACT.Copy).then_inc(xT_moved, 1)

            def move_agg(s, half):
                act.wait_ge(agg_ready, s + 1)
                act.activation(aggS[:, half, :], agg_ps[:, 0:SBN], ACT.Copy).then_inc(agg_moved, 1)
                act.activation(agg3S[:, half, :], agg3_ps[0:F + 1, 0:SBN], ACT.Copy).then_inc(agg_moved, 1)

            def superblock(s, half, mult=True, layer=True):
                dest = Asb(half)
                with act.Fori(0, BODIES) as b:
                    for k in range(BG):
                        act.wait_ge(groups_summed, (s * BODIES + b) * BG + (k + 1 + SLOTS))
                        act.sem_inc(act_at, 1)
                        act.activation(dest[:, :, bass.ds((b * BG + k) * GROUP, GROUP)],
                                       cnt_ps[k % 2][:, 0:CODES].rearrange("p (b j) -> p b j", j=GROUP),
                                       ACT.Copy).then_inc(counts_moved, 1)
                if mult:
                    move_agg(s - 1, 1 - half)
                if layer:
                    move_xT(s - 2)

            move_windows(0)
            superblock(0, 0, False, False)
            move_windows(1)
            superblock(1, 1, True, False)

            def pair_of(pair):
                act.wait_ge(A_stored[0], pair * 16)
                act.sem_inc(act_at, 1)
                superblock(pair * 2, 0)
                move_windows(pair + 1)
                act.wait_ge(A_stored[1], pair * 16)
                act.sem_inc(act_at, 1)
                superblock(pair * 2 + 1, 1)
            with act.Fori(1, PAIRS) as pair:
                pair_of(pair)
            move_xT(NSB - 2)
            move_agg(NSB - 1, 1)
            move_xT(NSB - 1)

            act.wait_ge(wt_turned, 1)
            act.activation(WbT[:, 0:F], t_ps[0:F, 0:F], ACT.Copy, scale=SCALE).then_inc(wt_moved, 1)

            def layer2(m, s=None):
                act.wait_ge(hT_turned, m + 1)
                act.activation(hTs[:, :], t_ps[:, 0:SBN], ACT.Copy).then_inc(hT_moved, 1)
                act.wait_ge(h2_turned, m + 1)
                act.activation(h2T, t2_ps[:, 0:SBN], ACT.Copy).then_inc(h2_moved, 1)
                act.wait_ge(var_ready, m + 1)
                act.activation(st[:, 3, :], st[:, 2, :], ACT.Sqrt, bias=eps_t[0:CH, 0:1], scale=1.0 / F).then_inc(std_ready, 1)
                act.wait_ge(x2_turned, m + 1)
                act.activation(x2T, cnt_ps[1][0:F, 0:SBN], ACT.Copy).then_inc(x2_moved, 1)
                if s is not None:
                    move_agg2(s)

            def move_agg2(s):
                act.wait_ge(agg2_ready, s + 1)
                act.activation(g2S, agg_ps[:, 0:SBN], ACT.Copy).then_inc(agg2_moved, 1)

            move_agg2(0)
            with act.Fori(1, NSB) as s:
                layer2(s - 1, s)
            layer2(NSB - 1)

            def indices(g, k):
                act.activation(src_cur[k][:, :], src_e[:, bass.ds(g, 1), :].rearrange("p a j -> p (a j)"), ACT.Copy).then_inc(idx_made, 1)

            def edge_group(g, k, ahead=True):
                act.wait_ge(attr_turned, g + 1)
                act.activation(attrT[k], t_ps[:, 0:EJ * F], ACT.Copy).then_inc(attr_moved, 1)
                act.wait_ge(z_made, g + 1)
                act.activation(ex, zs, ACT.Exp, bias=ln_alpha[:, 0:1]).then_inc(selu_act, 1)
                act.activation(rl, zs, ACT.Relu).then_inc(selu_act, 1)
                if ahead:
                    indices(g + NB, k)

            act.wait_ge(edges_in, 96)
            for k in range(NB):
                indices(k, k)
            with act.Fori(0, (NEG - 1) // NB - 1) as r:
                for k in range(NB):
                    edge_group(r * NB + k, k)
            edge_group(NEG - 1 - NB, 0)
            edge_group(NEG - NB, 1, False)
            edge_group(NEG + 1 - NB, 2, False)
            edge_group(NEG - 1, 0, False)

            act.wait_ge(acc_added, NEG)

            def copy_sums(m, half):
                act.activation(accS[half], acc[:, bass.ds(m * SBN, SBN)], ACT.Copy).then_inc(accS_moved, 1)

            def first_half(m):
                act.wait_ge(zq_made, m + 1)
                act.activation(ex4, yv4, ACT.Exp, bias=ln_alpha[0:CH, 0:1]).then_inc(selu4, 1)
                act.activation(rl4, yv4, ACT.Relu).then_inc(selu4, 1)

            def second_half(m):
                act.wait_ge(msg4_turned, m + 1)
                act.activation(x2T, t_ps[0:F, 0:SBN], ACT.Copy).then_inc(msg4_moved, 1)
                act.wait_ge(var4, m + 1)
                act.activation(st[:, 3, :], st[:, 2, :], ACT.Sqrt, bias=eps_t[0:CH, 0:1], scale=1.0 / F).then_inc(std4, 1)

            copy_sums(0, 0)
            first_half(0)
            with act.Fori(0, NSB - 1) as m:
                act.wait_ge(m_ready, m + 1)
                act.sem_inc(act_at, 1)
                copy_sums(m + 1, 0)
                act.wait_ge(msg4_turned, m + 1)
                act.activation(x2T, t_ps[0:F, 0:SBN], ACT.Copy).then_inc(msg4_moved, 1)
                first_half(m + 1)
                act.wait_ge(var4, m + 1)
                act.activation(st[:, 3, :], st[:, 2, :], ACT.Sqrt, bias=eps_t[0:CH, 0:1], scale=1.0 / F).then_inc(std4, 1)
            second_half(NSB - 1)

        @block.tensor
        def _(pe):
            pe.sem_inc(groups_summed, SLOTS)
            pe.sem_inc(counts_moved, 2)
            pe.wait_ge(iota_set, 9)

            def turn_windows(n):
                pe.wait_ge(rel_ready, (n + 1) * 2)
                if not isinstance(n, int) or n > 0:
                    pe.wait_ge(win_moved, n * 2)
                for k in range(CHUNKS):
                    pe.transpose(t_ps[:, k * P:(k + 1) * P], rel[:, 0, k * P:(k + 1) * P], ident[:, :])
                for k in range(CHUNKS):
                    ins = pe.transpose(t2_ps[:, k * P:(k + 1) * P], rel[:, 1, k * P:(k + 1) * P], ident[:, :])
                ins.then_inc(win_turned, 1)

            def open_agg(s):
                if not isinstance(s, int) or s > 0:
                    pe.wait_ge(agg_moved, s * 2)
                pe.matmul(agg_ps[:, 0:SBN], zrow[:, 0:P], zrow[:, 0:SBN], start=True, stop=False, skip_group_check=True)
                pe.matmul(agg3_ps[:, 0:SBN], zrow[:, 0:P], zrow[:, 0:SBN], start=True, stop=False, skip_group_check=True)

            def layer(m, half):
                if isinstance(m, int):
                    pe.wait_ge(xm_in[half], 16 * (m // 2 + 1) + (16 if m == NSB - 1 else 0))
                else:
                    pe.wait_ge(xm_in[half], (m - half) * 8 + 16)
                if not isinstance(m, int) or m > 0:
                    pe.wait_ge(h_ready, m)
                pe.sem_inc(pe_at, 1)
                for c in range(NCH):
                    ins = pe.transpose(t_ps[0:F, c * CH:(c + 1) * CH], xm[:, half, c, :], ident[0:CH, 0:CH])
                ins.then_inc(xT_ready, 1)
                pe.wait_ge(agg_moved, m * 2 + 2)
                for c in range(NCH):
                    cols = slice(c * CH, (c + 1) * CH)
                    pe.matmul(u_ps[0:CH, c * H:(c + 1) * H], aggS[:, half, cols], Wl1s[:, :], start=True, stop=False, skip_group_check=True)
                    pe.matmul(u_ps[0:CH, c * H:(c + 1) * H], agg3S[0:F, half, cols], Wl1s[0:F, :], start=False, stop=True, skip_group_check=True)
                pe.wait_ge(xT_moved, m + 1)
                for c in range(NCH):
                    pe.matmul(t_ps[0:CH, SBN + c:SBN + c + 1], agg3S[:, half, c * CH:(c + 1) * CH], cnt_sel[:, :], start=True, stop=True)
                for c in range(NCH):
                    ins = pe.matmul(v_ps[0:CH, c * H:(c + 1) * H], xTs[0:F, c * CH:(c + 1) * CH], Wr1s[:, :], start=True, stop=True)
                ins.then_inc(uv_ready, 1)

            def superblock(s, half, build=True, mult=True, with_layer=True):
                if mult:
                    open_agg(s - 1)
                    pe.wait_ge(counts_moved, s * SB_GROUPS + 2)
                    pe.sem_inc(pe_at, 1)
                with pe.Fori(0, BODIES) as b:
                    for k in range(BG):
                        if build:
                            G = (s * BODIES + b) * BG + (k + 1)
                            pe.wait_ge(hot_ready, G)
                            pe.wait_ge(counts_moved, G)
                            for c in range(CHUNKS):
                                ins = pe.matmul(cnt_ps[k % 2][:, 0:CODES], lane_hot[:, k % SLOTS, :, c],
                                                code_hot[:, k % SLOTS, :, c], start=(c == 0), stop=(c == CHUNKS - 1))
                            ins.then_inc(groups_summed, 1)
                        if mult and k < BH:
                            rhs = Asb(1 - half)[:, bass.ds(b * BH + k, 1), :].rearrange("p a n -> p (a n)")
                            l1 = X12[:, bass.ds(b * BH + k, 1), :].rearrange("p a n -> p (a n)")
                            l2 = X3[:, bass.ds(b * BH + k, 1), :].rearrange("p a n -> p (a n)")
                            pe.matmul(agg_ps[:, 0:SBN], l1, rhs, start=False, stop=True, skip_group_check=True)
                            pe.matmul(agg3_ps[0:F + 1, 0:SBN], l2, rhs, start=False, stop=True, skip_group_check=True)
                if mult:
                    pe.matmul(agg3_ps[0:F + 1, 0:SBN], zrow[:, 0:F + 1], zrow[:, 0:SBN], start=False, stop=True, skip_group_check=True).then_inc(agg_ready, 1)
                if with_layer:
                    layer(s - 2, half)

            turn_windows(0)
            superblock(0, 0, mult=False, with_layer=False)
            turn_windows(1)
            superblock(1, 1, with_layer=False)
            pe.wait_ge(w_in, 64)
            superblock(2, 0)
            turn_windows(2)
            superblock(3, 1)
            with pe.Fori(2, PAIRS) as pair:
                superblock(pair * 2, 0)
                turn_windows(pair + 1)
                superblock(pair * 2 + 1, 1)
            superblock(NSB, 0, build=False)
            layer(NSB - 1, 1)

            pe.wait_ge(w2_in, 16 * 18)
            pe.wait_ge(ones_set, 4)
            pe.wait_ge(h_ready, NSB)
            pe.transpose(t_ps[0:F, 0:F], W1bs[:, :], ident[0:F, 0:F])
            pe.matmul(v_ps[0:F, 0:1], W1bs[:, :], shift_b[:, 0:1], start=True, stop=True, skip_group_check=True).then_inc(wt_turned, 1)
            pe.wait_ge(wts_made, 1)
            pe.matmul(t2_ps[0:CH, 0:F], u0b[:, :], W2au[:, :], start=True, stop=True)
            pe.matmul(t2_ps[0:CH, F:2 * F], shift_b[:, :], W2bs[:, :], start=True, stop=True, skip_group_check=True)
            pe.wait_ge(wt_moved, 1)
            pe.wait_ge(wts_made, 2)
            pe.matmul(t2_ps[0:F + 1, 2 * F:3 * F], WbT[:, :], W2am[:, :], start=True, stop=True, skip_group_check=True).then_inc(wts_ready, 1)
            pe.wait_ge(wts_made, 5)

            def sums2(s, half, m=None):
                if not isinstance(s, int) or s > 0:
                    pe.wait_ge(agg2_moved, s)
                pe.matmul(agg_ps[:, 0:SBN], zrow[:, 0:P], zrow[:, 0:SBN], start=True, stop=False, skip_group_check=True)
                if isinstance(s, int):
                    pe.wait_ge(A_in[half], (s // 2 + 1) * 16)
                else:
                    pe.wait_ge(A_in[half], (s - half) * 8 + 16)
                for b in range(BODIES):
                    for blk in range(b * BH, (b + 1) * BH):
                        for part in range(3):
                            ins = pe.matmul(agg_ps[:, 0:SBN], Hsb[:, part, blk, :], Asb(half)[:, blk, :], start=False,
                                            stop=(part == 2), skip_group_check=True)
                    if b == BODIES - 1:
                        ins.then_inc(agg2_ready, 1)
                    if m is not None:
                        layer2(m, b, 1 - half)

            def layer2(m, b, half):
                chunks = [slice(c * CH, (c + 1) * CH) for c in range(NCH)]
                if b == 0:
                    pe.wait_ge(hx_in[half], (m // 2 + 1) * 32 + (16 if m == NSB - 1 else 0) if isinstance(m, int) else (m - half) * 16 + 32)
                    for c in range(NCH):
                        ins = pe.transpose(t_ps[:, chunks[c]], h1m[half][:, c, :], ident[0:CH, 0:CH])
                    ins.then_inc(hT_turned, 1)
                    pe.wait_ge(agg2_moved, m + 1)
                    for c in range(NCH):
                        ins = pe.matmul(u_ps[0:CH, c * H:(c + 1) * H], g2S[:, chunks[c]], Wl2s[:, :], start=True, stop=True)
                    ins.then_inc(u2_ready, 1)
                if b == 1:
                    pe.wait_ge(hT_moved, m + 1)
                    for c in range(NCH):
                        ins = pe.matmul(v_ps[0:CH, c * H:(c + 1) * H], hTs[:, chunks[c]], Wr2s[:, :], start=True, stop=True)
                    ins.then_inc(v2_ready, 1)
                if b == 2:
                    pe.wait_ge(h2_ready, m + 1)
                    for c in range(NCH):
                        ins = pe.transpose(t2_ps[:, chunks[c]], hs[:, c, :], ident[0:CH, 0:CH])
                    ins.then_inc(h2_turned, 1)
                if b == 3:
                    pe.wait_ge(h2_moved, m + 1)
                    for c in range(NCH):
                        ins = pe.matmul(cnt_ps[0][0:CH, c * F:(c + 1) * F], h2T[:, chunks[c]], Wouts[:, :], start=True, stop=True)
                    ins.then_inc(o_ready, 1)
                if b == 5:
                    pe.wait_ge(x2_ready, m + 3)
                    pe.sem_inc(pe_at, 1)
                    for c in range(NCH):
                        ins = pe.transpose(cnt_ps[1][0:F, chunks[c]], x2c[:, c, :], ident[0:CH, 0:CH])
                    ins.then_inc(x2_turned, 1)
                if b == 6:
                    pe.wait_ge(x2_moved, m + 1)
                    for c in range(NCH):
                        ins = pe.matmul(agg3_ps[0:CH, c * 2 * F:(c + 1) * 2 * F], x2T[:, chunks[c]], Wxx[:, :], start=True, stop=True)
                    ins.then_inc(pq_ready, 1)

            pe.wait_ge(parts_in, 48)
            sums2(0, 0)
            with pe.Fori(0, PAIRS - 1) as j:
                sums2(j * 2 + 1, 1, j * 2)
                sums2(j * 2 + 2, 0, j * 2 + 1)
            sums2(NSB - 1, 1, NSB - 2)
            for b in range(BODIES):
                layer2(NSB - 1, b, 1)

            pe.wait_ge(base_made, 1)
            pe.matmul(t2_ps[:, 0:NEG], ones_r[:, :], base_f[:, :], start=True, stop=True).then_inc(bases_ready, 1)

            def edge_group(g, k, z_ps, s_ps, first=False):
                if isinstance(g, int):
                    pe.wait_ge(attr_in[k], 16 * (g // NB + 1) + (16 if g == NEG - 1 else 0))
                else:
                    pe.wait_ge(attr_in[k], g_round * 16 + 16)
                if not first:
                    pe.wait_ge(attr_moved, g)
                for c in range(EJ // 2):
                    ins = pe.transpose(t_ps[:, c * P:(c + 1) * P], attr[k][:, c * P:(c + 1) * P], ident[:, :])
                ins.then_inc(attr_turned, 1)
                pe.wait_ge(attr_moved, g + 1)
                for c in range(EJ // 2):
                    ins = pe.matmul(z_ps[:, c * P:(c + 1) * P], attrT[k][:, c * P:(c + 1) * P], Wedge[:, :], start=True, stop=True)
                ins.then_inc(z_ready, 1)
                pe.wait_ge(msg_made, g + 1)
                for j in range(EJ):
                    ins = pe.matmul(s_ps[0:F + 1, 0:WIN], msg[k][:, j, :], hot[k][:, j, :], start=(j == 0), stop=(j == EJ - 1))
                ins.then_inc(seg_ready, 1)

            zb, sbk = [cnt_ps[0], cnt_ps[1], agg_ps], [agg3_ps, u_ps, v_ps]
            pe.wait_ge(p_ready, NSB)
            for k in range(NB):
                edge_group(k, k, zb[k], sbk[k], first=(k == 0))
            with pe.Fori(1, (NEG - 1) // NB) as r:
                g_round = r
                for k in range(NB):
                    edge_group(r * NB + k, k, zb[k], sbk[k])
            edge_group(NEG - 1, 0, zb[0], sbk[0])

            chunks = [slice(c * CH, (c + 1) * CH) for c in range(NCH)]
            pe.wait_ge(acc_added, NEG)

            def sums_times(m):
                pe.wait_ge(accS_moved, m + 1)
                for c in range(NCH):
                    ins = pe.matmul(u_ps[0:CH, c * F:(c + 1) * F], accS[0][:, chunks[c]], Wc[:, :], start=True, stop=True)
                ins.then_inc(m_ready, 1)

            def turn_msg(m):
                pe.wait_ge(msg4_made, m + 1)
                pe.sem_inc(pe_at, 1)
                for c in range(NCH):
                    ins = pe.transpose(t_ps[0:F, chunks[c]], msg4[:, c * F:(c + 1) * F], ident[0:CH, 0:CH])
                ins.then_inc(msg4_turned, 1)

            def last_product(m):
                pe.wait_ge(msg4_moved, m + 1)
                for c in range(NCH):
                    ins = pe.matmul(v_ps[0:CH, c * F:(c + 1) * F], x2T[:, chunks[c]], W2bs[:, :], start=True, stop=True)
                ins.then_inc(y_ready, 1)

            sums_times(0)
            with pe.Fori(0, NSB - 1) as m:
                turn_msg(m)
                sums_times(m + 1)
                last_product(m)
            turn_msg(NSB - 1)
            last_product(NSB - 1)

        @block.vector
        def _(dve):
            n0 = [0]

            def step(ins):
                n0[0] += 1
                ins.then_inc(dve0, 1)
                dve.wait_ge(dve0, n0[0])

            dve.sem_inc(x2_ready, 2)
            dve.wait_ge(dst_in, 32)
            dve.tensor_copy(f16, dst_i.rearrange("p (r c) -> p r c", c=ROW)[:, :, 0]).then_inc(firsts_made, 1)
            dve.tensor_scalar(grp_i, dst_i, 3, None, ALU.arith_shift_right).then_inc(dve0, 1)
            dve.tensor_scalar(pos_i, dst_i, GROUP - 1, None, ALU.bitwise_and).then_inc(dve0, 1)
            dve.wait_ge(src_in, 32)
            dve.tensor_scalar(lane_i, src_i, P - 1, None, ALU.bitwise_and).then_inc(dve0, 1)
            dve.tensor_scalar(blk_i, src_i, 7, None, ALU.arith_shift_right).then_inc(dve0, 1)
            n0[0] = 4
            dve.wait_ge(dve0, 4)
            step(dve.scalar_tensor_tensor(code_a, grp_i, float(CODES), pos_i, ALU.mult, ALU.add))
            r3 = lambda ap: ap.rearrange("p (r c) -> p r c", c=ROW)
            dve.scalar_tensor_tensor(comb[:, :, ROW:2 * ROW], r3(blk_i), float(GROUP), r3(code_a), ALU.mult, ALU.add).then_inc(dve0, 1)
            dve.tensor_copy(comb[:, :, 0:ROW], r3(lane_i)).then_inc(dve0, 1)
            n0[0] += 2
            dve.wait_ge(dve0, n0[0])
            dve.sem_inc(table_made, 1)

            def find_windows(n, first=False):
                dve.tensor_scalar(junk, firsts, thr[:, bass.ds(n, 1)], None, ALU.is_lt, ALU.add,
                                  accum_out=below[:, bass.ds(n, 1)]).then_inc(win_dve, 1)
                dve.wait_ge(win_dve, n * 3 + 1)
                dve.tensor_scalar(start[:, bass.ds(n, 1)], below[:, bass.ds(n, 1)], -1.0, 0.0, ALU.add, ALU.max).then_inc(win_dve, 1)
                dve.wait_ge(win_dve, n * 3 + 2)
                if not first:
                    dve.wait_ge(win_in, n * (16 * WROWS))
                dve.tensor_scalar(rows12[:, 0, :], iota_w[:, 0:WROWS], start[:, bass.ds(n, 1)], None, ALU.add).then_inc(rows_ready, 1)

            def rel_windows(n):
                dve.wait_ge(win_in, (n + 1) * (16 * WROWS))
                dve.tensor_scalar(start[:, bass.ds(n, 1)], code0[:, bass.ds(n, 1)], float(CODES), -1.0, ALU.mult, ALU.add).then_inc(win_dve, 1)
                dve.wait_ge(win_dve, n * 3 + 3)
                r4 = rel.rearrange("p a (r c) -> p a r c", c=ROW)
                dve.tensor_scalar(r4[:, 0], win[:, :, 0:ROW], 1.0, None, ALU.add).then_inc(rel_ready, 1)
                dve.tensor_scalar(r4[:, 1], win[:, :, ROW:2 * ROW], start[:, bass.ds(n, 1)], 2040.0, ALU.subtract, ALU.min).then_inc(rel_ready, 1)

            def superblock(s, with_layer=True):
                with dve.Fori(0, BODIES) as b:
                    for k in range(BG):
                        g = s * SB_GROUPS + b * BG + k
                        dve.wait_ge(groups_summed, g + 1)
                        dve.tensor_tensor(lane_hot[:, k % SLOTS], iota_code[:, 0:P, :],
                                          laneT[:, bass.ds(g, 1), :].to_broadcast([P, P, CHUNKS]), ALU.is_equal)
                        dve.tensor_tensor(code_hot[:, k % SLOTS], iota_code[:, :, :],
                                          codeT[:, bass.ds(g, 1), :].to_broadcast([P, CODES, CHUNKS]), ALU.is_equal).then_inc(hot_ready, 1)
                if with_layer:
                    layer(s - 2)

            def grid(ap, f):
                return ap[0:CH, 0:NCH * f].rearrange("p (c f) -> p c f", f=f)

            def wide(ap, f):
                return ap.unsqueeze(2).to_broadcast([CH, NCH, f])

            def every(ap, f):
                return ap.unsqueeze(1).to_broadcast([CH, NCH, f])

            def layer(m):
                i = [0]

                def link(ins):
                    i[0] += 1
                    ins.then_inc(layer_dve, 1)
                    dve.wait_ge(layer_dve, m * 6 + i[0])
                dve.wait_ge(uv_ready, m + 1)
                link(dve.tensor_scalar(ctmp[:, :], t_ps[0:CH, SBN:SBN + NCH], 1.0, None, ALU.max))
                link(dve.reciprocal(inv_c[:, :], ctmp[:, :]))
                link(dve.tensor_tensor(inv[:, bass.ds(m, 1), :].rearrange("p a c -> p (a c)"), inv_c[:, :], zero_c[:, :], ALU.add))
                link(dve.tensor_tensor(ht[:, :, :], grid(u_ps, H), wide(inv_c[:, :], H), ALU.mult))
                link(dve.tensor_tensor(hv[:, :, :], grid(v_ps, H), every(bl1s[:, :], H), ALU.add))
                link(dve.tensor_tensor(ht[:, :, :], ht[:, :, :], hv[:, :, :], ALU.add))
                if not isinstance(m, int) or m > 0:
                    dve.wait_ge(h_stored, m * 64)
                dve.tensor_scalar(hs[:, :, :], ht[:, :, :], 0.0, None, ALU.max).then_inc(h_ready, 1)

            dve.wait_ge(iota_set, 9)
            dve.wait_ge(firsts_in, 16)
            dve.wait_ge(consts, 2)
            step(dve.memset(zero_c[:, :], 0.0))
            find_windows(0, True)
            dve.wait_ge(x1_made, 1)
            x3 = x_rows.rearrange("p (b f) -> p b f", f=F)
            xr = x_rest.rearrange("p (b f) -> p b f", f=F)
            step(dve.tensor_tensor(xr, x3, X12[:, :, 0:F], ALU.subtract))
            step(dve.tensor_copy(X12[:, :, F:2 * F], xr))
            step(dve.tensor_tensor(xr, xr, X12[:, :, F:2 * F], ALU.subtract))
            step(dve.tensor_copy(X3[:, :, 0:F], xr))
            rel_windows(0)
            find_windows(1)
            dve.wait_ge(win_moved, 2)
            superblock(0, False)
            rel_windows(1)
            dve.wait_ge(win_moved, 4)
            superblock(1, False)
            with dve.Fori(1, PAIRS) as pair:
                find_windows(pair + 1)
                superblock(pair * 2)
                rel_windows(pair + 1)
                dve.wait_ge(win_moved, pair * 2 + 4)
                dve.sem_inc(dve_at, 1)
                superblock(pair * 2 + 1)
            layer(NSB - 2)
            layer(NSB - 1)

            dve.wait_ge(w2_in, 16 * 18)
            dve.tensor_scalar(u0b[:, :], shift_b[:, :], 0.0, u0[:, 0:1], ALU.mult, ALU.add).then_inc(wts_made, 1)
            dve.wait_ge(wt_turned, 1)
            dve.tensor_tensor(WbT[:, F:F + 1], v_ps[0:F, 0:1], b1bcol[:, :], ALU.add).then_inc(wts_made, 1)
            dve.wait_ge(wts_ready, 1)
            dve.tensor_tensor(c2[:, :], t2_ps[0:CH, 0:F], b2as[:, :], ALU.add).then_inc(wts_made, 1)
            dve.tensor_copy(Wc[:, :], t2_ps[0:F + 1, 2 * F:3 * F]).then_inc(wts_made, 1)
            dve.tensor_scalar(W2bs[:, :], W2bs[:, :], SCALE, None, ALU.mult).then_inc(wts_made, 1)
            step(dve.tensor_tensor(b2bs[:, :], t2_ps[0:CH, F:2 * F], b2bs[:, :], ALU.add))

            def normalise(link, to, var, std, m):
                link(dve.tensor_reduce(st[:, 0, :], yv[:, :, :], AX_X, ALU.add))
                link(dve.tensor_scalar(st[:, 1, :], st[:, 0, :], -1.0 / F, None, ALU.mult))
                link(dve.tensor_tensor(yd[:, :, :], yv[:, :, :], wide(st[:, 1, :], F), ALU.add))
                link(dve.tensor_tensor(yv[:, :, :], yd[:, :, :], yd[:, :, :], ALU.mult))
                dve.tensor_reduce(st[:, 2, :], yv[:, :, :], AX_X, ALU.add).then_inc(var, 1)
                dve.wait_ge(std, m + 1)
                link(dve.reciprocal(st[:, 0, :], st[:, 3, :]))

            def layer2(m, half):
                i = [0]

                def link(ins):
                    i[0] += 1
                    ins.then_inc(dve2, 1)
                    dve.wait_ge(dve2, m * 11 + i[0])
                dve.wait_ge(u2_ready, m + 1)
                link(dve.tensor_tensor(inv_c[:, :], inv[:, bass.ds(m, 1), :].rearrange("p a c -> p (a c)"), zero_c[:, :], ALU.add))
                link(dve.tensor_tensor(ht[:, :, :], grid(u_ps, H), wide(inv_c[:, :], H), ALU.mult))
                dve.wait_ge(v2_ready, m + 1)
                link(dve.tensor_tensor(hv[:, :, :], grid(v_ps, H), every(bl2s[:, :], H), ALU.add))
                link(dve.tensor_tensor(ht[:, :, :], ht[:, :, :], hv[:, :, :], ALU.add))
                dve.tensor_scalar(hs[:, :, :], ht[:, :, :], 0.0, None, ALU.max).then_inc(h2_ready, 1)
                dve.wait_ge(o_ready, m + 1)
                link(dve.tensor_tensor(yd[:, :, :], grid(cnt_ps[0], F), every(bouts[:, :], F), ALU.add))
                link(dve.tensor_tensor(yv[:, :, :], yd[:, :, :], xm[:, half, :, :], ALU.add))
                normalise(link, None, var_ready, std_ready, m)
                if not isinstance(m, int) or m > 0:
                    dve.wait_ge(x2_kept, m)
                dve.tensor_tensor(x2c[:, :, :], yd[:, :, :], wide(st[:, 0, :], F), ALU.mult).then_inc(x2_ready, 1)
                dve.wait_ge(pq_ready, m + 1)
                pq = grid(agg3_ps, 2 * F)
                dve.tensor_tensor(q2all[:, bass.ds(m, 1), :, :].rearrange("p a c f -> p (a c) f"), pq[:, :, F:2 * F], every(c2[:, :], F), ALU.add)
                if not isinstance(m, int) or m > 0:
                    dve.wait_ge(p_stored, m * 16)
                dve.tensor_tensor(pc[:, :, :], pq[:, :, 0:F], every(b1as[:, :], F), ALU.add).then_inc(p_ready, 1)

            dve.wait_ge(hx_in[0], 32)
            layer2(0, 0)
            with dve.Fori(0, PAIRS - 1) as j:
                dve.wait_ge(hx_in[1], j * 32 + 32)
                layer2(j * 2 + 1, 1)
                dve.wait_ge(hx_in[0], j * 32 + 64)
                layer2(j * 2 + 2, 0)
            dve.wait_ge(hx_in[1], 32 * PAIRS + 16)
            layer2(NSB - 1, 1)

            dve.wait_ge(base_in, 32)
            dve.wait_ge(edges_in, 96)
            dve.tensor_copy(base_f[:, :], base_i[:, :]).then_inc(base_made, 1)
            dve.wait_ge(bases_ready, 1)
            dve.tensor_tensor(drel, dst_e, t2_ps[:, 0:NEG].unsqueeze(2).to_broadcast([P, NEG, EJ]), ALU.subtract).then_inc(drel_made, 1)
            dve.wait_ge(drel_made, 1)
            dve.wait_ge(acc_zero, 1 + NB)

            def edge_group(g, k, z_ps, last=None, r=None, first=False):
                dve.wait_ge(gath_in[k], (g // NB + 1) * (16 * EJ) if isinstance(g, int) else r * (16 * EJ) + 16 * EJ)
                dve.wait_ge(z_ready, g + 1)
                if not first:
                    dve.wait_ge(selu_act, g * 2)
                dve.tensor_tensor(zs, z_ps[:, 0:EJ * F], gath[k], ALU.add).then_inc(z_made, 1)
                if not first:
                    dve.wait_ge(seg_ready, g)
                dve.tensor_tensor(hot[k], iota_w[:, :].unsqueeze(1).to_broadcast([P, EJ, WIN]),
                                  drel[:, bass.ds(g, 1), :].rearrange("p a j -> p (a j)").unsqueeze(2).to_broadcast([P, EJ, WIN]),
                                  ALU.is_equal).then_inc(hot_made, 1)
                if last is not None:
                    last()
                dve.wait_ge(selu_act, g * 2 + 2)
                e3, r3 = (b.rearrange("p (j f) -> p j f", f=F) for b in (ex, rl))
                dve.scalar_tensor_tensor(msg[k][:, :, 0:F], e3, ALPHA, r3, ALU.min, ALU.add).then_inc(msg_made, 1)

            def add_sums(g, s_ps, first=False):
                dve.wait_ge(seg_ready, g + 1)
                if not first:
                    dve.wait_ge(acc_added, g)
                base = dve.value_load(base_i[0:1, bass.ds(g, 1)], min_val=0, max_val=N - 1)
                win_acc = acc[:, bass.ds(base, WIN)]
                dve.tensor_tensor(win_acc, win_acc, s_ps[0:F + 1, 0:WIN], ALU.add).then_inc(acc_added, 1)

            zb, sbk = [cnt_ps[0], cnt_ps[1], agg_ps], [agg3_ps, u_ps, v_ps]
            edge_group(0, 0, zb[0], first=True)
            edge_group(1, 1, zb[1], lambda: add_sums(0, sbk[0], True))
            edge_group(2, 2, zb[2], lambda: add_sums(1, sbk[1]))
            with dve.Fori(1, (NEG - 1) // NB) as r:
                for k in range(NB):
                    edge_group(r * NB + k, k, zb[k], lambda: add_sums(r * NB + (k - 1), sbk[(k - 1) % NB]), r)
            edge_group(NEG - 1, 0, zb[0], lambda: add_sums(NEG - 2, sbk[2]))
            add_sums(NEG - 1, sbk[0])

            def link4(m, i):
                def link(ins):
                    i[0] += 1
                    ins.then_inc(dve4, 1)
                    dve.wait_ge(dve4, m * 7 + i[0])
                return link

            def first_half(m):
                dve.wait_ge(m_ready, m + 1)
                dve.sem_inc(dve_at, 1)
                dve.tensor_tensor(zm4.rearrange("p (c f) -> p c f", f=F), grid(u_ps, F), wide(inv[:, bass.ds(m, 1), :].rearrange("p a c -> p (a c)"), F), ALU.mult).then_inc(zm_made, 1)
                dve.wait_ge(zm_made, m + 1)
                dve.tensor_tensor(yv4.rearrange("p (c f) -> p c f", f=F), zm4.rearrange("p (c f) -> p c f", f=F), q2all[:, bass.ds(m, 1), :, :].rearrange("p a c f -> p (a c) f"), ALU.add).then_inc(zq_made, 1)

            def make_msg(m):
                dve.wait_ge(selu4, m * 2 + 2)
                dve.scalar_tensor_tensor(msg4, ex4, ALPHA, rl4, ALU.min, ALU.add).then_inc(msg4_made, 1)

            def second_half(m):
                link = link4(m, [0])
                dve.wait_ge(y_ready, m + 1)
                link(dve.tensor_tensor(yd[:, :, :], grid(v_ps, F), every(b2bs[:, :], F), ALU.add))
                if not isinstance(m, int) or m > 0:
                    dve.wait_ge(row_stored, m * 16)
                link(dve.tensor_tensor(yv[:, :, :], yd[:, :, :], x2all[:, bass.ds(m, 1), :, :].rearrange("p a c f -> p (a c) f"), ALU.add))
                normalise(link, None, var4, std4, m)
                dve.tensor_tensor(yv[:, :, :], yd[:, :, :], wide(st[:, 0, :], F), ALU.mult).then_inc(row_made, 1)

            first_half(0)
            make_msg(0)
            with dve.Fori(0, NSB - 1) as m:
                first_half(m + 1)
                second_half(m)
                make_msg(m + 1)
            second_half(NSB - 1)


_INS = ['x', 'src', 'dst', 'edge_attr_64', 'L0_gnn_W_l1', 'L0_gnn_b_l1', 'L0_gnn_W_r1', 'L0_gnn_W_l2', 'L0_gnn_b_l2',
        'L0_gnn_W_r2', 'L0_gnn_W_out', 'L0_gnn_b_out', 'L1_gnn_u', 'L1_gnn_W1a', 'L1_gnn_b1a', 'L1_gnn_W1b',
        'L1_gnn_b1b', 'L1_gnn_W2a', 'L1_gnn_b2a', 'L1_gnn_W2b', 'L1_gnn_b2b']


def kernel(**inputs):
    import numpy as _np
    import concourse.bacc as _bacc
    from concourse import mybir as _mybir
    from concourse.bass_utils import run_bass_kernel_spmd as _run

    nc = _bacc.Bacc("TRN2", target_bir_lowering=False, num_devices=1)
    arrays, args = {}, []
    for name in _INS:
        a = _np.ascontiguousarray(inputs[name])
        arrays[f"in_{name}_dram"] = a
        args.append(nc.dram_tensor(f"in_{name}_dram", a.shape, _mybir.dt.from_np(a.dtype), kind="ExternalInput").ap())
    out = nc.dram_tensor("out_0_dram", (N, F), F32, kind="ExternalOutput").ap()
    build(nc, *args, out)
    r = _run(nc, [arrays], core_ids=[0])
    return r.results[0]["out_0_dram"]
```

```python
from contextlib import ExitStack

import math

import concourse.bass as bass
from concourse import mybir

F32 = mybir.dt.float32
BF16 = mybir.dt.bfloat16
FP16 = mybir.dt.float16
I32 = mybir.dt.int32
I16 = mybir.dt.int16
ALU = mybir.AluOpType
ACT = mybir.ActivationFunctionType
AX_X = mybir.AxisListType.X

P = 128
N = 6250
E = 206250
F = 64
H = 128
EPS = 1e-5
ALPHA = 1.6732632423543772848170429916717
SCALE = 1.0507009873554804934193349852946
LN_ALPHA = math.log(ALPHA)

SRC_BLOCKS = -(-N // P)
GROUP = 8
CODES = SRC_BLOCKS * GROUP
CHUNKS = 3
ROW = 32
WROWS = CHUNKS * P // ROW
EPP = 51 * ROW
TROWS = P * EPP // ROW
NO_NODE = 20000

SB_GROUPS = 56
SBN = SB_GROUPS * GROUP
NSB = 14
PAIRS = NSB // 2
BODIES = 7
BG = SB_GROUPS // BODIES
BH = SRC_BLOCKS // BODIES
SLOTS = 4
CH = 112
NCH = SBN // CH
NPAD = NSB * SBN

EG = 1024
EJ = EG // P
NEG = -(-E // EG)
ETAIL = E - (NEG - 1) * EG
WIN = 64

GN = 250
GE = 1250

assert N % GN == 0 and E % GE == 0
assert NPAD >= N and SRC_BLOCKS == BODIES * BH and NCH * CH == SBN


def build(nc, x, src, dst, edge_attr, Wl1, bl1, Wr1, Wl2, bl2, Wr2, Wout, bout,
          u, W1a, b1a, W1b, b1b, W2a, b2a, W2b, b2b, out, PH=9):
    def dram(name, shape, dt):
        return nc.dram_tensor(name, shape, dt, kind="Internal").ap()

    table = dram("edge_table", [TROWS, 2 * ROW], F32)
    firsts_d = dram("first_dst", [TROWS], I16)
    A_d = dram("counts_matrix", [NSB, P, SRC_BLOCKS * SBN], FP16)
    hp_d = dram("h1_parts", [3, NPAD, H], BF16)
    h1_d = dram("h1_rows", [NPAD, H], F32)
    p_d = dram("source_terms", [NPAD, F], F32)

    with ExitStack() as ctx:
        def sb(name, shape, dt):
            return ctx.enter_context(nc.sbuf_tensor(name, shape, dt))

        def sem(name):
            return ctx.enter_context(nc.semaphore(name))

        def bank(name, shape, dt=F32):
            return ctx.enter_context(nc.psum_tensor(name, shape, dt))

        A_sb = sb("A_sb", [P, 2, SRC_BLOCKS * SBN], FP16)
        wT = CHUNKS * 8 * P // 2
        ar1 = sb("arena1", [P, 3 * SRC_BLOCKS * H // 2 + 2 * NCH * H + NCH * F], F32)
        w1 = SRC_BLOCKS * 2 * F // 2
        w2 = w1 + SRC_BLOCKS * (F + 2) // 2
        X12 = ar1[:, 0:w1].bitcast(BF16).rearrange("p (b f) -> p b f", f=2 * F)
        X3 = ar1[:, w1:w2].bitcast(BF16).rearrange("p (b f) -> p b f", f=F + 2)[:, :, 0:F + 1]
        laneT = ar1[:, w2:w2 + wT].bitcast(FP16).rearrange("p (g k) -> p g k", k=CHUNKS)
        codeT = ar1[:, w2 + wT:w2 + 2 * wT].bitcast(FP16).rearrange("p (g k) -> p g k", k=CHUNKS)
        Hsb = ar1[:, 0:3 * SRC_BLOCKS * H // 2].bitcast(BF16).rearrange("p (a b f) -> p a b f", a=3, f=H)
        wl = SLOTS * CHUNKS * P // 2
        wc = wl + SLOTS * CHUNKS * CODES // 2
        ww = wc + WROWS * 2 * ROW
        wr = ww + 2 * WROWS * ROW
        ar2 = sb("arena2", [P, max(wr + TROWS // 4, 2 * NSB * NCH * F)], F32)
        lane_hot = ar2[:, 0:wl].bitcast(FP16).rearrange("p (s n c) -> p s n c", s=SLOTS, c=CHUNKS)
        code_hot = ar2[:, wl:wc].bitcast(FP16).rearrange("p (s n c) -> p s n c", s=SLOTS, c=CHUNKS)
        win = ar2[:, wc:ww].rearrange("p (r c) -> p r c", c=2 * ROW)
        rel = ar2[:, ww:wr].rearrange("p (a n) -> p a n", a=2)
        junk = ar2[:, wr:wr + TROWS // 4].bitcast(mybir.dt.uint8)
        x2all = ar2[0:CH, 0:NSB * NCH * F].rearrange("p (m c f) -> p m c f", c=NCH, f=F)
        q2all = ar2[0:CH, NSB * NCH * F:2 * NSB * NCH * F].rearrange("p (m c f) -> p m c f", c=NCH, f=F)
        ar3 = sb("arena3", [P, max(TROWS // 2, 2 * NEG * EJ)], F32)
        firsts = ar3[:, 0:TROWS // 2].bitcast(I16)
        src_e = ar3[:, 0:NEG * EJ].bitcast(I32).rearrange("p (g j) -> p g j", j=EJ)
        dst_e = ar3[:, NEG * EJ:2 * NEG * EJ].bitcast(I32).rearrange("p (g j) -> p g j", j=EJ)
        drel = ar3[:, NEG * EJ:2 * NEG * EJ].rearrange("p (g j) -> p g j", j=EJ)
        rows12 = sb("rows12", [P, 1, WROWS], I32)
        below = sb("below", [P, 8], F32)
        start = sb("start", [P, 8], F32)
        iota_code = sb("iota_code", [P, CODES, CHUNKS], FP16)
        iota_i = sb("iota_i", [P, 512], I32)
        iota_w = sb("iota_w", [P, WIN], F32)
        thr = sb("thr", [P, 8], F32)
        code0 = sb("code0", [P, 8], F32)
        ident = sb("ident", [P, P], F32)
        zrow = sb("zrow", [P, 512], BF16)
        aggS = sb("aggS", [P, 2, SBN], F32)
        agg3S = sb("agg3S", [F + 1, 2, SBN], F32)
        xm = sb("xm", [CH, 2, NCH, F], F32)
        xTs = sb("xTs", [P, SBN], F32)
        Wl1s = sb("Wl1s", [P, H], F32)
        Wr1s = sb("Wr1s", [F, H], F32)
        cnt_sel = sb("cnt_sel", [F + 1, 1], F32)
        bl1s = sb("bl1s", [CH, H], F32)
        ctmp = sb("ctmp", [CH, NCH], F32)
        inv_c = sb("inv_c", [CH, NCH], F32)
        inv = sb("inv", [CH, NSB, NCH], F32)
        cnt_all = sb("cnt_all", [CH, NSB, NCH], F32)
        chk = sb("chk", [P, 8], F32)
        flag_i = sb("flag_i", [1, 2], I32)
        hs = sb("hs", [CH, NCH, H], F32)
        ht = sb("ht", [CH, NCH, H], F32)
        hv = sb("hv", [CH, NCH, H], F32)
        hpart = sb("hpart", [CH, 3, NCH, H], BF16)
        Wl2s, Wr2s = sb("Wl2s", [H, H], F32), sb("Wr2s", [H, H], F32)
        Wouts = sb("Wouts", [H, F], F32)
        bl2s, bouts = sb("bl2s", [CH, H], F32), sb("bouts", [CH, F], F32)
        Wxx = sb("Wxx", [F, 2 * F], F32)
        Wedge = sb("Wedge", [P, 2 * F], F32)
        W1bs, W2am, W2au, W2bs = (sb(n, [F, F], F32) for n in ("W1bs", "W2am", "W2au", "W2bs"))
        b1as, b2as, b2bs = (sb(n, [CH, F], F32) for n in ("b1as", "b2as", "b2bs"))
        b1bcol, u0 = sb("b1bcol", [F, 1], F32), sb("u0", [F, 1], F32)
        u0b = sb("u0b", [F, CH], F32)
        shift_b = sb("shift_b", [F, CH], F32)
        WbT = sb("WbT", [F, F + 1], F32)
        Wc = sb("Wc", [F + 1, F], F32)
        c2 = sb("c2", [CH, F], F32)
        ln_alpha = sb("ln_alpha", [P, 1], F32)
        eps_t = sb("eps_t", [P, 1], F32)
        base_i = sb("base_i", [1, NEG], I32)
        base_f = sb("base_f", [1, NEG], F32)
        ones_r = sb("ones_r", [1, P], F32)
        ones_c = sb("ones_c", [P, 1], F32)

        A_raw = A_sb[:, :, :].rearrange("p a b -> p (a b)")

        def over(at, n, dt):
            return A_raw[:, at // 2:(at + n * 4) // 2].bitcast(dt)

        src_i = over(0, EPP, I32)
        dst_i = over(4 * EPP, EPP, I32)
        lane_i = over(8 * EPP, EPP, I32)
        blk_i = over(12 * EPP, EPP, I32)
        grp_i = over(16 * EPP, EPP, I32)
        pos_i = over(20 * EPP, EPP, I32)
        comb = over(24 * EPP, 2 * EPP, F32).rearrange("p (r c) -> p r c", c=2 * ROW)
        code_a = over(32 * EPP, EPP, F32)
        x_rows = over(36 * EPP, SRC_BLOCKS * F, F32)
        x_rest = over(36 * EPP + 4 * SRC_BLOCKS * F, SRC_BLOCKS * F, F32)
        featT = over(0, NPAD, F32)
        sumT = over(4 * NPAD, NPAD, F32)
        ends = over(8 * NPAD, 2 * GE, I32).rearrange("p (a e) -> p a e", a=2)
        at = [0]

        def edge_buf(n, parts=P):
            w = A_raw[0:parts, 2 * at[0]:2 * (at[0] + n)].bitcast(F32)
            at[0] += n
            return w

        NB = 3
        acc = edge_buf(N + WIN, F + 1)
        attr, gath, attrT = ([edge_buf(EJ * F)] for _ in range(3))
        zs, ex, rl = (edge_buf(EJ * F) for _ in range(3))
        msg = [edge_buf(EJ * (F + 1)).rearrange("p (j f) -> p j f", j=EJ)]
        attr += [edge_buf(EJ * F) for _ in range(NB - 1)]
        gath += [edge_buf(EJ * F) for _ in range(NB - 1)]
        attrT += [edge_buf(EJ * F) for _ in range(NB - 1)]
        msg += [edge_buf(EJ * (F + 1)).rearrange("p (j f) -> p j f", j=EJ) for _ in range(NB - 1)]
        hot = [edge_buf(EJ * WIN).rearrange("p (j n) -> p j n", j=EJ) for _ in range(NB)]
        accS = [edge_buf(SBN, F + 1)]
        dst_row = edge_buf(EG, 1).bitcast(I32)
        assert at[0] * 4 <= 4 * SRC_BLOCKS * SBN
        in_window = zs.bitcast(mybir.dt.uint8)[:, 0:NEG * EJ]
        f16 = over(36 * EPP + 8 * SRC_BLOCKS * F, TROWS // P, I32).bitcast(I16)[:, 0:TROWS // P]

        hw = 3 * SRC_BLOCKS * H // 2
        h1m = [ar1[0:CH, hw + i * NCH * H:hw + (i + 1) * NCH * H].rearrange("p (c f) -> p c f", f=H) for i in range(2)]
        g2S = aggS[:, 0, :]
        h2T = aggS[:, 1, :]
        x2T = agg3S[0:F, 0, :]
        hTs = xTs
        yv = sb("yv", [CH, NCH, F], F32)
        yd = sb("yd", [CH, NCH, F], F32)
        x2c = ar1[0:CH, hw + 2 * NCH * H:hw + 2 * NCH * H + NCH * F].rearrange("p (c f) -> p c f", f=F)
        pc = iota_i[0:CH, 0:NCH * F].bitcast(F32).rearrange("p (c f) -> p c f", f=F)
        st = sb("st", [CH, 4, NCH], F32)
        hr = iota_i[0:CH, :].bitcast(F32).rearrange("p (c f) -> p c f", f=H)
        zero_c = sb("zero_c", [CH, NCH], F32)
        src_cur = [sb(f"src_cur{i}", [P, EJ], I32) for i in range(NB)]
        ex4, rl4, yv4, zm4, msg4 = (b[0:CH, 0:NCH * F] for b in (ex, rl, gath[0], gath[1], gath[2]))
        cnt_ps = [bank(f"cnt_ps{i}", [P, 512]) for i in range(2)]
        agg_ps = bank("agg_ps", [P, 512])
        agg3_ps = bank("agg3_ps", [P, 512])
        u_ps = bank("u_ps", [P, 512])
        v_ps = bank("v_ps", [P, 512])
        t_ps = bank("t_ps", [P, 512])
        t2_ps = bank("t2_ps", [P, 512])

        pads_set = sem("pads_set")
        dst_in, src_in, x_in, w_in, w2_in = sem("dst_in"), sem("src_in"), sem("x_in"), sem("w_in"), sem("w2_in")
        iota_set = sem("iota_set")
        consts = sem("consts")
        firsts_made, firsts_out, firsts_in = sem("firsts_made"), sem("firsts_out"), sem("firsts_in")
        table_made, table_out = sem("table_made"), sem("table_out")
        x1_made = sem("x1_made")
        dve0 = sem("dve0")
        rows_ready, win_in, rel_ready, win_turned, win_moved = (sem(n) for n in (
            "rows_ready", "win_in", "rel_ready", "win_turned", "win_moved"))
        win_dve = sem("win_dve")
        hot_ready = sem("hot_ready")
        groups_summed = sem("groups_summed")
        counts_moved = sem("counts_moved")
        agg_ready, agg_moved = sem("agg_ready"), sem("agg_moved")
        A_stored = [sem("A_stored0"), sem("A_stored1")]
        xm_in = [sem("xm_in0"), sem("xm_in1")]
        xT_ready, xT_moved, uv_ready, layer_dve, h_ready, h_split, h_stored = (sem(n) for n in (
            "xT_ready", "xT_moved", "uv_ready", "layer_dve", "h_ready", "h_split", "h_stored"))
        sp_at, pool_at, act_at, pe_at, dve_at = sem("sp_at"), sem("pool_at"), sem("act_at"), sem("pe_at"), sem("dve_at")
        pool_dep, idx_made, zm_made = sem("pool_dep"), sem("idx_made"), sem("zm_made")
        parts_in = sem("parts_in")
        A_in = [sem("A_in0"), sem("A_in1")]
        hx_in = [sem("hx_in0"), sem("hx_in1")]
        (agg2_ready, agg2_moved, hT_turned, hT_moved, u2_ready, v2_ready, h2_ready, h2_turned, h2_moved, o_ready,
         var_ready, std_ready, x2_ready, x2_kept, x2_turned, x2_moved, pq_ready, p_ready, p_stored, dve2) = (
            sem(n) for n in ("agg2_ready", "agg2_moved", "hT_turned", "hT_moved", "u2_ready", "v2_ready", "h2_ready",
                             "h2_turned", "h2_moved", "o_ready", "var_ready", "std_ready", "x2_ready", "x2_kept",
                             "x2_turned", "x2_moved", "pq_ready", "p_ready", "p_stored", "dve2"))
        inv_made = sem("inv_made")
        chk_made, chk_sum, flags = sem("chk_made"), sem("chk_sum"), sem("flags")
        chkB_made, chkB_sum, flagB = sem("chkB_made"), sem("chkB_sum"), sem("flagB")
        (g_set, feat_in, ends_in, col_added, chunk_added, sums_done, gl_in) = (sem(n) for n in (
            "g_set", "feat_in", "ends_in", "col_added", "chunk_added", "sums_done", "gl_in"))
        (ge_zero, ge_in, ge_idx, ge_rows, ge_turned, ge_moved, ge_z, ge_zs, ge_selu, ge_msg, ge_msgT, ge_col, ge_added) = (
            sem(n) for n in ("ge_zero", "ge_in", "ge_idx", "ge_rows", "ge_turned", "ge_moved", "ge_z", "ge_zs",
                             "ge_selu", "ge_msg", "ge_msgT", "ge_col", "ge_added"))
        edges_in, base_in, base_made, bases_ready = sem("edges_in"), sem("base_in"), sem("base_made"), sem("bases_ready")
        drel_made, acc_zero, ones_set = sem("drel_made"), sem("acc_zero"), sem("ones_set")
        wt_turned, wt_moved, wts_ready, wts_made = sem("wt_turned"), sem("wt_moved"), sem("wts_ready"), sem("wts_made")
        attr_in = [sem(f"attr_in{i}") for i in range(3)]
        gath_in = [sem(f"gath_in{i}") for i in range(3)]
        (attr_turned, attr_moved, z_ready, z_made, selu_act, hot_made, msg_made, seg_ready, acc_added) = (sem(n) for n in (
            "attr_turned", "attr_moved", "z_ready", "z_made", "selu_act", "hot_made", "msg_made", "seg_ready",
            "acc_added"))
        (accS_moved, m_ready, dve4, zq_made, selu4, msg4_made, msg4_turned, msg4_moved, y_ready, var4, std4, row_made,
         row_stored) = (sem(n) for n in (
            "accS_moved", "m_ready", "dve4", "zq_made", "selu4", "msg4_made", "msg4_turned", "msg4_moved", "y_ready",
            "var4", "std4", "row_made", "row_stored"))

        block = ctx.enter_context(nc.Block())
        full = E // EPP
        tail = E - full * EPP
        whole = N // P

        def Asb(half):
            return A_sb[:, half, :].rearrange("p (b n) -> p b n", n=SBN)

        def by_node(t, m):
            return t[bass.ds(m * SBN, SBN), :].rearrange("(c q) f -> q c f", q=CH)

        LAST = (NSB - 1) * SBN
        LCH = (N - LAST) // CH
        LREST = N - LAST - LCH * CH

        def general_begins(eng):
            eng.wait_ge(p_stored, 16 * NSB)
            eng.wait_ge(x2_kept, NSB)
            eng.wait_ge(x2_moved, NSB)
            eng.wait_ge(pq_ready, NSB)
            eng.wait_ge(edges_in, 96)

        def general_ends(eng):
            eng.wait_ge(p_stored, 2 * 16 * NSB)
            eng.wait_ge(x2_kept, 2 * NSB)
            eng.wait_ge(x2_moved, 2 * NSB)
            eng.wait_ge(pq_ready, 2 * NSB)

        def edges_end(eng):
            eng.wait_ge(acc_added, NEG)
            eng.wait_ge(seg_ready, NEG)
            eng.wait_ge(selu_act, 2 * NEG)

        @block.sync
        def _(sp):
            sp.wait_ge(pads_set, 2)
            sp.dma_start(dst_i[0:full, :], dst[0:full * EPP].rearrange("(p j) -> p j", j=EPP)).then_inc(dst_in, 16)
            sp.dma_start(dst_i[full:full + 1, 0:tail], dst[full * EPP:E].rearrange("(p j) -> p j", p=1)).then_inc(dst_in, 16)
            sp.dma_start(src_i[0:full, :], src[0:full * EPP].rearrange("(p j) -> p j", j=EPP)).then_inc(src_in, 16)
            sp.dma_start(src_i[full:full + 1, 0:tail], src[full * EPP:E].rearrange("(p j) -> p j", p=1)).then_inc(src_in, 16)
            xr3 = x_rows.rearrange("p (b f) -> p b f", f=F)
            sp.wait_ge(pads_set, 3)
            sp.dma_start(xr3[:, 0:whole, :], x[0:whole * P, :].rearrange("(b p) f -> p b f", p=P)).then_inc(x_in, 16)
            sp.dma_start(xr3[0:N - whole * P, whole, :], x[whole * P:N, :]).then_inc(x_in, 16)
            for half in range(2):
                sp.dma_start(Wl1s[half * F:(half + 1) * F, :], Wl1).then_inc(w_in, 16)
            sp.dma_start(Wr1s[:, :], Wr1).then_inc(w_in, 16)
            sp.dma_start(bl1s[:, :], bl1.partition_broadcast(CH)).then_inc(w_in, 16)
            sp.wait_ge(firsts_made, 1)
            sp.dma_start(firsts_d.rearrange("(p r) -> p r", p=P), f16).then_inc(firsts_out, 16)
            sp.wait_ge(firsts_out, 16)
            sp.dma_start(firsts, firsts_d.partition_broadcast(P)).then_inc(firsts_in, 16)
            sp.wait_ge(table_made, 1)
            sp.dma_start(table.rearrange("(p r) c -> p (r c)", p=P), comb.rearrange("p r c -> p (r c)")).then_inc(table_out, 16)
            for to, frm in ((Wl2s, Wl2), (Wr2s, Wr2), (Wouts, Wout), (bl2s, bl2.partition_broadcast(CH)),
                            (bouts, bout.partition_broadcast(CH)), (Wxx[:, 0:F], W1a[0:F, :]), (Wxx[:, F:2 * F], W2a[0:F, :]),
                            (W1bs, W1b), (W2am, W2a[F:2 * F, :]), (W2au, W2a[2 * F:3 * F, :]), (W2bs, W2b),
                            (b1as, b1a.partition_broadcast(CH)), (b2as, b2a.partition_broadcast(CH)),
                            (b2bs, b2b.partition_broadcast(CH)), (b1bcol, b1b.rearrange("(f a) -> f a", a=1)),
                            (u0, u[0:1, :].rearrange("a f -> f a"))):
                sp.dma_start(to if isinstance(to, bass.AP) else to[:, :], frm).then_inc(w2_in, 16)
            sp.wait_ge(pads_set, 4)
            for half in range(2):
                sp.dma_start(Wedge[half * F:(half + 1) * F, half * F:(half + 1) * F], W1a[F:2 * F, :]).then_inc(w2_in, 16)

            def store_h(m, half):
                sp.wait_ge(h_split, m + 1)
                sp.dma_start(by_node(h1_d, m), hs[:, :, :]).then_inc(h_stored, 16)
                for part in range(3):
                    sp.dma_start(by_node(hp_d[part], m), hpart[:, part, :, :]).then_inc(h_stored, 16)

            def superblock(s, half, layer):
                if layer:
                    if not isinstance(s, int):
                        sp.wait_ge(xT_ready, s - 3)
                    sp.dma_start(xm[:, half, :, :], by_node(x, s - 2)).then_inc(xm_in[half], 16)
                sp.wait_ge(counts_moved, (s + 1) * SB_GROUPS + 2)
                sp.dma_start(A_d[bass.ds(s, 1), :, :].rearrange("a p n -> (a p) n"), A_sb[:, half, :]).then_inc(A_stored[half], 16)
                if layer:
                    store_h(s - 2, half)

            superblock(0, 0, False)
            superblock(1, 1, False)
            superblock(2, 0, True)
            superblock(3, 1, True)
            with sp.Fori(2, PAIRS) as pair:
                superblock(pair * 2, 0, True)
                superblock(pair * 2 + 1, 1, True)
            sp.wait_ge(xT_ready, NSB - 3)
            sp.dma_start(xm[:, 0, :, :], by_node(x, NSB - 2)).then_inc(xm_in[0], 16)
            sp.wait_ge(xT_ready, NSB - 2)

            def last_rows(rows, done):
                sp.dma_start(rows[:, 0:LCH, :], x[LAST:LAST + LCH * CH, :].rearrange("(c q) f -> q c f", q=CH)).then_inc(done, 16)
                sp.dma_start(rows[0:LREST, LCH, :], x[LAST + LCH * CH:N, :]).then_inc(done, 16)
            last_rows(xm[:, 1], xm_in[1])
            store_h(NSB - 2, 0)
            sp.wait_ge(firsts_in, 16)
            sp.wait_ge(rows_ready, PAIRS + 1)
            sp.wait_ge(pads_set, 6)
            gE = NEG - 1
            for to, frm in ((src_e, src), (dst_e, dst)):
                sp.dma_start(to[:, 0:gE, :], frm[0:gE * EG].rearrange("(g p j) -> p g j", p=P, j=EJ)).then_inc(edges_in, 16)
                sp.dma_start(to[0:ETAIL // EJ, gE, :], frm[gE * EG:gE * EG + ETAIL // EJ * EJ].rearrange("(p j) -> p j", j=EJ)).then_inc(edges_in, 16)
                sp.dma_start(to[ETAIL // EJ:ETAIL // EJ + 1, gE, 0:ETAIL % EJ], frm[gE * EG + ETAIL // EJ * EJ:E].rearrange("(p j) -> p j", p=1)).then_inc(edges_in, 16)
            with nc.allow_non_contiguous_dma(reason="one destination of every 1024"):
                sp.dma_start(base_i[0:1, 0:gE], dst[0:gE * EG].rearrange("(a g q) -> a g q", a=1, q=EG)[:, :, 0]).then_inc(base_in, 16)
            sp.dma_start(base_i[0:1, gE:NEG], dst[gE * EG:gE * EG + 1].rearrange("(a g) -> a g", a=1)).then_inc(base_in, 16)
            store_h(NSB - 1, 1)

            sp.wait_ge(A_stored[0], 16 * PAIRS)
            sp.wait_ge(A_stored[1], 16 * PAIRS)
            sp.wait_ge(h_stored, 64 * NSB)
            sp.wait_ge(agg_ready, NSB)
            sp.dma_start(A_sb[:, 0, :], A_d[0]).then_inc(A_in[0], 16)
            for part in range(3):
                sp.dma_start(Hsb[:, part], hp_d[part, 0:SRC_BLOCKS * P, :].rearrange("(b p) f -> p b f", p=P)).then_inc(parts_in, 16)
            sp.dma_start(A_sb[:, 1, :], A_d[1]).then_inc(A_in[1], 16)

            def load_hx(m, half):
                sp.dma_start(h1m[half][:, :, :], by_node(h1_d, m)).then_inc(hx_in[half], 16)
                sp.dma_start(xm[:, half, :, :], by_node(x, m)).then_inc(hx_in[half], 16)

            load_hx(0, 0)

            def superblock2(s, half):
                sp.wait_ge(agg2_ready, s)
                if not (isinstance(s, int) and s == NSB - 1):
                    sp.dma_start(A_sb[:, 1 - half, :], A_d[bass.ds(s + 1, 1), :, :].rearrange("a p n -> (a p) n")).then_inc(A_in[1 - half], 16)
                    sp.wait_ge(x2_ready, s + 1)
                    load_hx(s, half)
                else:
                    sp.wait_ge(x2_ready, NSB)
                    sp.dma_start(h1m[1][:, :, :], by_node(h1_d, NSB - 1)).then_inc(hx_in[1], 16)
                    last_rows(xm[:, 1], hx_in[1])
                sp.wait_ge(p_ready, s)
                sp.dma_start(by_node(p_d, s - 1), pc[:, :, :]).then_inc(p_stored, 16)

            with sp.Fori(0, PAIRS - 1) as j:
                superblock2(j * 2 + 1, 1)
                superblock2(j * 2 + 2, 0)
            superblock2(NSB - 1, 1)
            sp.wait_ge(p_ready, NSB)
            sp.dma_start(by_node(p_d, NSB - 1), pc[:, :, :]).then_inc(p_stored, 16)

            def general_sums(table_d, width, i):
                sp.wait_ge(g_set, 2 * i + 2)
                with nc.allow_non_contiguous_dma(reason="turns the rows of nodes"):
                    with sp.Fori(0, N // GN) as c:
                        sp.dma_start(featT[0:width, bass.ds(c * GN, GN)], table_d[bass.ds(c * GN, GN), :].rearrange("n f -> f n")).then_inc(feat_in, 16)
                        sp.wait_ge(feat_in, c * 16 + 16 * (i * (N // GN) + 1))
                        sp.sem_inc(sp_at, 1)
                with sp.Fori(0, E // GE) as c:
                    sp.wait_ge(chunk_added, c + (i * (E // GE) + 1))
                    sp.sem_inc(sp_at, 1)
                    for a, frm in enumerate((src, dst)):
                        sp.dma_start(ends[0:1, a, :], frm[bass.ds(c * GE, GE)].rearrange("(a e) -> a e", a=1)).then_inc(ends_in, 16)

            def general_layer1(m):
                if isinstance(m, int):
                    last_rows(xm[:, 0], gl_in)
                else:
                    sp.dma_start(xm[:, 0], by_node(x, m)).then_inc(gl_in, 32)
                sp.wait_ge(h_ready, m + (NSB + 1))
                sp.dma_start(by_node(h1_d, m), hs[:, :, :]).then_inc(h_stored, 64)

            def general_layer2(m):
                sp.dma_start(h1m[0], by_node(h1_d, m)).then_inc(gl_in, 16)
                if isinstance(m, int):
                    last_rows(xm[:, 0], gl_in)
                else:
                    sp.dma_start(xm[:, 0], by_node(x, m)).then_inc(gl_in, 32)
                sp.wait_ge(p_ready, m + (NSB + 1))
                sp.dma_start(by_node(p_d, m), pc).then_inc(p_stored, 16)
                sp.wait_ge(p_stored, m * 16 + 16 * (NSB + 1))
                sp.sem_inc(sp_at, 1)

            sp.wait_ge(flags, 1)
            left = sp.value_load(flag_i[0:1, 0:1], min_val=0, max_val=1)
            with sp.If_ne(sp.to_reg(left), 0):
                general_begins(sp)
                general_sums(x, F, 0)
                with sp.Fori(0, NSB - 1) as m:
                    general_layer1(m)
                general_layer1(NSB - 1)
                sp.wait_ge(h_stored, 2 * 64 * NSB)
                general_sums(h1_d, H, 1)
                with sp.Fori(0, NSB - 1) as m:
                    general_layer2(m)
                general_layer2(NSB - 1)
                general_ends(sp)

            sp.wait_ge(agg2_ready, NSB)

            def load_attr(g, k):
                sp.dma_start(attr[k], edge_attr[bass.ds(g * EG, EG), :].rearrange("(p j) f -> p (j f)", p=P)).then_inc(attr_in[k], 16)
            for k in range(NB):
                load_attr(k, k)
            with sp.Fori(1, gE // NB) as r:
                for k in range(NB):
                    sp.wait_ge(attr_turned, r * NB + (k - NB + 1))
                    load_attr(r * NB + k, k)
            sp.wait_ge(attr_turned, gE - NB + 1)
            te = gE * EG
            sp.dma_start(attr[0][0:ETAIL // EJ, :], edge_attr[te:te + ETAIL // EJ * EJ, :].rearrange("(p j) f -> p (j f)", j=EJ)).then_inc(attr_in[0], 16)
            sp.dma_start(attr[0][ETAIL // EJ:ETAIL // EJ + 1, 0:ETAIL % EJ * F], edge_attr[te + ETAIL // EJ * EJ:E, :].rearrange("(p j) f -> p (j f)", p=1)).then_inc(attr_in[0], 16)

            sp.wait_ge(flagB, 1)
            left = sp.value_load(flag_i[0:1, 1:2], min_val=0, max_val=1)
            with sp.If_ne(sp.to_reg(left), 0):
                edges_end(sp)
                with sp.Fori(0, gE) as g:
                    sp.wait_ge(ge_added, g + 1)
                    sp.sem_inc(sp_at, 1)
                    sp.dma_start(attr[0], edge_attr[bass.ds(g * EG, EG), :].rearrange("(p j) f -> p (j f)", p=P)).then_inc(ge_in, 16)
                    sp.dma_start(dst_row, dst[bass.ds(g * EG, EG)].rearrange("(a e) -> a e", a=1)).then_inc(ge_in, 16)
                sp.wait_ge(ge_zero, 2)
                sp.dma_start(attr[0][0:ETAIL // EJ, :], edge_attr[te:te + ETAIL // EJ * EJ, :].rearrange("(p j) f -> p (j f)", j=EJ)).then_inc(ge_in, 16)
                sp.dma_start(attr[0][ETAIL // EJ:ETAIL // EJ + 1, 0:ETAIL % EJ * F], edge_attr[te + ETAIL // EJ * EJ:E, :].rearrange("(p j) f -> p (j f)", p=1)).then_inc(ge_in, 16)
                sp.dma_start(dst_row[:, 0:ETAIL], dst[te:E].rearrange("(a e) -> a e", a=1)).then_inc(ge_in, 16)
                sp.wait_ge(ge_added, NEG + 1)

            with sp.Fori(0, NSB - 1) as m:
                sp.wait_ge(row_made, m + 1)
                sp.dma_start(by_node(out, m), yv[:, :, :]).then_inc(row_stored, 16)
            sp.wait_ge(row_made, NSB)
            sp.dma_start(out[LAST:LAST + LCH * CH, :].rearrange("(c q) f -> q c f", q=CH), yv[:, 0:LCH, :]).then_inc(row_stored, 16)
            sp.dma_start(out[LAST + LCH * CH:N, :], yv[0:LREST, LCH, :]).then_inc(row_stored, 16)
            sp.wait_ge(row_stored, 16 * (NSB + 1))

        @block.gpsimd
        def _(pool):
            pool.memset(src_i, 0).then_inc(pads_set, 1)
            pool.memset(dst_i, NO_NODE).then_inc(pads_set, 1)
            pool.memset(x_rows, 0.0).then_inc(pads_set, 1)
            pool.memset(Wedge[:, :], 0.0).then_inc(pads_set, 1)
            pool.iota(iota_i[:, :], [[1, 512]], 0, 0).then_inc(iota_set, 1)
            pool.memset(ident[:, :], 0.0).then_inc(iota_set, 1)
            pool.memset(zrow[:, :], 0.0).then_inc(iota_set, 1)
            pool.memset(X3[:, :, F:F + 1], 1.0).then_inc(iota_set, 1)
            pool.memset(cnt_sel[:, :], 0.0).then_inc(iota_set, 1)
            pool.wait_ge(iota_set, 5)
            pool.affine_select(out=ident[:, :], in_=ident[:, :], compare_op=ALU.not_equal, fill=1.0,
                               base=0, pattern=[[-1, P]], channel_multiplier=1).then_inc(iota_set, 1)
            pool.affine_select(out=cnt_sel[:, :], in_=cnt_sel[:, :], compare_op=ALU.not_equal, fill=1.0,
                               base=-F, pattern=[[0, 1]], channel_multiplier=1).then_inc(iota_set, 1)
            pool.iota(thr[:, :], [[GROUP * P, 8]], 0, GROUP, allow_small_or_imprecise_dtypes=True).then_inc(iota_set, 1)
            pool.iota(code0[:, :], [[P, 8]], 0, 1, allow_small_or_imprecise_dtypes=True).then_inc(iota_set, 1)
            pool.memset(shift_b[:, :], -SCALE * ALPHA).then_inc(ones_set, 1)
            pool.memset(ln_alpha[:, :], LN_ALPHA).then_inc(ones_set, 1)
            pool.memset(eps_t[:, :], EPS).then_inc(ones_set, 1)
            pool.memset(ones_r[:, :], 1.0).then_inc(ones_set, 1)
            pool.memset(ones_c[:, :], 1.0).then_inc(ones_set, 1)
            pool.wait_ge(table_out, 16)

            def gather_windows(n):
                pool.wait_ge(rows_ready, n + 1)
                pool.sem_inc(pool_at, 1)
                for j in range(WROWS):
                    pool.indirect_dma_start(
                        out=win[:, j, :], out_offset=None, in_=table,
                        in_offset=bass.IndirectOffsetOnAxis(ap=rows12[:, 0, j:j + 1], axis=0)).then_inc(win_in, 16)

            def split_h(m):
                pool.wait_ge(h_ready, m + 1)
                pool.wait_ge(h_stored, m * 64)
                pool.sem_inc(pool_at, 1)
                seq = [lambda: pool.tensor_copy(hpart[:, 0], hs[:, :, :]),
                       lambda: pool.tensor_tensor(hr[:, :, :], hs[:, :, :], hpart[:, 0], ALU.subtract),
                       lambda: pool.tensor_copy(hpart[:, 1], hr[:, :, :]),
                       lambda: pool.tensor_tensor(hr[:, :, :], hr[:, :, :], hpart[:, 1], ALU.subtract),
                       lambda: pool.tensor_copy(hpart[:, 2], hr[:, :, :])]
                for i, op in enumerate(seq):
                    if i < 4:
                        op().then_inc(pool_dep, 1)
                        pool.wait_ge(pool_dep, m * 4 + (i + 1))
                        pool.sem_inc(pool_at, 1)
                    else:
                        op().then_inc(h_split, 1)

            gather_windows(0)
            pool.wait_ge(win_turned, 1)
            gather_windows(1)
            pool.wait_ge(win_turned, 2)
            gather_windows(2)
            split_h(0)
            split_h(1)
            with pool.Fori(2, PAIRS) as pair:
                pool.wait_ge(win_turned, pair + 1)
                pool.sem_inc(pool_at, 1)
                gather_windows(pair + 1)
                split_h(pair * 2 - 2)
                split_h(pair * 2 - 1)
            pool.wait_ge(rows_ready, PAIRS + 1)
            pool.memset(src_e[:, NEG - 1, :], 0).then_inc(pads_set, 1)
            pool.memset(dst_e[:, NEG - 1, :], NO_NODE).then_inc(pads_set, 1)
            split_h(NSB - 2)
            split_h(NSB - 1)

            pool.wait_ge(hot_ready, NSB * SB_GROUPS)
            pool.wait_ge(groups_summed, NSB * SB_GROUPS + SLOTS)
            pool.wait_ge(win_turned, PAIRS + 1)
            with pool.Fori(0, NSB) as m:
                pool.wait_ge(x2_ready, m + 3)
                pool.sem_inc(pool_at, 1)
                pool.tensor_copy(x2all[:, bass.ds(m, 1), :, :].rearrange("p a c f -> p (a c) f"), x2c[:, :, :]).then_inc(x2_kept, 1)

            pool.wait_ge(flags, 1)
            left = pool.value_load(flag_i[0:1, 0:1], min_val=0, max_val=1)
            with pool.If_ne(pool.to_reg(left), 0):
                general_begins(pool)
                pool.memset(featT, 1.0).then_inc(g_set, 1)
                pool.memset(sumT, 0.0).then_inc(g_set, 1)
                pool.wait_ge(h_stored, 2 * 64 * NSB)
                pool.memset(featT, 0.0).then_inc(g_set, 1)
                pool.memset(sumT, 0.0).then_inc(g_set, 1)
                with pool.Fori(NSB, 2 * NSB) as m:
                    pool.wait_ge(x2_ready, m + 3)
                    pool.sem_inc(pool_at, 1)
                    pool.tensor_copy(x2all[:, bass.ds(m - NSB, 1), :, :].rearrange("p a c f -> p (a c) f"), x2c[:, :, :]).then_inc(x2_kept, 1)
                general_ends(pool)

            pool.wait_ge(agg2_ready, NSB)
            pool.memset(acc[:, :], 0.0).then_inc(acc_zero, 1)
            for k in range(NB):
                pool.memset(msg[k][:, :, F:F + 1], 1.0).then_inc(acc_zero, 1)
            pool.wait_ge(edges_in, 96)
            pool.wait_ge(p_stored, 16 * NSB)

            def gather(g, k):
                for j in range(EJ):
                    pool.indirect_dma_start(
                        out=gath[k][:, j * F:(j + 1) * F], out_offset=None, in_=p_d,
                        in_offset=bass.IndirectOffsetOnAxis(ap=src_cur[k][:, j:j + 1], axis=0)).then_inc(gath_in[k], 16)

            for k in range(NB):
                pool.wait_ge(idx_made, k + 1)
                gather(k, k)
            with pool.Fori(1, (NEG - 1) // NB) as r:
                for k in range(NB):
                    pool.wait_ge(z_made, r * NB + (k - NB + 1))
                    pool.wait_ge(idx_made, r * NB + (k + 1))
                    pool.sem_inc(pool_at, 1)
                    gather(r * NB + k, k)
            pool.wait_ge(z_made, NEG - NB)
            pool.wait_ge(idx_made, NEG)
            gather(NEG - 1, 0)

            pool.wait_ge(flagB, 1)
            left = pool.value_load(flag_i[0:1, 1:2], min_val=0, max_val=1)
            with pool.If_ne(pool.to_reg(left), 0):
                edges_end(pool)
                pool.memset(acc[:, :], 0.0).then_inc(ge_zero, 1)

                def general_gather(g):
                    pool.wait_ge(ge_idx, g + 1)
                    pool.sem_inc(pool_at, 1)
                    for j in range(EJ):
                        pool.indirect_dma_start(
                            out=gath[0][:, j * F:(j + 1) * F], out_offset=None, in_=p_d,
                            in_offset=bass.IndirectOffsetOnAxis(ap=src_cur[0][:, j:j + 1], axis=0)).then_inc(ge_rows, 16)
                with pool.Fori(0, NEG - 1) as g:
                    general_gather(g)
                pool.wait_ge(ge_added, NEG)
                pool.memset(dst_row, N + WIN - 1).then_inc(ge_zero, 1)
                general_gather(NEG - 1)
                pool.wait_ge(ge_added, NEG + 1)

        @block.scalar
        def _(act):
            act.wait_ge(iota_set, 9)
            act.activation(iota_code[:, :, :], iota_i[:, 0:CODES].unsqueeze(2).to_broadcast([P, CODES, CHUNKS]), ACT.Copy, bias=1.0).then_inc(consts, 1)
            act.activation(iota_w[:, :], iota_i[:, 0:WIN], ACT.Copy).then_inc(consts, 1)
            act.wait_ge(x_in, 32)
            act.activation(X12[:, :, 0:F], x_rows.rearrange("p (b f) -> p b f", f=F), ACT.Copy).then_inc(x1_made, 1)

            def move_windows(n):
                act.wait_ge(win_turned, n + 1)
                act.sem_inc(act_at, 1)
                cols = bass.ds(n * P, P)
                act.activation(laneT[:, cols, :], t_ps[:, 0:CHUNKS * P].rearrange("p (k g) -> p g k", g=P), ACT.Copy).then_inc(win_moved, 1)
                act.activation(codeT[:, cols, :], t2_ps[:, 0:CHUNKS * P].rearrange("p (k g) -> p g k", g=P), ACT.Relu).then_inc(win_moved, 1)

            def move_xT(m):
                act.wait_ge(xT_ready, m + 1)
                act.activation(xTs[0:F, :], t_ps[0:F, 0:SBN], ACT.Copy).then_inc(xT_moved, 1)

            def move_agg(s, half):
                act.wait_ge(agg_ready, s + 1)
                act.activation(aggS[:, half, :], agg_ps[:, 0:SBN], ACT.Copy).then_inc(agg_moved, 1)
                act.activation(agg3S[:, half, :], agg3_ps[0:F + 1, 0:SBN], ACT.Copy).then_inc(agg_moved, 1)

            def superblock(s, half, mult=True, layer=True):
                dest = Asb(half)
                with act.Fori(0, BODIES) as b:
                    for k in range(BG):
                        act.wait_ge(groups_summed, (s * BODIES + b) * BG + (k + 1 + SLOTS))
                        act.sem_inc(act_at, 1)
                        act.activation(dest[:, :, bass.ds((b * BG + k) * GROUP, GROUP)],
                                       cnt_ps[k % 2][:, 0:CODES].rearrange("p (b j) -> p b j", j=GROUP),
                                       ACT.Copy).then_inc(counts_moved, 1)
                if mult:
                    move_agg(s - 1, 1 - half)
                if layer:
                    move_xT(s - 2)

            move_windows(0)
            superblock(0, 0, False, False)
            move_windows(1)
            superblock(1, 1, True, False)

            def pair_of(pair):
                act.wait_ge(A_stored[0], pair * 16)
                act.sem_inc(act_at, 1)
                superblock(pair * 2, 0)
                move_windows(pair + 1)
                act.wait_ge(A_stored[1], pair * 16)
                act.sem_inc(act_at, 1)
                superblock(pair * 2 + 1, 1)
            with act.Fori(1, PAIRS) as pair:
                pair_of(pair)
            move_xT(NSB - 2)
            move_agg(NSB - 1, 1)
            move_xT(NSB - 1)

            act.wait_ge(wt_turned, 1)
            act.activation(WbT[:, 0:F], t_ps[0:F, 0:F], ACT.Copy, scale=SCALE).then_inc(wt_moved, 1)

            def layer2(m, s=None):
                act.wait_ge(hT_turned, m + 1)
                act.activation(hTs[:, :], t_ps[:, 0:SBN], ACT.Copy).then_inc(hT_moved, 1)
                act.wait_ge(h2_turned, m + 1)
                act.activation(h2T, t2_ps[:, 0:SBN], ACT.Copy).then_inc(h2_moved, 1)
                act.wait_ge(var_ready, m + 1)
                act.activation(st[:, 3, :], st[:, 2, :], ACT.Sqrt, bias=eps_t[0:CH, 0:1], scale=1.0 / F).then_inc(std_ready, 1)
                act.wait_ge(x2_turned, m + 1)
                act.activation(x2T, cnt_ps[1][0:F, 0:SBN], ACT.Copy).then_inc(x2_moved, 1)
                if s is not None:
                    move_agg2(s)

            def move_agg2(s):
                act.wait_ge(agg2_ready, s + 1)
                act.activation(g2S, agg_ps[:, 0:SBN], ACT.Copy).then_inc(agg2_moved, 1)

            move_agg2(0)
            with act.Fori(1, NSB) as s:
                layer2(s - 1, s)
            layer2(NSB - 1)

            act.wait_ge(flags, 1)
            left = act.value_load(flag_i[0:1, 0:1], min_val=0, max_val=1)
            with act.If_ne(act.to_reg(left), 0):
                general_begins(act)
                act.wait_ge(sums_done, 1)
                with act.Fori(0, NSB) as m:
                    act.wait_ge(h_ready, m + NSB)
                    act.sem_inc(act_at, 1)
                    act.activation(agg3S[:, 0, :], sumT[0:F + 1, bass.ds(m * SBN, SBN)], ACT.Copy).then_inc(agg_moved, 2)
                    move_xT(m + NSB)
                act.wait_ge(sums_done, 2)
                with act.Fori(0, NSB) as m:
                    act.wait_ge(u2_ready, m + NSB)
                    act.sem_inc(act_at, 1)
                    act.activation(g2S, sumT[:, bass.ds(m * SBN, SBN)], ACT.Copy).then_inc(agg2_moved, 1)
                    layer2(m + NSB)
                general_ends(act)

            def indices(g, k):
                act.activation(src_cur[k][:, :], src_e[:, bass.ds(g, 1), :].rearrange("p a j -> p (a j)"), ACT.Copy).then_inc(idx_made, 1)

            def edge_group(g, k, ahead=True):
                act.wait_ge(attr_turned, g + 1)
                act.activation(attrT[k], t_ps[:, 0:EJ * F], ACT.Copy).then_inc(attr_moved, 1)
                act.wait_ge(z_made, g + 1)
                act.activation(ex, zs, ACT.Exp, bias=ln_alpha[:, 0:1]).then_inc(selu_act, 1)
                act.activation(rl, zs, ACT.Relu).then_inc(selu_act, 1)
                if ahead:
                    indices(g + NB, k)

            act.wait_ge(edges_in, 96)
            for k in range(NB):
                indices(k, k)
            with act.Fori(0, (NEG - 1) // NB - 1) as r:
                for k in range(NB):
                    edge_group(r * NB + k, k)
            edge_group(NEG - 1 - NB, 0)
            edge_group(NEG - NB, 1, False)
            edge_group(NEG + 1 - NB, 2, False)
            edge_group(NEG - 1, 0, False)

            act.wait_ge(flagB, 1)
            left = act.value_load(flag_i[0:1, 1:2], min_val=0, max_val=1)
            with act.If_ne(act.to_reg(left), 0):
                edges_end(act)
                with act.Fori(0, NEG) as g:
                    act.wait_ge(ge_added, g + 1)
                    act.sem_inc(act_at, 1)
                    act.activation(src_cur[0][:, :], src_e[:, bass.ds(g, 1), :].rearrange("p a j -> p (a j)"), ACT.Copy).then_inc(ge_idx, 1)
                    act.wait_ge(ge_turned, g + 1)
                    act.activation(attrT[0], t_ps[:, 0:EJ * F], ACT.Copy).then_inc(ge_moved, 1)
                    act.wait_ge(ge_zs, g + 1)
                    act.activation(ex, zs, ACT.Exp, bias=ln_alpha[:, 0:1]).then_inc(ge_selu, 1)
                    act.activation(rl, zs, ACT.Relu).then_inc(ge_selu, 1)
                act.wait_ge(ge_added, NEG + 1)

            act.wait_ge(acc_added, NEG)

            def copy_sums(m, half):
                act.activation(accS[half], acc[:, bass.ds(m * SBN, SBN)], ACT.Copy).then_inc(accS_moved, 1)

            def first_half(m):
                act.wait_ge(zq_made, m + 1)
                act.activation(ex4, yv4, ACT.Exp, bias=ln_alpha[0:CH, 0:1]).then_inc(selu4, 1)
                act.activation(rl4, yv4, ACT.Relu).then_inc(selu4, 1)

            def second_half(m):
                act.wait_ge(msg4_turned, m + 1)
                act.activation(x2T, t_ps[0:F, 0:SBN], ACT.Copy).then_inc(msg4_moved, 1)
                act.wait_ge(var4, m + 1)
                act.activation(st[:, 3, :], st[:, 2, :], ACT.Sqrt, bias=eps_t[0:CH, 0:1], scale=1.0 / F).then_inc(std4, 1)

            copy_sums(0, 0)
            first_half(0)
            with act.Fori(0, NSB - 1) as m:
                act.wait_ge(m_ready, m + 1)
                act.sem_inc(act_at, 1)
                copy_sums(m + 1, 0)
                act.wait_ge(msg4_turned, m + 1)
                act.activation(x2T, t_ps[0:F, 0:SBN], ACT.Copy).then_inc(msg4_moved, 1)
                first_half(m + 1)
                act.wait_ge(var4, m + 1)
                act.activation(st[:, 3, :], st[:, 2, :], ACT.Sqrt, bias=eps_t[0:CH, 0:1], scale=1.0 / F).then_inc(std4, 1)
            second_half(NSB - 1)

        @block.tensor
        def _(pe):
            pe.sem_inc(groups_summed, SLOTS)
            pe.sem_inc(counts_moved, 2)
            pe.wait_ge(iota_set, 9)

            def turn_windows(n):
                pe.wait_ge(rel_ready, (n + 1) * 2)
                if not isinstance(n, int) or n > 0:
                    pe.wait_ge(win_moved, n * 2)
                for k in range(CHUNKS):
                    pe.transpose(t_ps[:, k * P:(k + 1) * P], rel[:, 0, k * P:(k + 1) * P], ident[:, :])
                for k in range(CHUNKS):
                    ins = pe.transpose(t2_ps[:, k * P:(k + 1) * P], rel[:, 1, k * P:(k + 1) * P], ident[:, :])
                ins.then_inc(win_turned, 1)

            def open_agg(s):
                if not isinstance(s, int) or s > 0:
                    pe.wait_ge(agg_moved, s * 2)
                pe.matmul(agg_ps[:, 0:SBN], zrow[:, 0:P], zrow[:, 0:SBN], start=True, stop=False, skip_group_check=True)
                pe.matmul(agg3_ps[:, 0:SBN], zrow[:, 0:P], zrow[:, 0:SBN], start=True, stop=False, skip_group_check=True)

            def layer(m, half, arrived=None):
                if arrived is not None:
                    pe.wait_ge(gl_in, arrived)
                elif isinstance(m, int):
                    pe.wait_ge(xm_in[half], 16 * (m // 2 + 1) + (16 if m == NSB - 1 else 0))
                else:
                    pe.wait_ge(xm_in[half], (m - half) * 8 + 16)
                if not isinstance(m, int) or m > 0:
                    pe.wait_ge(h_ready, m)
                pe.sem_inc(pe_at, 1)
                for c in range(NCH):
                    ins = pe.transpose(t_ps[0:F, c * CH:(c + 1) * CH], xm[:, half, c, :], ident[0:CH, 0:CH])
                ins.then_inc(xT_ready, 1)
                pe.wait_ge(agg_moved, m * 2 + 2)
                for c in range(NCH):
                    cols = slice(c * CH, (c + 1) * CH)
                    if arrived is None:
                        pe.matmul(u_ps[0:CH, c * H:(c + 1) * H], aggS[:, half, cols], Wl1s[:, :], start=True, stop=False, skip_group_check=True)
                    pe.matmul(u_ps[0:CH, c * H:(c + 1) * H], agg3S[0:F, half, cols], Wl1s[0:F, :], start=arrived is not None, stop=True, skip_group_check=True)
                pe.wait_ge(xT_moved, m + 1)
                for c in range(NCH):
                    pe.matmul(t_ps[0:CH, SBN + c:SBN + c + 1], agg3S[:, half, c * CH:(c + 1) * CH], cnt_sel[:, :], start=True, stop=True)
                for c in range(NCH):
                    ins = pe.matmul(v_ps[0:CH, c * H:(c + 1) * H], xTs[0:F, c * CH:(c + 1) * CH], Wr1s[:, :], start=True, stop=True)
                ins.then_inc(uv_ready, 1)

            def superblock(s, half, build=True, mult=True, with_layer=True):
                if mult:
                    open_agg(s - 1)
                    pe.wait_ge(counts_moved, s * SB_GROUPS + 2)
                    pe.sem_inc(pe_at, 1)
                with pe.Fori(0, BODIES) as b:
                    for k in range(BG):
                        if build:
                            G = (s * BODIES + b) * BG + (k + 1)
                            pe.wait_ge(hot_ready, G)
                            pe.wait_ge(counts_moved, G)
                            for c in range(CHUNKS):
                                ins = pe.matmul(cnt_ps[k % 2][:, 0:CODES], lane_hot[:, k % SLOTS, :, c],
                                                code_hot[:, k % SLOTS, :, c], start=(c == 0), stop=(c == CHUNKS - 1))
                            ins.then_inc(groups_summed, 1)
                        if mult and k < BH:
                            rhs = Asb(1 - half)[:, bass.ds(b * BH + k, 1), :].rearrange("p a n -> p (a n)")
                            l1 = X12[:, bass.ds(b * BH + k, 1), :].rearrange("p a n -> p (a n)")
                            l2 = X3[:, bass.ds(b * BH + k, 1), :].rearrange("p a n -> p (a n)")
                            pe.matmul(agg_ps[:, 0:SBN], l1, rhs, start=False, stop=True, skip_group_check=True)
                            pe.matmul(agg3_ps[0:F + 1, 0:SBN], l2, rhs, start=False, stop=True, skip_group_check=True)
                if mult:
                    pe.matmul(agg3_ps[0:F + 1, 0:SBN], zrow[:, 0:F + 1], zrow[:, 0:SBN], start=False, stop=True, skip_group_check=True).then_inc(agg_ready, 1)
                if with_layer:
                    layer(s - 2, half)

            turn_windows(0)
            superblock(0, 0, mult=False, with_layer=False)
            turn_windows(1)
            superblock(1, 1, with_layer=False)
            pe.wait_ge(w_in, 64)
            superblock(2, 0)
            turn_windows(2)
            superblock(3, 1)
            with pe.Fori(2, PAIRS) as pair:
                superblock(pair * 2, 0)
                turn_windows(pair + 1)
                superblock(pair * 2 + 1, 1)
            superblock(NSB, 0, build=False)
            layer(NSB - 1, 1)

            pe.wait_ge(w2_in, 16 * 18)
            pe.wait_ge(ones_set, 5)
            pe.wait_ge(h_ready, NSB)
            pe.wait_ge(chk_made, 1)
            pe.matmul(t2_ps[0:1, 0:1], chk[0:CH, 0:1], ones_c[0:CH, :], start=True, stop=True, skip_group_check=True).then_inc(chk_sum, 1)
            pe.transpose(t_ps[0:F, 0:F], W1bs[:, :], ident[0:F, 0:F])
            pe.matmul(v_ps[0:F, 0:1], W1bs[:, :], shift_b[:, 0:1], start=True, stop=True, skip_group_check=True).then_inc(wt_turned, 1)
            pe.wait_ge(wts_made, 1)
            pe.wait_ge(flags, 1)
            pe.matmul(t2_ps[0:CH, 0:F], u0b[:, :], W2au[:, :], start=True, stop=True)
            pe.matmul(t2_ps[0:CH, F:2 * F], shift_b[:, :], W2bs[:, :], start=True, stop=True, skip_group_check=True)
            pe.wait_ge(wt_moved, 1)
            pe.wait_ge(wts_made, 2)
            pe.matmul(t2_ps[0:F + 1, 2 * F:3 * F], WbT[:, :], W2am[:, :], start=True, stop=True, skip_group_check=True).then_inc(wts_ready, 1)
            pe.wait_ge(wts_made, 5)

            def sums2(s, half, m=None):
                if not isinstance(s, int) or s > 0:
                    pe.wait_ge(agg2_moved, s)
                pe.matmul(agg_ps[:, 0:SBN], zrow[:, 0:P], zrow[:, 0:SBN], start=True, stop=False, skip_group_check=True)
                if isinstance(s, int):
                    pe.wait_ge(A_in[half], (s // 2 + 1) * 16)
                else:
                    pe.wait_ge(A_in[half], (s - half) * 8 + 16)
                for b in range(BODIES):
                    for blk in range(b * BH, (b + 1) * BH):
                        for part in range(3):
                            ins = pe.matmul(agg_ps[:, 0:SBN], Hsb[:, part, blk, :], Asb(half)[:, blk, :], start=False,
                                            stop=(part == 2), skip_group_check=True)
                    if b == BODIES - 1:
                        ins.then_inc(agg2_ready, 1)
                    if m is not None:
                        layer2(m, b, 1 - half)

            def layer2(m, b, half, arrived=None):
                chunks = [slice(c * CH, (c + 1) * CH) for c in range(NCH)]
                if b == 0:
                    pe.wait_ge(gl_in, arrived) if arrived is not None else pe.wait_ge(hx_in[half], (m // 2 + 1) * 32 + (16 if m == NSB - 1 else 0) if isinstance(m, int) else (m - half) * 16 + 32)
                    for c in range(NCH):
                        ins = pe.transpose(t_ps[:, chunks[c]], h1m[half][:, c, :], ident[0:CH, 0:CH])
                    ins.then_inc(hT_turned, 1)
                    pe.wait_ge(agg2_moved, m + 1)
                    for c in range(NCH):
                        ins = pe.matmul(u_ps[0:CH, c * H:(c + 1) * H], g2S[:, chunks[c]], Wl2s[:, :], start=True, stop=True)
                    ins.then_inc(u2_ready, 1)
                if b == 1:
                    pe.wait_ge(hT_moved, m + 1)
                    for c in range(NCH):
                        ins = pe.matmul(v_ps[0:CH, c * H:(c + 1) * H], hTs[:, chunks[c]], Wr2s[:, :], start=True, stop=True)
                    ins.then_inc(v2_ready, 1)
                if b == 2:
                    pe.wait_ge(h2_ready, m + 1)
                    for c in range(NCH):
                        ins = pe.transpose(t2_ps[:, chunks[c]], hs[:, c, :], ident[0:CH, 0:CH])
                    ins.then_inc(h2_turned, 1)
                if b == 3:
                    pe.wait_ge(h2_moved, m + 1)
                    for c in range(NCH):
                        ins = pe.matmul(cnt_ps[0][0:CH, c * F:(c + 1) * F], h2T[:, chunks[c]], Wouts[:, :], start=True, stop=True)
                    ins.then_inc(o_ready, 1)
                if b == 5:
                    pe.wait_ge(x2_ready, m + 3)
                    pe.sem_inc(pe_at, 1)
                    for c in range(NCH):
                        ins = pe.transpose(cnt_ps[1][0:F, chunks[c]], x2c[:, c, :], ident[0:CH, 0:CH])
                    ins.then_inc(x2_turned, 1)
                if b == 6:
                    pe.wait_ge(x2_moved, m + 1)
                    for c in range(NCH):
                        ins = pe.matmul(agg3_ps[0:CH, c * 2 * F:(c + 1) * 2 * F], x2T[:, chunks[c]], Wxx[:, :], start=True, stop=True)
                    ins.then_inc(pq_ready, 1)

            pe.wait_ge(parts_in, 48)
            sums2(0, 0)
            with pe.Fori(0, PAIRS - 1) as j:
                sums2(j * 2 + 1, 1, j * 2)
                sums2(j * 2 + 2, 0, j * 2 + 1)
            sums2(NSB - 1, 1, NSB - 2)
            for b in range(BODIES):
                layer2(NSB - 1, b, 1)

            left = pe.value_load(flag_i[0:1, 0:1], min_val=0, max_val=1)
            with pe.If_ne(pe.to_reg(left), 0):
                general_begins(pe)
                with pe.Fori(0, NSB) as m:
                    layer(m + NSB, 0, m * 32 + 32)
                with pe.Fori(0, NSB) as m:
                    for b in range(BODIES):
                        layer2(m + NSB, b, 0, m * 48 + 48 + 32 * NSB)
                general_ends(pe)

            pe.wait_ge(base_made, 1)
            pe.matmul(t2_ps[:, 0:NEG], ones_r[:, :], base_f[:, :], start=True, stop=True).then_inc(bases_ready, 1)

            pe.wait_ge(chkB_made, 3)
            pe.matmul(t2_ps[0:1, 0:1], chk[:, 7:8], ones_c[:, :], start=True, stop=True).then_inc(chkB_sum, 1)

            def edge_group(g, k, z_ps, s_ps, first=False):
                if isinstance(g, int):
                    pe.wait_ge(attr_in[k], 16 * (g // NB + 1) + (16 if g == NEG - 1 else 0))
                else:
                    pe.wait_ge(attr_in[k], g_round * 16 + 16)
                if not first:
                    pe.wait_ge(attr_moved, g)
                for c in range(EJ // 2):
                    ins = pe.transpose(t_ps[:, c * P:(c + 1) * P], attr[k][:, c * P:(c + 1) * P], ident[:, :])
                ins.then_inc(attr_turned, 1)
                pe.wait_ge(attr_moved, g + 1)
                for c in range(EJ // 2):
                    ins = pe.matmul(z_ps[:, c * P:(c + 1) * P], attrT[k][:, c * P:(c + 1) * P], Wedge[:, :], start=True, stop=True)
                ins.then_inc(z_ready, 1)
                pe.wait_ge(msg_made, g + 1)
                for j in range(EJ):
                    ins = pe.matmul(s_ps[0:F + 1, 0:WIN], msg[k][:, j, :], hot[k][:, j, :], start=(j == 0), stop=(j == EJ - 1))
                ins.then_inc(seg_ready, 1)

            zb, sbk = [cnt_ps[0], cnt_ps[1], agg_ps], [agg3_ps, u_ps, v_ps]
            pe.wait_ge(p_ready, NSB)
            for k in range(NB):
                edge_group(k, k, zb[k], sbk[k], first=(k == 0))
            with pe.Fori(1, (NEG - 1) // NB) as r:
                g_round = r
                for k in range(NB):
                    edge_group(r * NB + k, k, zb[k], sbk[k])
            edge_group(NEG - 1, 0, zb[0], sbk[0])

            left = pe.value_load(flag_i[0:1, 1:2], min_val=0, max_val=1)
            with pe.If_ne(pe.to_reg(left), 0):
                edges_end(pe)

                def general_messages(g, arrived):
                    pe.wait_ge(ge_in, arrived)
                    for c in range(EJ // 2):
                        ins = pe.transpose(t_ps[:, c * P:(c + 1) * P], attr[0][:, c * P:(c + 1) * P], ident[:, :])
                    ins.then_inc(ge_turned, 1)
                    pe.wait_ge(ge_moved, g + 1)
                    for c in range(EJ // 2):
                        ins = pe.matmul(cnt_ps[0][:, c * P:(c + 1) * P], attrT[0][:, c * P:(c + 1) * P], Wedge[:, :], start=True, stop=True)
                    ins.then_inc(ge_z, 1)
                    pe.wait_ge(ge_msg, g + 1)
                    for j in range(EJ):
                        ins = pe.transpose((u_ps, v_ps)[j // 4][0:F + 1, (j % 4) * P:(j % 4 + 1) * P], msg[0][:, j, :], ident[:, :])
                    ins.then_inc(ge_msgT, 1)
                with pe.Fori(0, NEG - 1) as g:
                    general_messages(g, g * 32 + 32)
                general_messages(NEG - 1, NEG * 32 + 16)
                pe.wait_ge(ge_added, NEG + 1)

            chunks = [slice(c * CH, (c + 1) * CH) for c in range(NCH)]
            pe.wait_ge(acc_added, NEG)

            def sums_times(m):
                pe.wait_ge(accS_moved, m + 1)
                for c in range(NCH):
                    ins = pe.matmul(u_ps[0:CH, c * F:(c + 1) * F], accS[0][:, chunks[c]], Wc[:, :], start=True, stop=True)
                ins.then_inc(m_ready, 1)

            def turn_msg(m):
                pe.wait_ge(msg4_made, m + 1)
                pe.sem_inc(pe_at, 1)
                for c in range(NCH):
                    ins = pe.transpose(t_ps[0:F, chunks[c]], msg4[:, c * F:(c + 1) * F], ident[0:CH, 0:CH])
                ins.then_inc(msg4_turned, 1)

            def last_product(m):
                pe.wait_ge(msg4_moved, m + 1)
                for c in range(NCH):
                    ins = pe.matmul(v_ps[0:CH, c * F:(c + 1) * F], x2T[:, chunks[c]], W2bs[:, :], start=True, stop=True)
                ins.then_inc(y_ready, 1)

            sums_times(0)
            with pe.Fori(0, NSB - 1) as m:
                turn_msg(m)
                sums_times(m + 1)
                last_product(m)
            turn_msg(NSB - 1)
            last_product(NSB - 1)

        @block.vector
        def _(dve):
            n0 = [0]

            def step(ins):
                n0[0] += 1
                ins.then_inc(dve0, 1)
                dve.wait_ge(dve0, n0[0])

            dve.sem_inc(x2_ready, 2)
            dve.wait_ge(dst_in, 32)
            dve.tensor_copy(f16, dst_i.rearrange("p (r c) -> p r c", c=ROW)[:, :, 0]).then_inc(firsts_made, 1)
            dve.tensor_scalar(grp_i, dst_i, 3, None, ALU.arith_shift_right).then_inc(dve0, 1)
            dve.tensor_scalar(pos_i, dst_i, GROUP - 1, None, ALU.bitwise_and).then_inc(dve0, 1)
            dve.wait_ge(src_in, 32)
            dve.tensor_scalar(lane_i, src_i, P - 1, None, ALU.bitwise_and).then_inc(dve0, 1)
            dve.tensor_scalar(blk_i, src_i, 7, None, ALU.arith_shift_right).then_inc(dve0, 1)
            n0[0] = 4
            dve.wait_ge(dve0, 4)
            step(dve.scalar_tensor_tensor(code_a, grp_i, float(CODES), pos_i, ALU.mult, ALU.add))
            r3 = lambda ap: ap.rearrange("p (r c) -> p r c", c=ROW)
            dve.scalar_tensor_tensor(comb[:, :, ROW:2 * ROW], r3(blk_i), float(GROUP), r3(code_a), ALU.mult, ALU.add).then_inc(dve0, 1)
            dve.tensor_copy(comb[:, :, 0:ROW], r3(lane_i)).then_inc(dve0, 1)
            n0[0] += 2
            dve.wait_ge(dve0, n0[0])
            dve.sem_inc(table_made, 1)

            def find_windows(n, first=False):
                dve.tensor_scalar(junk, firsts, thr[:, bass.ds(n, 1)], None, ALU.is_lt, ALU.add,
                                  accum_out=below[:, bass.ds(n, 1)]).then_inc(win_dve, 1)
                dve.wait_ge(win_dve, n * 3 + 1)
                dve.tensor_scalar(start[:, bass.ds(n, 1)], below[:, bass.ds(n, 1)], -1.0, 0.0, ALU.add, ALU.max).then_inc(win_dve, 1)
                dve.wait_ge(win_dve, n * 3 + 2)
                if not first:
                    dve.wait_ge(win_in, n * (16 * WROWS))
                dve.tensor_scalar(rows12[:, 0, :], iota_w[:, 0:WROWS], start[:, bass.ds(n, 1)], None, ALU.add).then_inc(rows_ready, 1)

            def rel_windows(n):
                dve.wait_ge(win_in, (n + 1) * (16 * WROWS))
                dve.tensor_scalar(start[:, bass.ds(n, 1)], code0[:, bass.ds(n, 1)], float(CODES), -1.0, ALU.mult, ALU.add).then_inc(win_dve, 1)
                dve.wait_ge(win_dve, n * 3 + 3)
                r4 = rel.rearrange("p a (r c) -> p a r c", c=ROW)
                dve.tensor_scalar(r4[:, 0], win[:, :, 0:ROW], 1.0, None, ALU.add).then_inc(rel_ready, 1)
                dve.tensor_scalar(r4[:, 1], win[:, :, ROW:2 * ROW], start[:, bass.ds(n, 1)], 2040.0, ALU.subtract, ALU.min).then_inc(rel_ready, 1)

            def superblock(s, with_layer=True):
                with dve.Fori(0, BODIES) as b:
                    for k in range(BG):
                        g = s * SB_GROUPS + b * BG + k
                        dve.wait_ge(groups_summed, g + 1)
                        dve.tensor_tensor(lane_hot[:, k % SLOTS], iota_code[:, 0:P, :],
                                          laneT[:, bass.ds(g, 1), :].to_broadcast([P, P, CHUNKS]), ALU.is_equal)
                        dve.tensor_tensor(code_hot[:, k % SLOTS], iota_code[:, :, :],
                                          codeT[:, bass.ds(g, 1), :].to_broadcast([P, CODES, CHUNKS]), ALU.is_equal).then_inc(hot_ready, 1)
                if with_layer:
                    layer(s - 2)

            def grid(ap, f):
                return ap[0:CH, 0:NCH * f].rearrange("p (c f) -> p c f", f=f)

            def wide(ap, f):
                return ap.unsqueeze(2).to_broadcast([CH, NCH, f])

            def every(ap, f):
                return ap.unsqueeze(1).to_broadcast([CH, NCH, f])

            def layer(m, at=None):
                i = [0]

                def link(ins):
                    i[0] += 1
                    ins.then_inc(layer_dve, 1)
                    dve.wait_ge(layer_dve, m * 6 + i[0])
                at = m if at is None else at
                dve.wait_ge(uv_ready, m + 1)
                link(dve.tensor_scalar(ctmp[:, :], t_ps[0:CH, SBN:SBN + NCH], 1.0, None, ALU.max))
                link(dve.reciprocal(inv_c[:, :], ctmp[:, :]))
                link(dve.tensor_tensor(cnt_all[:, bass.ds(at, 1), :].rearrange("p a c -> p (a c)"), t_ps[0:CH, SBN:SBN + NCH], zero_c[:, :], ALU.add))
                link(dve.tensor_tensor(ht[:, :, :], grid(u_ps, H), wide(inv_c[:, :], H), ALU.mult))
                link(dve.tensor_tensor(hv[:, :, :], grid(v_ps, H), every(bl1s[:, :], H), ALU.add))
                link(dve.tensor_tensor(ht[:, :, :], ht[:, :, :], hv[:, :, :], ALU.add))
                if not isinstance(m, int) or m > 0:
                    dve.wait_ge(h_stored, m * 64)
                dve.tensor_scalar(hs[:, :, :], ht[:, :, :], 0.0, None, ALU.max).then_inc(h_ready, 1)

            dve.wait_ge(iota_set, 9)
            dve.wait_ge(firsts_in, 16)
            dve.wait_ge(consts, 2)
            step(dve.memset(zero_c[:, :], 0.0))
            find_windows(0, True)
            dve.wait_ge(x1_made, 1)
            x3 = x_rows.rearrange("p (b f) -> p b f", f=F)
            xr = x_rest.rearrange("p (b f) -> p b f", f=F)
            step(dve.tensor_tensor(xr, x3, X12[:, :, 0:F], ALU.subtract))
            step(dve.tensor_copy(X12[:, :, F:2 * F], xr))
            step(dve.tensor_tensor(xr, xr, X12[:, :, F:2 * F], ALU.subtract))
            step(dve.tensor_copy(X3[:, :, 0:F], xr))
            rel_windows(0)
            find_windows(1)
            dve.wait_ge(win_moved, 2)
            superblock(0, False)
            rel_windows(1)
            dve.wait_ge(win_moved, 4)
            superblock(1, False)
            with dve.Fori(1, PAIRS) as pair:
                find_windows(pair + 1)
                superblock(pair * 2)
                rel_windows(pair + 1)
                dve.wait_ge(win_moved, pair * 2 + 4)
                dve.sem_inc(dve_at, 1)
                superblock(pair * 2 + 1)
            layer(NSB - 2)
            layer(NSB - 1)

            all_counts = cnt_all[:, :, :].rearrange("p m c -> p (m c)")

            def inverses(i):
                dve.tensor_scalar(inv[:, :, :], cnt_all[:, :, :], 1.0, None, ALU.max).then_inc(inv_made, 1)
                dve.wait_ge(inv_made, 2 * i + 1)
                dve.reciprocal(inv[:, :, :], inv[:, :, :]).then_inc(inv_made, 1)
                dve.wait_ge(inv_made, 2 * i + 2)
            dve.wait_ge(h_ready, NSB)
            inverses(0)
            dve.tensor_reduce(chk[0:CH, 0:1], all_counts, AX_X, ALU.add).then_inc(chk_made, 1)
            dve.wait_ge(chk_sum, 1)
            dve.tensor_scalar(flag_i[0:1, 0:1], t2_ps[0:1, 0:1], float(E), None, ALU.not_equal).then_inc(flags, 1)

            dve.wait_ge(w2_in, 16 * 18)
            dve.tensor_scalar(u0b[:, :], shift_b[:, :], 0.0, u0[:, 0:1], ALU.mult, ALU.add).then_inc(wts_made, 1)
            dve.wait_ge(wt_turned, 1)
            dve.tensor_tensor(WbT[:, F:F + 1], v_ps[0:F, 0:1], b1bcol[:, :], ALU.add).then_inc(wts_made, 1)
            dve.wait_ge(wts_ready, 1)
            dve.tensor_tensor(c2[:, :], t2_ps[0:CH, 0:F], b2as[:, :], ALU.add).then_inc(wts_made, 1)
            dve.tensor_copy(Wc[:, :], t2_ps[0:F + 1, 2 * F:3 * F]).then_inc(wts_made, 1)
            dve.tensor_scalar(W2bs[:, :], W2bs[:, :], SCALE, None, ALU.mult).then_inc(wts_made, 1)
            step(dve.tensor_tensor(b2bs[:, :], t2_ps[0:CH, F:2 * F], b2bs[:, :], ALU.add))

            def normalise(link, to, var, std, m):
                link(dve.tensor_reduce(st[:, 0, :], yv[:, :, :], AX_X, ALU.add))
                link(dve.tensor_scalar(st[:, 1, :], st[:, 0, :], -1.0 / F, None, ALU.mult))
                link(dve.tensor_tensor(yd[:, :, :], yv[:, :, :], wide(st[:, 1, :], F), ALU.add))
                link(dve.tensor_tensor(yv[:, :, :], yd[:, :, :], yd[:, :, :], ALU.mult))
                dve.tensor_reduce(st[:, 2, :], yv[:, :, :], AX_X, ALU.add).then_inc(var, 1)
                dve.wait_ge(std, m + 1)
                link(dve.reciprocal(st[:, 0, :], st[:, 3, :]))

            def layer2(m, half, at=None):
                i = [0]
                at = m if at is None else at

                def link(ins):
                    i[0] += 1
                    ins.then_inc(dve2, 1)
                    dve.wait_ge(dve2, m * 11 + i[0])
                dve.wait_ge(u2_ready, m + 1)
                link(dve.tensor_tensor(inv_c[:, :], inv[:, bass.ds(at, 1), :].rearrange("p a c -> p (a c)"), zero_c[:, :], ALU.add))
                link(dve.tensor_tensor(ht[:, :, :], grid(u_ps, H), wide(inv_c[:, :], H), ALU.mult))
                dve.wait_ge(v2_ready, m + 1)
                link(dve.tensor_tensor(hv[:, :, :], grid(v_ps, H), every(bl2s[:, :], H), ALU.add))
                link(dve.tensor_tensor(ht[:, :, :], ht[:, :, :], hv[:, :, :], ALU.add))
                dve.tensor_scalar(hs[:, :, :], ht[:, :, :], 0.0, None, ALU.max).then_inc(h2_ready, 1)
                dve.wait_ge(o_ready, m + 1)
                link(dve.tensor_tensor(yd[:, :, :], grid(cnt_ps[0], F), every(bouts[:, :], F), ALU.add))
                link(dve.tensor_tensor(yv[:, :, :], yd[:, :, :], xm[:, half, :, :], ALU.add))
                normalise(link, None, var_ready, std_ready, m)
                if not isinstance(m, int) or m > 0:
                    dve.wait_ge(x2_kept, m)
                dve.tensor_tensor(x2c[:, :, :], yd[:, :, :], wide(st[:, 0, :], F), ALU.mult).then_inc(x2_ready, 1)
                dve.wait_ge(pq_ready, m + 1)
                pq = grid(agg3_ps, 2 * F)
                dve.tensor_tensor(q2all[:, bass.ds(at, 1), :, :].rearrange("p a c f -> p (a c) f"), pq[:, :, F:2 * F], every(c2[:, :], F), ALU.add)
                if not isinstance(m, int) or m > 0:
                    dve.wait_ge(p_stored, m * 16)
                dve.tensor_tensor(pc[:, :, :], pq[:, :, 0:F], every(b1as[:, :], F), ALU.add).then_inc(p_ready, 1)

            dve.wait_ge(hx_in[0], 32)
            layer2(0, 0)
            with dve.Fori(0, PAIRS - 1) as j:
                dve.wait_ge(hx_in[1], j * 32 + 32)
                layer2(j * 2 + 1, 1)
                dve.wait_ge(hx_in[0], j * 32 + 64)
                layer2(j * 2 + 2, 0)
            dve.wait_ge(hx_in[1], 32 * PAIRS + 16)
            layer2(NSB - 1, 1)

            def general_sums(rows, i):
                dve.wait_ge(g_set, 2 * i + 2)
                dve.wait_ge(feat_in, 16 * (N // GN) * (i + 1))
                with dve.Fori(0, E // GE) as c:
                    dve.wait_ge(ends_in, c * 32 + 32 * (i * (E // GE) + 1))
                    dve.sem_inc(dve_at, 1)
                    with dve.Fori(0, GE) as e:
                        of = dve.value_load(ends[0:1, 0, bass.ds(e, 1)], min_val=0, max_val=N - 1)
                        to = dve.value_load(ends[0:1, 1, bass.ds(e, 1)], min_val=0, max_val=N - 1)
                        dve.tensor_tensor(sumT[0:rows, bass.ds(to, 1)], sumT[0:rows, bass.ds(to, 1)],
                                          featT[0:rows, bass.ds(of, 1)], ALU.add).then_inc(col_added, 1)
                        dve.wait_ge(col_added, c * GE + (e + (i * E + 1)))
                        dve.sem_inc(dve_at, 1)
                    dve.sem_inc(chunk_added, 1)
                dve.sem_inc(sums_done, 1)

            dve.wait_ge(flags, 1)
            left = dve.value_load(flag_i[0:1, 0:1], min_val=0, max_val=1)
            with dve.If_ne(dve.to_reg(left), 0):
                general_begins(dve)
                dve.sem_inc(chunk_added, 1)
                general_sums(F + 1, 0)
                with dve.Fori(0, NSB) as m:
                    layer(m + NSB, m)
                dve.wait_ge(h_ready, 2 * NSB)
                inverses(1)
                general_sums(H, 1)
                with dve.Fori(0, NSB) as m:
                    layer2(m + NSB, 0, m)
                general_ends(dve)

            dve.wait_ge(base_in, 32)
            dve.wait_ge(edges_in, 96)
            dve.tensor_copy(base_f[:, :], base_i[:, :]).then_inc(base_made, 1)
            dve.wait_ge(bases_ready, 1)
            dve.tensor_tensor(drel, dst_e, t2_ps[:, 0:NEG].unsqueeze(2).to_broadcast([P, NEG, EJ]), ALU.subtract).then_inc(drel_made, 1)
            dve.wait_ge(drel_made, 1)
            flat = drel.rearrange("p g j -> p (g j)")
            dve.tensor_scalar(in_window, flat, 0.0, None, ALU.is_ge, ALU.add, accum_out=chk[:, 5:6]).then_inc(chkB_made, 1)
            dve.wait_ge(chkB_made, 1)
            dve.tensor_scalar(in_window, flat, float(WIN), None, ALU.is_ge, ALU.add, accum_out=chk[:, 6:7]).then_inc(chkB_made, 1)
            dve.wait_ge(chkB_made, 2)
            dve.tensor_tensor(chk[:, 7:8], chk[:, 5:6], chk[:, 6:7], ALU.subtract).then_inc(chkB_made, 1)
            dve.wait_ge(chkB_sum, 1)
            dve.tensor_scalar(flag_i[0:1, 1:2], t2_ps[0:1, 0:1], float(E), None, ALU.not_equal).then_inc(flagB, 1)
            dve.wait_ge(acc_zero, 1 + NB)

            def edge_group(g, k, z_ps, last=None, r=None, first=False):
                dve.wait_ge(gath_in[k], (g // NB + 1) * (16 * EJ) if isinstance(g, int) else r * (16 * EJ) + 16 * EJ)
                dve.wait_ge(z_ready, g + 1)
                if not first:
                    dve.wait_ge(selu_act, g * 2)
                dve.tensor_tensor(zs, z_ps[:, 0:EJ * F], gath[k], ALU.add).then_inc(z_made, 1)
                if not first:
                    dve.wait_ge(seg_ready, g)
                dve.tensor_tensor(hot[k], iota_w[:, :].unsqueeze(1).to_broadcast([P, EJ, WIN]),
                                  drel[:, bass.ds(g, 1), :].rearrange("p a j -> p (a j)").unsqueeze(2).to_broadcast([P, EJ, WIN]),
                                  ALU.is_equal).then_inc(hot_made, 1)
                if last is not None:
                    last()
                dve.wait_ge(selu_act, g * 2 + 2)
                e3, r3 = (b.rearrange("p (j f) -> p j f", f=F) for b in (ex, rl))
                dve.scalar_tensor_tensor(msg[k][:, :, 0:F], e3, ALPHA, r3, ALU.min, ALU.add).then_inc(msg_made, 1)

            def add_sums(g, s_ps, first=False):
                dve.wait_ge(seg_ready, g + 1)
                if not first:
                    dve.wait_ge(acc_added, g)
                base = dve.value_load(base_i[0:1, bass.ds(g, 1)], min_val=0, max_val=N - 1)
                win_acc = acc[:, bass.ds(base, WIN)]
                dve.tensor_tensor(win_acc, win_acc, s_ps[0:F + 1, 0:WIN], ALU.add).then_inc(acc_added, 1)

            zb, sbk = [cnt_ps[0], cnt_ps[1], agg_ps], [agg3_ps, u_ps, v_ps]
            edge_group(0, 0, zb[0], first=True)
            edge_group(1, 1, zb[1], lambda: add_sums(0, sbk[0], True))
            edge_group(2, 2, zb[2], lambda: add_sums(1, sbk[1]))
            with dve.Fori(1, (NEG - 1) // NB) as r:
                for k in range(NB):
                    edge_group(r * NB + k, k, zb[k], lambda: add_sums(r * NB + (k - 1), sbk[(k - 1) % NB]), r)
            edge_group(NEG - 1, 0, zb[0], lambda: add_sums(NEG - 2, sbk[2]))
            add_sums(NEG - 1, sbk[0])

            dve.wait_ge(flagB, 1)
            left = dve.value_load(flag_i[0:1, 1:2], min_val=0, max_val=1)
            with dve.If_ne(dve.to_reg(left), 0):
                edges_end(dve)
                dve.sem_inc(ge_added, 1)
                dve.wait_ge(ge_zero, 1)

                def general_edges(g, arrived):
                    dve.wait_ge(ge_rows, g * 16 * EJ + 16 * EJ)
                    dve.wait_ge(ge_z, g + 1)
                    dve.tensor_tensor(zs, cnt_ps[0][:, 0:EJ * F], gath[0], ALU.add).then_inc(ge_zs, 1)
                    dve.wait_ge(ge_selu, g * 2 + 2)
                    e3, r3 = (b.rearrange("p (j f) -> p j f", f=F) for b in (ex, rl))
                    dve.scalar_tensor_tensor(msg[0][:, :, 0:F], e3, ALPHA, r3, ALU.min, ALU.add).then_inc(ge_msg, 1)
                    dve.wait_ge(ge_msgT, g + 1)
                    dve.wait_ge(ge_in, arrived)
                    dve.sem_inc(dve_at, 1)
                    with dve.Fori(0, P) as e:
                        for j in range(EJ):
                            to = dve.value_load(dst_row[0:1, bass.ds(e * EJ + j, 1)], min_val=0, max_val=N + WIN - 1)
                            dve.tensor_tensor(acc[:, bass.ds(to, 1)], acc[:, bass.ds(to, 1)],
                                              (u_ps, v_ps)[j // 4][0:F + 1, bass.ds(e + (j % 4) * P, 1)], ALU.add).then_inc(ge_col, 1)
                            dve.wait_ge(ge_col, g * EG + (e * EJ + (j + 1)))
                            dve.sem_inc(dve_at, 1)
                    dve.sem_inc(ge_added, 1)
                with dve.Fori(0, NEG - 1) as g:
                    general_edges(g, g * 32 + 32)
                general_edges(NEG - 1, NEG * 32 + 16)

            def link4(m, i):
                def link(ins):
                    i[0] += 1
                    ins.then_inc(dve4, 1)
                    dve.wait_ge(dve4, m * 7 + i[0])
                return link

            def first_half(m):
                dve.wait_ge(m_ready, m + 1)
                dve.sem_inc(dve_at, 1)
                dve.tensor_tensor(zm4.rearrange("p (c f) -> p c f", f=F), grid(u_ps, F), wide(inv[:, bass.ds(m, 1), :].rearrange("p a c -> p (a c)"), F), ALU.mult).then_inc(zm_made, 1)
                dve.wait_ge(zm_made, m + 1)
                dve.tensor_tensor(yv4.rearrange("p (c f) -> p c f", f=F), zm4.rearrange("p (c f) -> p c f", f=F), q2all[:, bass.ds(m, 1), :, :].rearrange("p a c f -> p (a c) f"), ALU.add).then_inc(zq_made, 1)

            def make_msg(m):
                dve.wait_ge(selu4, m * 2 + 2)
                dve.scalar_tensor_tensor(msg4, ex4, ALPHA, rl4, ALU.min, ALU.add).then_inc(msg4_made, 1)

            def second_half(m):
                link = link4(m, [0])
                dve.wait_ge(y_ready, m + 1)
                link(dve.tensor_tensor(yd[:, :, :], grid(v_ps, F), every(b2bs[:, :], F), ALU.add))
                if not isinstance(m, int) or m > 0:
                    dve.wait_ge(row_stored, m * 16)
                link(dve.tensor_tensor(yv[:, :, :], yd[:, :, :], x2all[:, bass.ds(m, 1), :, :].rearrange("p a c f -> p (a c) f"), ALU.add))
                normalise(link, None, var4, std4, m)
                dve.tensor_tensor(yv[:, :, :], yd[:, :, :], wide(st[:, 0, :], F), ALU.mult).then_inc(row_made, 1)

            first_half(0)
            make_msg(0)
            with dve.Fori(0, NSB - 1) as m:
                first_half(m + 1)
                second_half(m)
                make_msg(m + 1)
            second_half(NSB - 1)


_INS = ['x', 'src', 'dst', 'edge_attr_64', 'L0_gnn_W_l1', 'L0_gnn_b_l1', 'L0_gnn_W_r1', 'L0_gnn_W_l2', 'L0_gnn_b_l2',
        'L0_gnn_W_r2', 'L0_gnn_W_out', 'L0_gnn_b_out', 'L1_gnn_u', 'L1_gnn_W1a', 'L1_gnn_b1a', 'L1_gnn_W1b',
        'L1_gnn_b1b', 'L1_gnn_W2a', 'L1_gnn_b2a', 'L1_gnn_W2b', 'L1_gnn_b2b']


def kernel(**inputs):
    import numpy as _np
    import concourse.bacc as _bacc
    from concourse import mybir as _mybir
    from concourse.bass_utils import run_bass_kernel_spmd as _run

    nc = _bacc.Bacc("TRN2", target_bir_lowering=False, num_devices=1)
    arrays, args = {}, []
    for name in _INS:
        a = _np.ascontiguousarray(inputs[name])
        arrays[f"in_{name}_dram"] = a
        args.append(nc.dram_tensor(f"in_{name}_dram", a.shape, _mybir.dt.from_np(a.dtype), kind="ExternalInput").ap())
    out = nc.dram_tensor("out_0_dram", (N, F), F32, kind="ExternalOutput").ap()
    build(nc, *args, out)
    r = _run(nc, [arrays], core_ids=[0])
    return r.results[0]["out_0_dram"]
```

```python
from contextlib import ExitStack

import math

import concourse.bass as bass
from concourse import mybir

F32 = mybir.dt.float32
BF16 = mybir.dt.bfloat16
FP16 = mybir.dt.float16
I32 = mybir.dt.int32
I16 = mybir.dt.int16
ALU = mybir.AluOpType
ACT = mybir.ActivationFunctionType
AX_X = mybir.AxisListType.X

P = 128
N = 6250
E = 206250
F = 64
H = 128
EPS = 1e-5
ALPHA = 1.6732632423543772848170429916717
SCALE = 1.0507009873554804934193349852946
LN_ALPHA = math.log(ALPHA)

SRC_BLOCKS = -(-N // P)
EARLY = 42
GROUP = 8
CODES = SRC_BLOCKS * GROUP
CHUNKS = 3
ROW = 32
WROWS = CHUNKS * P // ROW
EPP = 51 * ROW
TROWS = P * EPP // ROW
RPP = EPP // ROW
NO_NODE = 20000

SB_GROUPS = 56
SBN = SB_GROUPS * GROUP
NSB = 14
PAIRS = NSB // 2
BODIES = 7
BG = SB_GROUPS // BODIES
BH = SRC_BLOCKS // BODIES
SLOTS = 8
CH = 112
NCH = SBN // CH
NPAD = NSB * SBN

EG = 1024
EJ = EG // P
NEG = -(-E // EG)
ETAIL = E - (NEG - 1) * EG
WIN = 64

GN = 250
GE = 1250

assert N % GN == 0 and E % GE == 0
assert EARLY * P == (NSB - 2) * SBN
assert NPAD >= N and SRC_BLOCKS == BODIES * BH and NCH * CH == SBN


def build(nc, x, src, dst, edge_attr, Wl1, bl1, Wr1, Wl2, bl2, Wr2, Wout, bout,
          u, W1a, b1a, W1b, b1b, W2a, b2a, W2b, b2b, out):
    def dram(name, shape, dt):
        return nc.dram_tensor(name, shape, dt, kind="Internal").ap()

    table = dram("edge_table", [TROWS, 2 * ROW], F32)
    firsts_d = dram("first_dst", [P, RPP], I16)
    coarse_d = dram("coarse_dst", [P], I16)
    A_d = dram("counts_matrix", [NSB, P, SRC_BLOCKS * SBN], FP16)
    hp_d = dram("h1_parts", [3, NPAD, H], BF16)
    h1_d = dram("h1_rows", [NPAD, H], F32)
    p_d = dram("source_terms", [NPAD, F], F32)

    with ExitStack() as ctx:
        def sb(name, shape, dt):
            return ctx.enter_context(nc.sbuf_tensor(name, shape, dt))

        def sem(name):
            return ctx.enter_context(nc.semaphore(name))

        def bank(name, shape, dt=F32):
            return ctx.enter_context(nc.psum_tensor(name, shape, dt))

        A_sb = sb("A_sb", [P, 2, SRC_BLOCKS * SBN], FP16)
        wT = CHUNKS * 8 * P // 2
        ar1 = sb("arena1", [P, 3 * SRC_BLOCKS * H // 2 + 2 * NCH * H + NCH * F], F32)
        w1 = SRC_BLOCKS * 2 * F // 2
        w2 = w1 + SRC_BLOCKS * (F + 2) // 2
        X12 = ar1[:, 0:w1].bitcast(BF16).rearrange("p (b f) -> p b f", f=2 * F)
        X3 = ar1[:, w1:w2].bitcast(BF16).rearrange("p (b f) -> p b f", f=F + 2)[:, :, 0:F + 1]
        laneT = ar1[:, w2:w2 + wT].bitcast(FP16).rearrange("p (g k) -> p g k", k=CHUNKS)
        codeT = ar1[:, w2 + wT:w2 + 2 * wT].bitcast(FP16).rearrange("p (g k) -> p g k", k=CHUNKS)
        Hsb = ar1[:, 0:3 * SRC_BLOCKS * H // 2].bitcast(BF16).rearrange("p (a b f) -> p a b f", a=3, f=H)
        wl = SLOTS * CHUNKS * P // 2
        wc = wl + SLOTS * CHUNKS * CODES // 2
        ar2 = sb("arena2", [P, max(wc + P // 4, 2 * NSB * NCH * F)], F32)
        lane_hot = ar2[:, 0:wl].bitcast(FP16).rearrange("p (s n c) -> p s n c", s=SLOTS, c=CHUNKS)
        code_hot = ar2[:, wl:wc].bitcast(FP16).rearrange("p (s n c) -> p s n c", s=SLOTS, c=CHUNKS)
        junk = ar2[:, wc:wc + P // 4].bitcast(mybir.dt.uint8)
        x2all = ar2[0:CH, 0:NSB * NCH * F].rearrange("p (m c f) -> p m c f", c=NCH, f=F)
        q2all = ar2[0:CH, NSB * NCH * F:2 * NSB * NCH * F].rearrange("p (m c f) -> p m c f", c=NCH, f=F)
        wf = P // 2 + 4 * RPP
        ww = wf + WROWS * 2 * ROW
        wr = ww + 2 * WROWS * ROW
        ar3 = sb("arena3", [P, max(wr, 2 * NEG * EJ)], F32)
        win = ar3[:, wf:ww].rearrange("p (r c) -> p r c", c=2 * ROW)
        rel = ar3[:, ww:wr].rearrange("p (a n) -> p a n", a=2)
        coarse = ar3[:, 0:P // 2].bitcast(I16)
        fine = ar3[:, P // 2:P // 2 + 4 * RPP].bitcast(I16).rearrange("p (n r) -> p n r", n=8)
        src_e = ar3[:, 0:NEG * EJ].bitcast(I32).rearrange("p (g j) -> p g j", j=EJ)
        dst_e = ar3[:, NEG * EJ:2 * NEG * EJ].bitcast(I32).rearrange("p (g j) -> p g j", j=EJ)
        drel = ar3[:, NEG * EJ:2 * NEG * EJ].rearrange("p (g j) -> p g j", j=EJ)
        rows12 = sb("rows12", [P, 1, WROWS], I32)
        below = sb("below", [P, 8], F32)
        part_of = sb("part_of", [P, 8], I32)
        part_row = sb("part_row", [P, 8], F32)
        start = sb("start", [P, 8], F32)
        iota_code = sb("iota_code", [P, CODES, CHUNKS], FP16)
        iota_i = sb("iota_i", [P, 512], I32)
        iota_w = sb("iota_w", [P, WIN], F32)
        thr = sb("thr", [P, 8], F32)
        code0 = sb("code0", [P, 8], F32)
        ident = sb("ident", [P, P], F32)
        zrow = sb("zrow", [P, 512], BF16)
        aggS = sb("aggS", [P, 2, SBN], F32)
        agg3S = sb("agg3S", [F + 1, 2, SBN], F32)
        xm = sb("xm", [CH, 2, NCH, F], F32)
        xTs = sb("xTs", [P, SBN], F32)
        Wl1s = sb("Wl1s", [P, H], F32)
        Wr1s = sb("Wr1s", [F + 1, H], F32)
        cnt_sel = sb("cnt_sel", [F + 1, 1], F32)
        ctmp = sb("ctmp", [CH, NCH], F32)
        inv_c = sb("inv_c", [CH, NCH], F32)
        inv = sb("inv", [CH, NSB, NCH], F32)
        cnt_all = sb("cnt_all", [CH, NSB, NCH], F32)
        chk = sb("chk", [P, 8], F32)
        flag_i = sb("flag_i", [1, 2], I32)
        hs = sb("hs", [CH, NCH, H], F32)
        ht = sb("ht", [CH, NCH, H], F32)
        hv = sb("hv", [CH, NCH, H], F32)
        hpart = sb("hpart", [CH, 3, NCH, H], BF16)
        Wl2s, Wr2s = sb("Wl2s", [H, H], F32), sb("Wr2s", [H, H], F32)
        Wouts = sb("Wouts", [H, F], F32)
        bl2s, bouts = sb("bl2s", [CH, H], F32), sb("bouts", [CH, F], F32)
        Wxx = sb("Wxx", [F, 2 * F], F32)
        Wedge = sb("Wedge", [P, 2 * F], F32)
        W1bs, W2am, W2au, W2bs = (sb(n, [F, F], F32) for n in ("W1bs", "W2am", "W2au", "W2bs"))
        b1as, b2as, b2bs = (sb(n, [CH, F], F32) for n in ("b1as", "b2as", "b2bs"))
        b1bcol, u0 = sb("b1bcol", [F, 1], F32), sb("u0", [F, 1], F32)
        u0b = sb("u0b", [F, CH], F32)
        shift_b = sb("shift_b", [F, CH], F32)
        WbT = sb("WbT", [F, F + 1], F32)
        Wc = sb("Wc", [F + 1, F], F32)
        c2 = sb("c2", [CH, F], F32)
        ln_alpha = sb("ln_alpha", [P, 1], F32)
        eps_t = sb("eps_t", [P, 1], F32)
        base_i = sb("base_i", [1, NEG], I32)
        base_f = sb("base_f", [1, NEG], F32)
        ones_r = sb("ones_r", [1, P], F32)
        ones_c = sb("ones_c", [P, 1], F32)

        A_raw = A_sb[:, :, :].rearrange("p a b -> p (a b)")

        def over(at, n, dt):
            return A_raw[:, at // 2:(at + n * 4) // 2].bitcast(dt)

        src_i = over(0, EPP, I32)
        dst_i = over(4 * EPP, EPP, I32)
        lane_i = over(8 * EPP, EPP, I32)
        blk_i = over(12 * EPP, EPP, I32)
        grp_i = over(16 * EPP, EPP, I32)
        comb = over(24 * EPP, 2 * EPP, F32).rearrange("p (r c) -> p r c", c=2 * ROW)
        code_a = over(32 * EPP, EPP, F32)
        x_rows = over(36 * EPP, SRC_BLOCKS * F, F32)
        x_rest = over(36 * EPP + 4 * SRC_BLOCKS * F, SRC_BLOCKS * F, F32)
        featT = over(0, NPAD, F32)
        sumT = over(4 * NPAD, NPAD, F32)
        ends = over(8 * NPAD, 2 * GE, I32).rearrange("p (a e) -> p a e", a=2)
        at = [0]

        def edge_buf(n, parts=P):
            w = A_raw[0:parts, 2 * at[0]:2 * (at[0] + n)].bitcast(F32)
            at[0] += n
            return w

        NB = 3
        acc = edge_buf(N + WIN, F + 1)
        attr, gath, attrT = ([edge_buf(EJ * F)] for _ in range(3))
        zs, ex, rl = (edge_buf(EJ * F) for _ in range(3))
        msg = [edge_buf(EJ * (F + 1)).rearrange("p (j f) -> p j f", j=EJ)]
        attr += [edge_buf(EJ * F) for _ in range(NB - 1)]
        gath += [edge_buf(EJ * F) for _ in range(NB - 1)]
        attrT += [edge_buf(EJ * F) for _ in range(NB - 1)]
        msg += [edge_buf(EJ * (F + 1)).rearrange("p (j f) -> p j f", j=EJ) for _ in range(NB - 1)]
        hot = [edge_buf(EJ * WIN).rearrange("p (j n) -> p j n", j=EJ) for _ in range(NB)]
        accS = edge_buf(2 * SBN, F + 1)
        dst_row = edge_buf(EG, 1).bitcast(I32)
        assert at[0] * 4 <= 4 * SRC_BLOCKS * SBN
        in_window = zs.bitcast(mybir.dt.uint8)[:, 0:NEG * EJ]
        f16 = over(36 * EPP + 8 * SRC_BLOCKS * F, TROWS // P, I32).bitcast(I16)[:, 0:TROWS // P]

        hw = 3 * SRC_BLOCKS * H // 2
        h1m = [ar1[0:CH, hw + i * NCH * H:hw + (i + 1) * NCH * H].rearrange("p (c f) -> p c f", f=H) for i in range(2)]
        g2S = aggS[:, 0, :]
        h2T = aggS[:, 1, :]
        x2T = agg3S[0:F, 0, :]
        hTs = xTs
        yv = sb("yv", [CH, NCH, F], F32)
        yd = sb("yd", [CH, NCH, F], F32)
        x2c = ar1[0:CH, hw + 2 * NCH * H:hw + 2 * NCH * H + NCH * F].rearrange("p (c f) -> p c f", f=F)
        pc = iota_i[0:CH, 0:NCH * F].bitcast(F32).rearrange("p (c f) -> p c f", f=F)
        st = sb("st", [CH, 4, NCH], F32)
        hr = iota_i[0:CH, :].bitcast(F32).rearrange("p (c f) -> p c f", f=H)
        zero_c = sb("zero_c", [CH, NCH], F32)
        src_cur = [sb(f"src_cur{i}", [P, EJ], I32) for i in range(NB)]
        ex4, rl4, yv4, zm4, msg4 = (b[0:CH, 0:2 * NCH * F] for b in (ex, rl, gath[0], gath[1], gath[2]))
        msgT4 = agg3S[0:F, :, :].rearrange("p a n -> p (a n)")
        y_all = x2all.rearrange("p m c f -> p (m c) f")
        sq_all = q2all.rearrange("p m c f -> p (m c) f")
        st4 = hot[0].rearrange("p j n -> p (j n)")[0:CH, 0:3 * NSB * NCH].rearrange("p (a m) -> p a m", a=3)
        cnt_ps = [bank(f"cnt_ps{i}", [P, 512]) for i in range(2)]
        agg_ps = bank("agg_ps", [P, 512])
        agg3_ps = bank("agg3_ps", [P, 512])
        u_ps = bank("u_ps", [P, 512])
        v_ps = bank("v_ps", [P, 512])
        t_ps = bank("t_ps", [P, 512])
        t2_ps = bank("t2_ps", [P, 512])

        pads_set = sem("pads_set")
        dst_in, src_in, x_in, w_in, w2_in = sem("dst_in"), sem("src_in"), sem("x_in"), sem("w_in"), sem("w2_in")
        iota_set = sem("iota_set")
        consts = sem("consts")
        firsts_made, firsts_out, firsts_in = sem("firsts_made"), sem("firsts_out"), sem("firsts_in")
        table_made, table_out = sem("table_made"), sem("table_out")
        x1_made = sem("x1_made")
        dve0 = sem("dve0")
        rows_ready, win_in, rel_ready, win_turned, win_moved = (sem(n) for n in (
            "rows_ready", "win_in", "rel_ready", "win_turned", "win_moved"))
        lane_made, lane_moved = sem("lane_made"), sem("lane_moved")
        parts_found, fine_in = sem("parts_found"), sem("fine_in")
        win_dve = sem("win_dve")
        x_ones, relu_made = sem("x_ones"), sem("relu_made")
        hot_ready = sem("hot_ready")
        groups_summed = sem("groups_summed")
        counts_moved = sem("counts_moved")
        agg_ready, agg_moved = sem("agg_ready"), sem("agg_moved")
        A_stored = [sem("A_stored0"), sem("A_stored1")]
        xm_in = [sem("xm_in0"), sem("xm_in1")]
        xT_ready, xT_moved, uv_ready, layer_dve, h_ready, h_split, h_stored = (sem(n) for n in (
            "xT_ready", "xT_moved", "uv_ready", "layer_dve", "h_ready", "h_split", "h_stored"))
        sp_at, pool_at, act_at, pe_at, dve_at = sem("sp_at"), sem("pool_at"), sem("act_at"), sem("pe_at"), sem("dve_at")
        pool_dep, idx_made, zm_made = sem("pool_dep"), sem("idx_made"), sem("zm_made")
        part_in, parts_in = [sem(f"part_in{i}") for i in range(3)], sem("parts_in")
        A_in = [sem("A_in0"), sem("A_in1")]
        hx_in = [sem("hx_in0"), sem("hx_in1")]
        (agg2_ready, agg2_moved, hT_turned, hT_moved, u2_ready, v2_ready, h2_ready, h2_turned, h2_moved, o_ready,
         var_ready, std_ready, x2_ready, x2_kept, x2_turned, x2_moved, pq_ready, p_ready, p_stored, dve2) = (
            sem(n) for n in ("agg2_ready", "agg2_moved", "hT_turned", "hT_moved", "u2_ready", "v2_ready", "h2_ready",
                             "h2_turned", "h2_moved", "o_ready", "var_ready", "std_ready", "x2_ready", "x2_kept",
                             "x2_turned", "x2_moved", "pq_ready", "p_ready", "p_stored", "dve2"))
        inv_made = sem("inv_made")
        chk_made, chk_sum, flags = sem("chk_made"), sem("chk_sum"), sem("flags")
        chkB_made, chkB_sum, flagB = sem("chkB_made"), sem("chkB_sum"), sem("flagB")
        (g_set, feat_in, ends_in, col_added, chunk_added, sums_done, gl_in) = (sem(n) for n in (
            "g_set", "feat_in", "ends_in", "col_added", "chunk_added", "sums_done", "gl_in"))
        (ge_zero, ge_in, ge_idx, ge_rows, ge_turned, ge_moved, ge_z, ge_zs, ge_selu, ge_msg, ge_msgT, ge_col, ge_added) = (
            sem(n) for n in ("ge_zero", "ge_in", "ge_idx", "ge_rows", "ge_turned", "ge_moved", "ge_z", "ge_zs",
                             "ge_selu", "ge_msg", "ge_msgT", "ge_col", "ge_added"))
        edges_in, base_in, base_made, bases_ready = sem("edges_in"), sem("base_in"), sem("base_made"), sem("bases_ready")
        drel_made, acc_zero, ones_set = sem("drel_made"), sem("acc_zero"), sem("ones_set")
        wt_turned, wt_moved, wts_ready, wts_made = sem("wt_turned"), sem("wt_moved"), sem("wts_ready"), sem("wts_made")
        attr_in = [sem(f"attr_in{i}") for i in range(3)]
        gath_in = [sem(f"gath_in{i}") for i in range(3)]
        (attr_turned, attr_moved, z_ready, z_made, selu_act, hot_made, msg_made, seg_ready, acc_added) = (sem(n) for n in (
            "attr_turned", "attr_moved", "z_ready", "z_made", "selu_act", "hot_made", "msg_made", "seg_ready",
            "acc_added"))
        centred4, squared4, y_kept = sem("centred4"), sem("squared4"), sem("y_kept")
        (accS_moved, m_ready, zq_made, selu4, msg4_made, msg4_turned, msg4_moved, y_ready, var4, std4, row_made,
         row_stored) = (sem(n) for n in (
            "accS_moved", "m_ready", "zq_made", "selu4", "msg4_made", "msg4_turned", "msg4_moved", "y_ready",
            "var4", "std4", "row_made", "row_stored"))

        block = ctx.enter_context(nc.Block())
        full = E // EPP
        tail = E - full * EPP
        whole = N // P

        def Asb(half):
            return A_sb[:, half, :].rearrange("p (b n) -> p b n", n=SBN)

        def by_node(t, m):
            return t[bass.ds(m * SBN, SBN), :].rearrange("(c q) f -> q c f", q=CH)

        LAST = (NSB - 1) * SBN
        LCH = (N - LAST) // CH
        LREST = N - LAST - LCH * CH

        HALF4 = NSB * NCH // 2
        HALVES4 = (slice(0, HALF4), slice(HALF4, NSB * NCH))

        def general_begins(eng):
            eng.wait_ge(p_stored, 16 * NSB)
            eng.wait_ge(x2_kept, NSB)
            eng.wait_ge(x2_moved, NSB)
            eng.wait_ge(pq_ready, NSB)
            eng.wait_ge(edges_in, 96)

        def general_ends(eng):
            eng.wait_ge(p_stored, 2 * 16 * NSB)
            eng.wait_ge(x2_kept, 2 * NSB)
            eng.wait_ge(x2_moved, 2 * NSB)
            eng.wait_ge(pq_ready, 2 * NSB)

        def edges_end(eng):
            eng.wait_ge(acc_added, NEG)
            eng.wait_ge(seg_ready, NEG)
            eng.wait_ge(selu_act, 2 * NEG)

        @block.sync
        def _(sp):
            sp.wait_ge(pads_set, 1)
            sp.dma_start(dst_i[0:full, :], dst[0:full * EPP].rearrange("(p j) -> p j", j=EPP)).then_inc(dst_in, 16)
            sp.dma_start(dst_i[full:full + 1, 0:tail], dst[full * EPP:E].rearrange("(p j) -> p j", p=1)).then_inc(dst_in, 16)
            sp.wait_ge(pads_set, 2)
            sp.dma_start(src_i[0:full, :], src[0:full * EPP].rearrange("(p j) -> p j", j=EPP)).then_inc(src_in, 16)
            sp.dma_start(src_i[full:full + 1, 0:tail], src[full * EPP:E].rearrange("(p j) -> p j", p=1)).then_inc(src_in, 16)
            xr3 = x_rows.rearrange("p (b f) -> p b f", f=F)
            sp.wait_ge(pads_set, 3)
            sp.dma_start(xr3[:, 0:whole, :], x[0:whole * P, :].rearrange("(b p) f -> p b f", p=P)).then_inc(x_in, 16)
            sp.dma_start(xr3[0:N - whole * P, whole, :], x[whole * P:N, :]).then_inc(x_in, 16)
            for half in range(2):
                sp.dma_start(Wl1s[half * F:(half + 1) * F, :], Wl1).then_inc(w_in, 16)
            sp.dma_start(Wr1s[0:F, :], Wr1).then_inc(w_in, 16)
            sp.dma_start(Wr1s[F:F + 1, :], bl1.rearrange("(a f) -> a f", a=1)).then_inc(w_in, 16)
            sp.wait_ge(firsts_made, 1)
            with nc.allow_non_contiguous_dma(reason="128 numbers, one of each partition"):
                sp.dma_start(coarse_d.rearrange("(p a) -> p a", a=1), f16[:, 0:1]).then_inc(firsts_out, 16)
            sp.dma_start(firsts_d, f16).then_inc(firsts_out, 16)
            sp.wait_ge(firsts_out, 32)
            sp.dma_start(coarse, coarse_d.partition_broadcast(P)).then_inc(firsts_in, 16)
            sp.wait_ge(table_made, 1)
            sp.wait_ge(lane_moved, 1)
            sp.dma_start(table.rearrange("(p r) c -> p (r c)", p=P), comb.rearrange("p r c -> p (r c)")).then_inc(table_out, 16)
            for to, frm in ((Wl2s, Wl2), (Wr2s, Wr2), (Wouts, Wout), (bl2s, bl2.partition_broadcast(CH)),
                            (bouts, bout.partition_broadcast(CH)), (Wxx[:, 0:F], W1a[0:F, :]), (Wxx[:, F:2 * F], W2a[0:F, :]),
                            (W1bs, W1b), (W2am, W2a[F:2 * F, :]), (W2au, W2a[2 * F:3 * F, :]), (W2bs, W2b),
                            (b1as, b1a.partition_broadcast(CH)), (b2as, b2a.partition_broadcast(CH)),
                            (b2bs, b2b.partition_broadcast(CH)), (b1bcol, b1b.rearrange("(f a) -> f a", a=1)),
                            (u0, u[0:1, :].rearrange("a f -> f a"))):
                sp.dma_start(to if isinstance(to, bass.AP) else to[:, :], frm).then_inc(w2_in, 16)
            sp.wait_ge(pads_set, 4)
            for half in range(2):
                sp.dma_start(Wedge[half * F:(half + 1) * F, half * F:(half + 1) * F], W1a[F:2 * F, :]).then_inc(w2_in, 16)

            def store_h(m, half):
                sp.wait_ge(h_split, m + 1)
                sp.dma_start(by_node(h1_d, m), hs[:, :, :]).then_inc(h_stored, 16)
                for part in range(3):
                    sp.dma_start(by_node(hp_d[part], m), hpart[:, part, :, :]).then_inc(h_stored, 16)

            def superblock(s, half, layer):
                if layer:
                    if not isinstance(s, int):
                        sp.wait_ge(xT_ready, s - 3)
                    sp.dma_start(xm[:, half, :, :], by_node(x, s - 2)).then_inc(xm_in[half], 16)
                sp.wait_ge(counts_moved, (s + 1) * SB_GROUPS + 2)
                sp.dma_start(A_d[bass.ds(s, 1), :, :].rearrange("a p n -> (a p) n"), A_sb[:, half, :]).then_inc(A_stored[half], 16)
                if layer:
                    store_h(s - 2, half)

            superblock(0, 0, False)
            superblock(1, 1, False)
            superblock(2, 0, True)
            superblock(3, 1, True)
            with sp.Fori(2, PAIRS) as pair:
                superblock(pair * 2, 0, True)
                superblock(pair * 2 + 1, 1, True)
            sp.wait_ge(xT_ready, NSB - 3)
            sp.dma_start(xm[:, 0, :, :], by_node(x, NSB - 2)).then_inc(xm_in[0], 16)
            sp.wait_ge(xT_ready, NSB - 2)

            def last_rows(rows, done):
                sp.dma_start(rows[:, 0:LCH, :], x[LAST:LAST + LCH * CH, :].rearrange("(c q) f -> q c f", q=CH)).then_inc(done, 16)
                sp.dma_start(rows[0:LREST, LCH, :], x[LAST + LCH * CH:N, :]).then_inc(done, 16)
            last_rows(xm[:, 1], xm_in[1])

            def load_parts(parts, blocks, done):
                for part in parts:
                    sp.dma_start(Hsb[:, part, blocks, :], hp_d[part, blocks.start * P:blocks.stop * P, :].rearrange("(b p) f -> p b f", p=P)).then_inc(done, 16)
            early, late = slice(0, EARLY), slice(EARLY, SRC_BLOCKS)
            sp.wait_ge(hot_ready, NSB * SB_GROUPS)
            sp.wait_ge(h_stored, 64 * (NSB - 2))
            load_parts((2,), early, part_in[2])
            sp.wait_ge(agg_ready, NSB)
            load_parts((0,), early, part_in[0])
            load_parts((1,), early, part_in[1])
            store_h(NSB - 2, 0)
            store_h(NSB - 1, 1)
            sp.wait_ge(h_stored, 64 * NSB)
            load_parts((0, 1, 2), late, parts_in)

            def load_hx(m, half):
                at = NSB - 2 if isinstance(m, int) and m == 0 else m - 2
                sp.dma_start(h1m[half][:, :, :], by_node(h1_d, at)).then_inc(hx_in[half], 16)
                sp.dma_start(xm[:, half, :, :], by_node(x, at)).then_inc(hx_in[half], 16)

            sp.wait_ge(xT_ready, NSB - 1)
            load_hx(0, 0)
            sp.wait_ge(A_stored[0], 16 * PAIRS)
            sp.wait_ge(A_stored[1], 16 * PAIRS)

            def superblock2(s, half, at_before=None):
                sp.wait_ge(agg2_ready, s)
                if not (isinstance(s, int) and s == NSB - 1):
                    sp.dma_start(A_sb[:, 1 - half, :], A_d[bass.ds(s - 1, 1), :, :].rearrange("a p n -> (a p) n")).then_inc(A_in[1 - half], 16)
                sp.wait_ge(x2_ready, s + 1)
                if isinstance(s, int) and s == 1:
                    sp.dma_start(h1m[1][:, :, :], by_node(h1_d, NSB - 1)).then_inc(hx_in[1], 16)
                    last_rows(xm[:, 1], hx_in[1])
                else:
                    load_hx(s, half)
                sp.wait_ge(p_ready, s)
                sp.dma_start(by_node(p_d, s - 3 if at_before is None else at_before), pc[:, :, :]).then_inc(p_stored, 16)

            superblock2(1, 1, NSB - 2)
            superblock2(2, 0, NSB - 1)
            sp.wait_ge(firsts_in, 16)
            sp.wait_ge(rows_ready, PAIRS + 1)
            sp.wait_ge(win_turned, PAIRS + 1)
            sp.wait_ge(pads_set, 6)
            gE = NEG - 1
            for to, frm in ((src_e, src), (dst_e, dst)):
                sp.dma_start(to[:, 0:gE, :], frm[0:gE * EG].rearrange("(g p j) -> p g j", p=P, j=EJ)).then_inc(edges_in, 16)
                sp.dma_start(to[0:ETAIL // EJ, gE, :], frm[gE * EG:gE * EG + ETAIL // EJ * EJ].rearrange("(p j) -> p j", j=EJ)).then_inc(edges_in, 16)
                sp.dma_start(to[ETAIL // EJ:ETAIL // EJ + 1, gE, 0:ETAIL % EJ], frm[gE * EG + ETAIL // EJ * EJ:E].rearrange("(p j) -> p j", p=1)).then_inc(edges_in, 16)
            with nc.allow_non_contiguous_dma(reason="one destination of every 1024"):
                sp.dma_start(base_i[0:1, 0:gE], dst[0:gE * EG].rearrange("(a g q) -> a g q", a=1, q=EG)[:, :, 0]).then_inc(base_in, 16)
            sp.dma_start(base_i[0:1, gE:NEG], dst[gE * EG:gE * EG + 1].rearrange("(a g) -> a g", a=1)).then_inc(base_in, 16)

            with sp.Fori(1, PAIRS - 1) as j:
                superblock2(j * 2 + 1, 1)
                superblock2(j * 2 + 2, 0)
            superblock2(NSB - 1, 1)
            sp.wait_ge(p_ready, NSB)
            sp.dma_start(by_node(p_d, NSB - 3), pc[:, :, :]).then_inc(p_stored, 16)

            def general_sums(table_d, width, i):
                sp.wait_ge(g_set, 2 * i + 2)
                with nc.allow_non_contiguous_dma(reason="turns the rows of nodes"):
                    with sp.Fori(0, N // GN) as c:
                        sp.dma_start(featT[0:width, bass.ds(c * GN, GN)], table_d[bass.ds(c * GN, GN), :].rearrange("n f -> f n")).then_inc(feat_in, 16)
                        sp.wait_ge(feat_in, c * 16 + 16 * (i * (N // GN) + 1))
                        sp.sem_inc(sp_at, 1)
                with sp.Fori(0, E // GE) as c:
                    sp.wait_ge(chunk_added, c + (i * (E // GE) + 1))
                    sp.sem_inc(sp_at, 1)
                    for a, frm in enumerate((src, dst)):
                        sp.dma_start(ends[0:1, a, :], frm[bass.ds(c * GE, GE)].rearrange("(a e) -> a e", a=1)).then_inc(ends_in, 16)

            def general_layer1(m):
                if isinstance(m, int):
                    last_rows(xm[:, 0], gl_in)
                else:
                    sp.dma_start(xm[:, 0], by_node(x, m)).then_inc(gl_in, 32)
                sp.wait_ge(h_ready, m + (NSB + 1))
                sp.dma_start(by_node(h1_d, m), hs[:, :, :]).then_inc(h_stored, 64)

            def general_layer2(m):
                sp.dma_start(h1m[0], by_node(h1_d, m)).then_inc(gl_in, 16)
                if isinstance(m, int):
                    last_rows(xm[:, 0], gl_in)
                else:
                    sp.dma_start(xm[:, 0], by_node(x, m)).then_inc(gl_in, 32)
                sp.wait_ge(p_ready, m + (NSB + 1))
                sp.dma_start(by_node(p_d, m), pc).then_inc(p_stored, 16)
                sp.wait_ge(p_stored, m * 16 + 16 * (NSB + 1))
                sp.sem_inc(sp_at, 1)

            sp.wait_ge(flags, 1)
            left = sp.value_load(flag_i[0:1, 0:1], min_val=0, max_val=1)
            with sp.If_ne(sp.to_reg(left), 0):
                general_begins(sp)
                general_sums(x, F, 0)
                with sp.Fori(0, NSB - 1) as m:
                    general_layer1(m)
                general_layer1(NSB - 1)
                sp.wait_ge(h_stored, 2 * 64 * NSB)
                general_sums(h1_d, H, 1)
                with sp.Fori(0, NSB - 1) as m:
                    general_layer2(m)
                general_layer2(NSB - 1)
                general_ends(sp)

            sp.wait_ge(agg2_ready, NSB)

            def load_attr(g, k):
                sp.dma_start(attr[k], edge_attr[bass.ds(g * EG, EG), :].rearrange("(p j) f -> p (j f)", p=P)).then_inc(attr_in[k], 16)
            for k in range(NB):
                load_attr(k, k)
            with sp.Fori(1, gE // NB) as r:
                for k in range(NB):
                    sp.wait_ge(attr_turned, r * NB + (k - NB + 1))
                    load_attr(r * NB + k, k)
            sp.wait_ge(attr_turned, gE - NB + 1)
            te = gE * EG
            sp.dma_start(attr[0][0:ETAIL // EJ, :], edge_attr[te:te + ETAIL // EJ * EJ, :].rearrange("(p j) f -> p (j f)", j=EJ)).then_inc(attr_in[0], 16)
            sp.dma_start(attr[0][ETAIL // EJ:ETAIL // EJ + 1, 0:ETAIL % EJ * F], edge_attr[te + ETAIL // EJ * EJ:E, :].rearrange("(p j) f -> p (j f)", p=1)).then_inc(attr_in[0], 16)

            sp.wait_ge(flagB, 1)
            left = sp.value_load(flag_i[0:1, 1:2], min_val=0, max_val=1)
            with sp.If_ne(sp.to_reg(left), 0):
                edges_end(sp)
                with sp.Fori(0, gE) as g:
                    sp.wait_ge(ge_added, g + 1)
                    sp.sem_inc(sp_at, 1)
                    sp.dma_start(attr[0], edge_attr[bass.ds(g * EG, EG), :].rearrange("(p j) f -> p (j f)", p=P)).then_inc(ge_in, 16)
                    sp.dma_start(dst_row, dst[bass.ds(g * EG, EG)].rearrange("(a e) -> a e", a=1)).then_inc(ge_in, 16)
                sp.wait_ge(ge_zero, 2)
                sp.dma_start(attr[0][0:ETAIL // EJ, :], edge_attr[te:te + ETAIL // EJ * EJ, :].rearrange("(p j) f -> p (j f)", j=EJ)).then_inc(ge_in, 16)
                sp.dma_start(attr[0][ETAIL // EJ:ETAIL // EJ + 1, 0:ETAIL % EJ * F], edge_attr[te + ETAIL // EJ * EJ:E, :].rearrange("(p j) f -> p (j f)", p=1)).then_inc(ge_in, 16)
                sp.dma_start(dst_row[:, 0:ETAIL], dst[te:E].rearrange("(a e) -> a e", a=1)).then_inc(ge_in, 16)
                sp.wait_ge(ge_added, NEG + 1)

            sp.wait_ge(row_made, 1)
            sp.dma_start(out[0:HALF4 * CH, :].rearrange("(a q) f -> q a f", q=CH), y_all[:, 0:HALF4, :]).then_inc(row_stored, 16)
            sp.wait_ge(row_made, 2)
            sp.dma_start(out[HALF4 * CH:N // CH * CH, :].rearrange("(a q) f -> q a f", q=CH), y_all[:, HALF4:N // CH, :]).then_inc(row_stored, 16)
            sp.dma_start(out[N // CH * CH:N, :], y_all[0:N % CH, N // CH, :]).then_inc(row_stored, 16)
            sp.wait_ge(row_stored, 48)

        @block.gpsimd
        def _(pool):
            pool.memset(dst_i, NO_NODE).then_inc(pads_set, 1)
            pool.memset(src_i, 0).then_inc(pads_set, 1)
            pool.memset(x_rows, 0.0).then_inc(pads_set, 1)
            pool.memset(Wedge[:, :], 0.0).then_inc(pads_set, 1)
            pool.iota(iota_i[:, :], [[1, 512]], 0, 0).then_inc(iota_set, 1)
            pool.memset(ident[:, :], 0.0).then_inc(iota_set, 1)
            pool.memset(zrow[:, :], 0.0).then_inc(iota_set, 1)
            pool.memset(X3[:, :, F:F + 1], 1.0).then_inc(iota_set, 1)
            pool.memset(cnt_sel[:, :], 0.0).then_inc(iota_set, 1)
            pool.wait_ge(iota_set, 5)
            pool.affine_select(out=ident[:, :], in_=ident[:, :], compare_op=ALU.not_equal, fill=1.0,
                               base=0, pattern=[[-1, P]], channel_multiplier=1).then_inc(iota_set, 1)
            pool.affine_select(out=cnt_sel[:, :], in_=cnt_sel[:, :], compare_op=ALU.not_equal, fill=1.0,
                               base=-F, pattern=[[0, 1]], channel_multiplier=1).then_inc(iota_set, 1)
            pool.iota(thr[:, :], [[GROUP * P, 8]], 0, GROUP, allow_small_or_imprecise_dtypes=True).then_inc(iota_set, 1)
            pool.iota(code0[:, :], [[P, 8]], 0, 1, allow_small_or_imprecise_dtypes=True).then_inc(iota_set, 1)
            pool.memset(shift_b[:, :], -SCALE * ALPHA).then_inc(ones_set, 1)
            pool.memset(ln_alpha[:, :], LN_ALPHA).then_inc(ones_set, 1)
            pool.memset(eps_t[:, :], EPS).then_inc(ones_set, 1)
            pool.memset(ones_r[:, :], 1.0).then_inc(ones_set, 1)
            pool.memset(ones_c[:, :], 1.0).then_inc(ones_set, 1)
            pool.wait_ge(firsts_out, 32)
            pool.wait_ge(parts_found, 1)
            for n in range(8):
                pool.indirect_dma_start(
                    out=fine[:, n, :], out_offset=None, in_=firsts_d,
                    in_offset=bass.IndirectOffsetOnAxis(ap=part_of[:, n:n + 1], axis=0)).then_inc(fine_in, 16)
            pool.wait_ge(table_out, 16)

            def gather_windows(n):
                pool.wait_ge(rows_ready, n + 1)
                pool.sem_inc(pool_at, 1)
                for j in range(WROWS):
                    pool.indirect_dma_start(
                        out=win[:, j, :], out_offset=None, in_=table,
                        in_offset=bass.IndirectOffsetOnAxis(ap=rows12[:, 0, j:j + 1], axis=0)).then_inc(win_in, 16)

            def split_h(m):
                pool.wait_ge(h_ready, m + 1)
                pool.wait_ge(h_stored, m * 64)
                pool.sem_inc(pool_at, 1)
                seq = [lambda: pool.tensor_scalar(hs[:, :, :], hs[:, :, :], 0.0, None, ALU.max),
                       lambda: pool.tensor_copy(hpart[:, 0], hs[:, :, :]),
                       lambda: pool.tensor_tensor(hr[:, :, :], hs[:, :, :], hpart[:, 0], ALU.subtract),
                       lambda: pool.tensor_copy(hpart[:, 1], hr[:, :, :]),
                       lambda: pool.tensor_tensor(hr[:, :, :], hr[:, :, :], hpart[:, 1], ALU.subtract),
                       lambda: pool.tensor_copy(hpart[:, 2], hr[:, :, :])]
                for i, op in enumerate(seq):
                    if i < 5:
                        op().then_inc(pool_dep, 1)
                        pool.wait_ge(pool_dep, m * 5 + (i + 1))
                        pool.sem_inc(pool_at, 1)
                    else:
                        op().then_inc(h_split, 1)

            gather_windows(0)
            pool.wait_ge(win_turned, 1)
            gather_windows(1)
            pool.wait_ge(win_turned, 2)
            gather_windows(2)
            split_h(0)
            split_h(1)
            with pool.Fori(2, PAIRS) as pair:
                pool.wait_ge(win_turned, pair + 1)
                pool.sem_inc(pool_at, 1)
                gather_windows(pair + 1)
                split_h(pair * 2 - 2)
                split_h(pair * 2 - 1)
            pool.wait_ge(rows_ready, PAIRS + 1)
            pool.wait_ge(win_turned, PAIRS + 1)
            pool.memset(src_e[:, NEG - 1, :], 0).then_inc(pads_set, 1)
            pool.memset(dst_e[:, NEG - 1, :], NO_NODE).then_inc(pads_set, 1)
            split_h(NSB - 2)
            split_h(NSB - 1)

            pool.wait_ge(hot_ready, NSB * SB_GROUPS)
            pool.wait_ge(groups_summed, NSB * SB_GROUPS + SLOTS)
            pool.wait_ge(win_turned, PAIRS + 1)
            for m in range(2):
                pool.wait_ge(x2_ready, m + 3)
                pool.tensor_copy(x2all[:, NSB - 2 + m, :, :], x2c[:, :, :]).then_inc(x2_kept, 1)
            with pool.Fori(2, NSB) as m:
                pool.wait_ge(x2_ready, m + 3)
                pool.sem_inc(pool_at, 1)
                pool.tensor_copy(x2all[:, bass.ds(m - 2, 1), :, :].rearrange("p a c f -> p (a c) f"), x2c[:, :, :]).then_inc(x2_kept, 1)

            pool.wait_ge(flags, 1)
            left = pool.value_load(flag_i[0:1, 0:1], min_val=0, max_val=1)
            with pool.If_ne(pool.to_reg(left), 0):
                general_begins(pool)
                pool.memset(featT, 1.0).then_inc(g_set, 1)
                pool.memset(sumT, 0.0).then_inc(g_set, 1)
                pool.wait_ge(h_stored, 2 * 64 * NSB)
                pool.memset(featT, 0.0).then_inc(g_set, 1)
                pool.memset(sumT, 0.0).then_inc(g_set, 1)
                with pool.Fori(NSB, 2 * NSB) as m:
                    pool.wait_ge(x2_ready, m + 3)
                    pool.sem_inc(pool_at, 1)
                    pool.tensor_copy(x2all[:, bass.ds(m - NSB, 1), :, :].rearrange("p a c f -> p (a c) f"), x2c[:, :, :]).then_inc(x2_kept, 1)
                general_ends(pool)

            pool.wait_ge(agg2_ready, NSB)
            pool.memset(acc[:, :], 0.0).then_inc(acc_zero, 1)
            for k in range(NB):
                pool.memset(msg[k][:, :, F:F + 1], 1.0).then_inc(acc_zero, 1)
            pool.wait_ge(edges_in, 96)
            pool.wait_ge(p_stored, 16 * NSB)

            def gather(g, k):
                for j in range(EJ):
                    pool.indirect_dma_start(
                        out=gath[k][:, j * F:(j + 1) * F], out_offset=None, in_=p_d,
                        in_offset=bass.IndirectOffsetOnAxis(ap=src_cur[k][:, j:j + 1], axis=0)).then_inc(gath_in[k], 16)

            for k in range(NB):
                pool.wait_ge(idx_made, k + 1)
                gather(k, k)
            with pool.Fori(1, (NEG - 1) // NB) as r:
                for k in range(NB):
                    pool.wait_ge(z_made, r * NB + (k - NB + 1))
                    pool.wait_ge(idx_made, r * NB + (k + 1))
                    pool.sem_inc(pool_at, 1)
                    gather(r * NB + k, k)
            pool.wait_ge(z_made, NEG - NB)
            pool.wait_ge(idx_made, NEG)
            gather(NEG - 1, 0)

            pool.wait_ge(flagB, 1)
            left = pool.value_load(flag_i[0:1, 1:2], min_val=0, max_val=1)
            with pool.If_ne(pool.to_reg(left), 0):
                edges_end(pool)
                pool.memset(acc[:, :], 0.0).then_inc(ge_zero, 1)

                def general_gather(g):
                    pool.wait_ge(ge_idx, g + 1)
                    pool.sem_inc(pool_at, 1)
                    for j in range(EJ):
                        pool.indirect_dma_start(
                            out=gath[0][:, j * F:(j + 1) * F], out_offset=None, in_=p_d,
                            in_offset=bass.IndirectOffsetOnAxis(ap=src_cur[0][:, j:j + 1], axis=0)).then_inc(ge_rows, 16)
                with pool.Fori(0, NEG - 1) as g:
                    general_gather(g)
                pool.wait_ge(ge_added, NEG)
                pool.memset(dst_row, N + WIN - 1).then_inc(ge_zero, 1)
                general_gather(NEG - 1)
                pool.wait_ge(ge_added, NEG + 1)

        @block.scalar
        def _(act):
            act.wait_ge(iota_set, 9)
            act.activation(iota_code[:, :, :], iota_i[:, 0:CODES].unsqueeze(2).to_broadcast([P, CODES, CHUNKS]), ACT.Copy, bias=1.0).then_inc(consts, 1)
            act.activation(iota_w[:, :], iota_i[:, 0:WIN], ACT.Copy).then_inc(consts, 1)
            act.wait_ge(lane_made, 1)
            act.activation(comb[:, :, 0:ROW], lane_i.rearrange("p (r c) -> p r c", c=ROW), ACT.Copy).then_inc(lane_moved, 1)
            act.wait_ge(x_in, 32)
            act.activation(X12[:, :, 0:F], x_rows.rearrange("p (b f) -> p b f", f=F), ACT.Copy).then_inc(x1_made, 1)

            def move_windows(n):
                act.wait_ge(win_turned, n + 1)
                act.sem_inc(act_at, 1)
                cols = bass.ds(n * P, P)
                act.activation(laneT[:, cols, :], t_ps[:, 0:CHUNKS * P].rearrange("p (k g) -> p g k", g=P), ACT.Copy).then_inc(win_moved, 1)
                act.activation(codeT[:, cols, :], t2_ps[:, 0:CHUNKS * P].rearrange("p (k g) -> p g k", g=P), ACT.Relu).then_inc(win_moved, 1)

            def move_xT(m):
                act.wait_ge(xT_ready, m + 1)
                act.activation(xTs[0:F, :], t_ps[0:F, 0:SBN], ACT.Copy).then_inc(xT_moved, 1)

            def move_agg(s, half):
                act.wait_ge(agg_ready, s + 1)
                act.activation(aggS[:, half, :], agg_ps[:, 0:SBN], ACT.Copy).then_inc(agg_moved, 1)
                act.activation(agg3S[:, half, :], agg3_ps[0:F + 1, 0:SBN], ACT.Copy).then_inc(agg_moved, 1)

            def superblock(s, half, mult=True, layer=True):
                dest = Asb(half)
                with act.Fori(0, BODIES) as b:
                    for k in range(BG):
                        act.wait_ge(groups_summed, (s * BODIES + b) * BG + (k + 1 + SLOTS))
                        act.sem_inc(act_at, 1)
                        act.activation(dest[:, :, bass.ds((b * BG + k) * GROUP, GROUP)],
                                       cnt_ps[k % 2][:, 0:CODES].rearrange("p (b j) -> p b j", j=GROUP),
                                       ACT.Copy).then_inc(counts_moved, 1)
                if mult:
                    move_agg(s - 1, 1 - half)
                if layer:
                    move_xT(s - 2)

            move_windows(0)
            superblock(0, 0, False, False)
            move_windows(1)
            superblock(1, 1, True, False)

            def pair_of(pair):
                act.wait_ge(A_stored[0], pair * 16)
                act.sem_inc(act_at, 1)
                superblock(pair * 2, 0)
                move_windows(pair + 1)
                act.wait_ge(A_stored[1], pair * 16)
                act.sem_inc(act_at, 1)
                superblock(pair * 2 + 1, 1)
            with act.Fori(1, PAIRS) as pair:
                pair_of(pair)
            move_xT(NSB - 2)
            move_agg(NSB - 1, 1)
            move_xT(NSB - 1)

            act.wait_ge(wt_turned, 1)
            act.activation(WbT[:, 0:F], t_ps[0:F, 0:F], ACT.Copy, scale=SCALE).then_inc(wt_moved, 1)

            def layer2(m, s=None):
                act.wait_ge(hT_turned, m + 1)
                act.activation(hTs[:, :], t_ps[:, 0:SBN], ACT.Copy).then_inc(hT_moved, 1)
                act.wait_ge(h2_turned, m + 1)
                act.activation(h2T, t2_ps[:, 0:SBN], ACT.Copy).then_inc(h2_moved, 1)
                act.wait_ge(var_ready, m + 1)
                act.activation(st[:, 3, :], st[:, 2, :], ACT.Sqrt, bias=eps_t[0:CH, 0:1], scale=1.0 / F).then_inc(std_ready, 1)
                act.wait_ge(x2_turned, m + 1)
                act.activation(x2T, cnt_ps[1][0:F, 0:SBN], ACT.Copy).then_inc(x2_moved, 1)
                if s is not None:
                    move_agg2(s)

            def move_agg2(s):
                act.wait_ge(agg2_ready, s + 1)
                act.activation(g2S, agg_ps[:, 0:SBN], ACT.Copy).then_inc(agg2_moved, 1)

            move_agg2(0)
            with act.Fori(1, NSB) as s:
                layer2(s - 1, s)
            layer2(NSB - 1)

            act.wait_ge(flags, 1)
            left = act.value_load(flag_i[0:1, 0:1], min_val=0, max_val=1)
            with act.If_ne(act.to_reg(left), 0):
                general_begins(act)
                act.wait_ge(sums_done, 1)
                with act.Fori(0, NSB) as m:
                    act.wait_ge(h_ready, m + NSB)
                    act.sem_inc(act_at, 1)
                    act.activation(agg3S[:, 0, :], sumT[0:F + 1, bass.ds(m * SBN, SBN)], ACT.Copy).then_inc(agg_moved, 2)
                    move_xT(m + NSB)
                act.wait_ge(sums_done, 2)
                with act.Fori(0, NSB) as m:
                    act.wait_ge(u2_ready, m + NSB)
                    act.sem_inc(act_at, 1)
                    act.activation(g2S, sumT[:, bass.ds(m * SBN, SBN)], ACT.Copy).then_inc(agg2_moved, 1)
                    layer2(m + NSB)
                general_ends(act)

            def indices(g, k):
                act.activation(src_cur[k][:, :], src_e[:, bass.ds(g, 1), :].rearrange("p a j -> p (a j)"), ACT.Copy).then_inc(idx_made, 1)

            def edge_group(g, k, ahead=True):
                act.wait_ge(attr_turned, g + 1)
                act.activation(attrT[k], t_ps[:, 0:EJ * F], ACT.Copy).then_inc(attr_moved, 1)
                act.wait_ge(z_made, g + 1)
                act.activation(ex, zs, ACT.Exp, bias=ln_alpha[:, 0:1]).then_inc(selu_act, 1)
                act.activation(rl, zs, ACT.Relu).then_inc(selu_act, 1)
                if ahead:
                    indices(g + NB, k)

            act.wait_ge(edges_in, 96)
            for k in range(NB):
                indices(k, k)
            with act.Fori(0, (NEG - 1) // NB - 1) as r:
                for k in range(NB):
                    edge_group(r * NB + k, k)
            edge_group(NEG - 1 - NB, 0)
            edge_group(NEG - NB, 1, False)
            edge_group(NEG + 1 - NB, 2, False)
            edge_group(NEG - 1, 0, False)

            act.wait_ge(flagB, 1)
            left = act.value_load(flag_i[0:1, 1:2], min_val=0, max_val=1)
            with act.If_ne(act.to_reg(left), 0):
                edges_end(act)
                with act.Fori(0, NEG) as g:
                    act.wait_ge(ge_added, g + 1)
                    act.sem_inc(act_at, 1)
                    act.activation(src_cur[0][:, :], src_e[:, bass.ds(g, 1), :].rearrange("p a j -> p (a j)"), ACT.Copy).then_inc(ge_idx, 1)
                    act.wait_ge(ge_turned, g + 1)
                    act.activation(attrT[0], t_ps[:, 0:EJ * F], ACT.Copy).then_inc(ge_moved, 1)
                    act.wait_ge(ge_zs, g + 1)
                    act.activation(ex, zs, ACT.Exp, bias=ln_alpha[:, 0:1]).then_inc(ge_selu, 1)
                    act.activation(rl, zs, ACT.Relu).then_inc(ge_selu, 1)
                act.wait_ge(ge_added, NEG + 1)

            act.wait_ge(acc_added, NEG)

            def copy_sums(j):
                if not isinstance(j, int) or j > 0:
                    act.wait_ge(m_ready, j)
                    act.sem_inc(act_at, 1)
                act.activation(accS, acc[:, bass.ds(j * (2 * SBN), 2 * SBN)], ACT.Copy).then_inc(accS_moved, 1)

            def first_half(j):
                act.wait_ge(zq_made, j + 1)
                if not isinstance(j, int) or j > 0:
                    act.wait_ge(msg4_made, j)
                act.activation(ex4, yv4, ACT.Exp, bias=ln_alpha[0:CH, 0:1]).then_inc(selu4, 1)
                act.activation(rl4, yv4, ACT.Relu).then_inc(selu4, 1)

            def move_msg(j):
                act.wait_ge(msg4_turned, j + 1)
                act.wait_ge(y_ready, j + 1)
                act.activation(msgT4[:, 0:SBN], t_ps[0:F, 0:SBN], ACT.Copy).then_inc(msg4_moved, 1)
                act.activation(msgT4[:, SBN:2 * SBN], t2_ps[0:F, 0:SBN], ACT.Copy).then_inc(msg4_moved, 1)

            copy_sums(0)
            first_half(0)
            copy_sums(1)
            with act.Fori(0, PAIRS - 2) as j:
                copy_sums(j + 2)
                first_half(j + 1)
                move_msg(j)
            first_half(PAIRS - 1)
            move_msg(PAIRS - 2)
            move_msg(PAIRS - 1)
            for i, a in enumerate(HALVES4):
                act.wait_ge(centred4, i + 1)
                act.activation(sq_all[:, a, :], y_all[:, a, :], ACT.Square).then_inc(squared4, 1)
            for i, a in enumerate(HALVES4):
                act.wait_ge(var4, i + 1)
                act.activation(st4[:, 2, a], st4[:, 1, a], ACT.Sqrt, bias=eps_t[0:CH, 0:1], scale=1.0 / F).then_inc(std4, 1)

        @block.tensor
        def _(pe):
            pe.sem_inc(groups_summed, SLOTS)
            pe.sem_inc(counts_moved, 2)
            pe.wait_ge(iota_set, 9)

            def turn_windows(n):
                pe.wait_ge(rel_ready, (n + 1) * 2)
                if not isinstance(n, int) or n > 0:
                    pe.wait_ge(win_moved, n * 2)
                for k in range(CHUNKS):
                    pe.transpose(t_ps[:, k * P:(k + 1) * P], rel[:, 0, k * P:(k + 1) * P], ident[:, :])
                for k in range(CHUNKS):
                    ins = pe.transpose(t2_ps[:, k * P:(k + 1) * P], rel[:, 1, k * P:(k + 1) * P], ident[:, :])
                ins.then_inc(win_turned, 1)

            def open_agg(s):
                if not isinstance(s, int) or s > 0:
                    pe.wait_ge(agg_moved, s * 2)
                pe.matmul(agg_ps[:, 0:SBN], zrow[:, 0:P], zrow[:, 0:SBN], start=True, stop=False, skip_group_check=True)
                pe.matmul(agg3_ps[:, 0:SBN], zrow[:, 0:P], zrow[:, 0:SBN], start=True, stop=False, skip_group_check=True)

            def layer(m, half, arrived=None):
                if arrived is not None:
                    pe.wait_ge(gl_in, arrived)
                elif isinstance(m, int):
                    pe.wait_ge(xm_in[half], 16 * (m // 2 + 1) + (16 if m == NSB - 1 else 0))
                else:
                    pe.wait_ge(xm_in[half], (m - half) * 8 + 16)
                if not isinstance(m, int) or m > 0:
                    pe.wait_ge(h_ready, m)
                pe.sem_inc(pe_at, 1)
                for c in range(NCH):
                    ins = pe.transpose(t_ps[0:F, c * CH:(c + 1) * CH], xm[:, half, c, :], ident[0:CH, 0:CH])
                ins.then_inc(xT_ready, 1)
                pe.wait_ge(agg_moved, m * 2 + 2)
                for c in range(NCH):
                    cols = slice(c * CH, (c + 1) * CH)
                    if arrived is None:
                        pe.matmul(u_ps[0:CH, c * H:(c + 1) * H], aggS[:, half, cols], Wl1s[:, :], start=True, stop=False, skip_group_check=True)
                    pe.matmul(u_ps[0:CH, c * H:(c + 1) * H], agg3S[0:F, half, cols], Wl1s[0:F, :], start=arrived is not None, stop=True, skip_group_check=True)
                pe.wait_ge(xT_moved, m + 1)
                for c in range(NCH):
                    pe.matmul(t_ps[0:CH, SBN + c:SBN + c + 1], agg3S[:, half, c * CH:(c + 1) * CH], cnt_sel[:, :], start=True, stop=True)
                for c in range(NCH):
                    ins = pe.matmul(v_ps[0:CH, c * H:(c + 1) * H], xTs[0:F + 1, c * CH:(c + 1) * CH], Wr1s[:, :], start=True, stop=True)
                ins.then_inc(uv_ready, 1)

            def superblock(s, half, build=True, mult=True, with_layer=True, bodies=(0, BODIES)):
                if mult and bodies[0] == 0:
                    open_agg(s - 1)
                    pe.wait_ge(counts_moved, s * SB_GROUPS + 2)
                    pe.sem_inc(pe_at, 1)
                with pe.Fori(*bodies) as b:
                    for k in range(BG):
                        if build:
                            G = (s * BODIES + b) * BG + (k + 1)
                            pe.wait_ge(hot_ready, G)
                            pe.wait_ge(counts_moved, G)
                            for c in range(CHUNKS):
                                ins = pe.matmul(cnt_ps[k % 2][:, 0:CODES], lane_hot[:, k % SLOTS, :, c],
                                                code_hot[:, k % SLOTS, :, c], start=(c == 0), stop=(c == CHUNKS - 1))
                            ins.then_inc(groups_summed, 1)
                        if mult and k < BH:
                            rhs = Asb(1 - half)[:, bass.ds(b * BH + k, 1), :].rearrange("p a n -> p (a n)")
                            l1 = X12[:, bass.ds(b * BH + k, 1), :].rearrange("p a n -> p (a n)")
                            l2 = X3[:, bass.ds(b * BH + k, 1), :].rearrange("p a n -> p (a n)")
                            pe.matmul(agg_ps[:, 0:SBN], l1, rhs, start=False, stop=True, skip_group_check=True)
                            pe.matmul(agg3_ps[0:F + 1, 0:SBN], l2, rhs, start=False, stop=True, skip_group_check=True)
                if mult and bodies[1] == BODIES:
                    pe.matmul(agg3_ps[0:F + 1, 0:SBN], zrow[:, 0:F + 1], zrow[:, 0:SBN], start=False, stop=True, skip_group_check=True).then_inc(agg_ready, 1)
                if with_layer and not (s == NSB and bodies[1] == BODIES if isinstance(s, int) else False):
                    layer(s - 2, half)

            turn_windows(0)
            superblock(0, 0, mult=False, with_layer=False)
            turn_windows(1)
            superblock(1, 1, with_layer=False)
            pe.wait_ge(w_in, 64)
            pe.wait_ge(x_ones, 1)
            superblock(2, 0)
            turn_windows(2)
            superblock(3, 1)
            with pe.Fori(2, PAIRS) as pair:
                superblock(pair * 2, 0)
                turn_windows(pair + 1)
                superblock(pair * 2 + 1, 1)
            superblock(NSB, 0, build=False, bodies=(0, 3))
            superblock(NSB, 0, build=False, bodies=(3, BODIES))
            layer(NSB - 1, 1)

            pe.wait_ge(w2_in, 16 * 18)
            pe.wait_ge(ones_set, 5)
            pe.wait_ge(h_ready, NSB)
            pe.wait_ge(chk_made, 1)
            pe.matmul(t2_ps[0:1, 0:1], chk[0:CH, 0:1], ones_c[0:CH, :], start=True, stop=True, skip_group_check=True).then_inc(chk_sum, 1)
            pe.transpose(t_ps[0:F, 0:F], W1bs[:, :], ident[0:F, 0:F])
            pe.matmul(v_ps[0:F, 0:1], W1bs[:, :], shift_b[:, 0:1], start=True, stop=True, skip_group_check=True).then_inc(wt_turned, 1)
            pe.wait_ge(wts_made, 1)
            pe.wait_ge(flags, 1)
            pe.matmul(t2_ps[0:CH, 0:F], u0b[:, :], W2au[:, :], start=True, stop=True)
            pe.matmul(t2_ps[0:CH, F:2 * F], shift_b[:, :], W2bs[:, :], start=True, stop=True, skip_group_check=True)
            pe.wait_ge(wt_moved, 1)
            pe.wait_ge(wts_made, 2)
            pe.matmul(t2_ps[0:F + 1, 2 * F:3 * F], WbT[:, :], W2am[:, :], start=True, stop=True, skip_group_check=True).then_inc(wts_ready, 1)
            pe.wait_ge(wts_made, 5)

            def sums2(s, half, m=None):
                if not isinstance(s, int) or s > 0:
                    pe.wait_ge(agg2_moved, s)
                pe.matmul(agg_ps[:, 0:SBN], zrow[:, 0:P], zrow[:, 0:SBN], start=True, stop=False, skip_group_check=True)
                if isinstance(s, int) and s < 2:
                    pe.wait_ge(counts_moved, NSB * SB_GROUPS + 2)
                elif isinstance(s, int):
                    pe.wait_ge(A_in[half], s // 2 * 16)
                else:
                    pe.wait_ge(A_in[half], (s - half) * 8)
                if isinstance(s, int) and s == 0:
                    for part in (2, 0, 1):
                        pe.wait_ge(part_in[part], 16)
                        for blk in range(EARLY):
                            pe.matmul(agg_ps[:, 0:SBN], Hsb[:, part, blk, :], Asb(half)[:, blk, :], start=False, stop=True, skip_group_check=True)
                    pe.wait_ge(parts_in, 48)
                    for blk in range(EARLY, SRC_BLOCKS):
                        for part in range(3):
                            ins = pe.matmul(agg_ps[:, 0:SBN], Hsb[:, part, blk, :], Asb(half)[:, blk, :], start=False, stop=True, skip_group_check=True)
                    ins.then_inc(agg2_ready, 1)
                    return
                for b in range(BODIES):
                    for blk in range(b * BH, (b + 1) * BH):
                        for part in range(3):
                            ins = pe.matmul(agg_ps[:, 0:SBN], Hsb[:, part, blk, :], Asb(half)[:, blk, :], start=False,
                                            stop=(part == 2), skip_group_check=True)
                    if b == BODIES - 1:
                        ins.then_inc(agg2_ready, 1)
                    if m is not None:
                        layer2(m, b, 1 - half)

            def layer2(m, b, half, arrived=None):
                chunks = [slice(c * CH, (c + 1) * CH) for c in range(NCH)]
                if b == 0:
                    pe.wait_ge(gl_in, arrived) if arrived is not None else pe.wait_ge(hx_in[half], (m - half) * 16 + 32 + 16 * half)
                    for c in range(NCH):
                        ins = pe.transpose(t_ps[:, chunks[c]], h1m[half][:, c, :], ident[0:CH, 0:CH])
                    ins.then_inc(hT_turned, 1)
                    pe.wait_ge(agg2_moved, m + 1)
                    for c in range(NCH):
                        ins = pe.matmul(u_ps[0:CH, c * H:(c + 1) * H], g2S[:, chunks[c]], Wl2s[:, :], start=True, stop=True)
                    ins.then_inc(u2_ready, 1)
                if b == 1:
                    pe.wait_ge(hT_moved, m + 1)
                    for c in range(NCH):
                        ins = pe.matmul(v_ps[0:CH, c * H:(c + 1) * H], hTs[:, chunks[c]], Wr2s[:, :], start=True, stop=True)
                    ins.then_inc(v2_ready, 1)
                if b == 2:
                    pe.wait_ge(h2_ready, m + 1)
                    for c in range(NCH):
                        ins = pe.transpose(t2_ps[:, chunks[c]], hs[:, c, :], ident[0:CH, 0:CH])
                    ins.then_inc(h2_turned, 1)
                if b == 3:
                    pe.wait_ge(h2_moved, m + 1)
                    for c in range(NCH):
                        ins = pe.matmul(cnt_ps[0][0:CH, c * F:(c + 1) * F], h2T[:, chunks[c]], Wouts[:, :], start=True, stop=True)
                    ins.then_inc(o_ready, 1)
                if b == 5:
                    pe.wait_ge(x2_ready, m + 3)
                    pe.sem_inc(pe_at, 1)
                    for c in range(NCH):
                        ins = pe.transpose(cnt_ps[1][0:F, chunks[c]], x2c[:, c, :], ident[0:CH, 0:CH])
                    ins.then_inc(x2_turned, 1)
                if b == 6:
                    pe.wait_ge(x2_moved, m + 1)
                    for c in range(NCH):
                        ins = pe.matmul(agg3_ps[0:CH, c * 2 * F:(c + 1) * 2 * F], x2T[:, chunks[c]], Wxx[:, :], start=True, stop=True)
                    ins.then_inc(pq_ready, 1)

            sums2(0, 0)
            sums2(1, 1, 0)
            sums2(2, 0, 1)
            with pe.Fori(1, PAIRS - 1) as j:
                sums2(j * 2 + 1, 1, j * 2)
                sums2(j * 2 + 2, 0, j * 2 + 1)
            sums2(NSB - 1, 1, NSB - 2)
            for b in range(BODIES):
                layer2(NSB - 1, b, 1)

            left = pe.value_load(flag_i[0:1, 0:1], min_val=0, max_val=1)
            with pe.If_ne(pe.to_reg(left), 0):
                general_begins(pe)
                pe.wait_ge(x_ones, 2)
                with pe.Fori(0, NSB) as m:
                    layer(m + NSB, 0, m * 32 + 32)
                with pe.Fori(0, NSB) as m:
                    for b in range(BODIES):
                        layer2(m + NSB, b, 0, m * 48 + 48 + 32 * NSB)
                general_ends(pe)

            pe.wait_ge(base_made, 1)
            pe.matmul(t2_ps[:, 0:NEG], ones_r[:, :], base_f[:, :], start=True, stop=True).then_inc(bases_ready, 1)

            pe.wait_ge(chkB_made, 3)
            pe.matmul(t2_ps[0:1, 0:1], chk[:, 7:8], ones_c[:, :], start=True, stop=True).then_inc(chkB_sum, 1)

            def edge_group(g, k, z_ps, s_ps, first=False):
                if isinstance(g, int):
                    pe.wait_ge(attr_in[k], 16 * (g // NB + 1) + (16 if g == NEG - 1 else 0))
                else:
                    pe.wait_ge(attr_in[k], g_round * 16 + 16)
                if not first:
                    pe.wait_ge(attr_moved, g)
                for c in range(EJ // 2):
                    ins = pe.transpose(t_ps[:, c * P:(c + 1) * P], attr[k][:, c * P:(c + 1) * P], ident[:, :])
                ins.then_inc(attr_turned, 1)
                pe.wait_ge(attr_moved, g + 1)
                for c in range(EJ // 2):
                    ins = pe.matmul(z_ps[:, c * P:(c + 1) * P], attrT[k][:, c * P:(c + 1) * P], Wedge[:, :], start=True, stop=True)
                ins.then_inc(z_ready, 1)
                pe.wait_ge(msg_made, g + 1)
                for j in range(EJ):
                    ins = pe.matmul(s_ps[0:F + 1, 0:WIN], msg[k][:, j, :], hot[k][:, j, :], start=(j == 0), stop=(j == EJ - 1))
                ins.then_inc(seg_ready, 1)

            zb, sbk = [cnt_ps[0], cnt_ps[1], agg_ps], [agg3_ps, u_ps, v_ps]
            pe.wait_ge(p_ready, NSB)
            for k in range(NB):
                edge_group(k, k, zb[k], sbk[k], first=(k == 0))
            with pe.Fori(1, (NEG - 1) // NB) as r:
                g_round = r
                for k in range(NB):
                    edge_group(r * NB + k, k, zb[k], sbk[k])
            edge_group(NEG - 1, 0, zb[0], sbk[0])

            left = pe.value_load(flag_i[0:1, 1:2], min_val=0, max_val=1)
            with pe.If_ne(pe.to_reg(left), 0):
                edges_end(pe)

                def general_messages(g, arrived):
                    pe.wait_ge(ge_in, arrived)
                    for c in range(EJ // 2):
                        ins = pe.transpose(t_ps[:, c * P:(c + 1) * P], attr[0][:, c * P:(c + 1) * P], ident[:, :])
                    ins.then_inc(ge_turned, 1)
                    pe.wait_ge(ge_moved, g + 1)
                    for c in range(EJ // 2):
                        ins = pe.matmul(cnt_ps[0][:, c * P:(c + 1) * P], attrT[0][:, c * P:(c + 1) * P], Wedge[:, :], start=True, stop=True)
                    ins.then_inc(ge_z, 1)
                    pe.wait_ge(ge_msg, g + 1)
                    for j in range(EJ):
                        ins = pe.transpose((u_ps, v_ps)[j // 4][0:F + 1, (j % 4) * P:(j % 4 + 1) * P], msg[0][:, j, :], ident[:, :])
                    ins.then_inc(ge_msgT, 1)
                with pe.Fori(0, NEG - 1) as g:
                    general_messages(g, g * 32 + 32)
                general_messages(NEG - 1, NEG * 32 + 16)
                pe.wait_ge(ge_added, NEG + 1)

            chunks = [slice(c * CH, (c + 1) * CH) for c in range(NCH)]
            pe.wait_ge(acc_added, NEG)

            def sums_times(j):
                pe.wait_ge(accS_moved, j + 1)
                if not isinstance(j, int) or j > 0:
                    pe.wait_ge(zm_made, j)
                for c in range(2 * NCH):
                    ins = pe.matmul(u_ps[0:CH, c * F:(c + 1) * F], accS[:, c * CH:(c + 1) * CH], Wc[:, :], start=True, stop=True)
                ins.then_inc(m_ready, 1)

            def turn_msg(j):
                if not isinstance(j, int) or j > 0:
                    pe.wait_ge(msg4_moved, j * 2)
                pe.wait_ge(msg4_made, j + 1)
                pe.sem_inc(pe_at, 1)
                for c in range(2 * NCH):
                    ins = pe.transpose((t_ps, t2_ps)[c // NCH][0:F, chunks[c % NCH]], msg4[:, c * F:(c + 1) * F], ident[0:CH, 0:CH])
                ins.then_inc(msg4_turned, 1)

            def last_product(j):
                pe.wait_ge(msg4_moved, j * 2 + 2)
                pe.wait_ge(y_kept, j + 1)
                for c in range(2 * NCH):
                    ins = pe.matmul(v_ps[0:CH, c * F:(c + 1) * F], msgT4[:, c * CH:(c + 1) * CH], W2bs[:, :], start=True, stop=True)
                ins.then_inc(y_ready, 1)

            pe.sem_inc(y_ready, 1)
            sums_times(0)
            sums_times(1)
            turn_msg(0)
            with pe.Fori(0, PAIRS - 2) as j:
                sums_times(j + 2)
                last_product(j)
                turn_msg(j + 1)
            last_product(PAIRS - 2)
            turn_msg(PAIRS - 1)
            last_product(PAIRS - 1)

        @block.vector
        def _(dve):
            n0 = [0]

            def step(ins):
                n0[0] += 1
                ins.then_inc(dve0, 1)
                dve.wait_ge(dve0, n0[0])

            dve.sem_inc(x2_ready, 2)
            dve.memset(xTs[F:F + 1, :], 1.0).then_inc(x_ones, 1)
            dve.wait_ge(dst_in, 32)
            dve.tensor_copy(f16, dst_i.rearrange("p (r c) -> p r c", c=ROW)[:, :, 0]).then_inc(firsts_made, 1)
            step(dve.tensor_scalar(grp_i, dst_i, 3, None, ALU.arith_shift_right))
            dve.wait_ge(src_in, 32)
            dve.tensor_scalar(lane_i, src_i, P - 1, None, ALU.bitwise_and).then_inc(lane_made, 1)
            dve.tensor_scalar(blk_i, src_i, 7, None, ALU.arith_shift_right).then_inc(dve0, 1)
            n0[0] += 1
            step(dve.scalar_tensor_tensor(code_a, grp_i, float(CODES - GROUP), dst_i, ALU.mult, ALU.add))
            r3 = lambda ap: ap.rearrange("p (r c) -> p r c", c=ROW)
            step(dve.scalar_tensor_tensor(comb[:, :, ROW:2 * ROW], r3(blk_i), float(GROUP), r3(code_a), ALU.mult, ALU.add))
            dve.sem_inc(table_made, 1)
            dve.wait_ge(iota_set, 9)
            dve.wait_ge(firsts_in, 16)
            for n in range(8):
                step(dve.tensor_scalar(junk, coarse, thr[:, n:n + 1], None, ALU.is_lt, ALU.add, accum_out=below[:, n:n + 1]))
            dve.tensor_scalar(part_of[:, :], below[:, :], -1.0, 0.0, ALU.add, ALU.max).then_inc(parts_found, 1)
            step(dve.tensor_scalar(part_row[:, :], below[:, :], -1.0, 0.0, ALU.add, ALU.max))
            step(dve.tensor_scalar(part_row[:, :], part_row[:, :], float(RPP), -1.0, ALU.mult, ALU.add))

            def find_windows(n, first=False):
                dve.tensor_scalar(junk[:, 0:RPP], fine[:, bass.ds(n, 1), :].rearrange("p a r -> p (a r)"), thr[:, bass.ds(n, 1)], None, ALU.is_lt, ALU.add,
                                  accum_out=below[:, bass.ds(n, 1)]).then_inc(win_dve, 1)
                dve.wait_ge(win_dve, n * 2 + 1)
                dve.tensor_scalar(start[:, bass.ds(n, 1)], below[:, bass.ds(n, 1)], part_row[:, bass.ds(n, 1)], 0.0, ALU.add, ALU.max).then_inc(win_dve, 1)
                dve.wait_ge(win_dve, n * 2 + 2)
                if not first:
                    dve.wait_ge(win_in, n * (16 * WROWS))
                dve.tensor_scalar(rows12[:, 0, :], iota_w[:, 0:WROWS], start[:, bass.ds(n, 1)], None, ALU.add).then_inc(rows_ready, 1)

            def rel_windows(n):
                dve.wait_ge(win_in, (n + 1) * (16 * WROWS))
                r4 = rel.rearrange("p a (r c) -> p a r c", c=ROW)
                dve.tensor_scalar(r4[:, 0], win[:, :, 0:ROW], 1.0, None, ALU.add).then_inc(rel_ready, 1)
                dve.tensor_scalar(r4[:, 1], win[:, :, ROW:2 * ROW], code0[:, bass.ds(n, 1)], 2040.0, ALU.subtract, ALU.min).then_inc(rel_ready, 1)

            def superblock(s, with_layer=True):
                with dve.Fori(0, BODIES) as b:
                    for k in range(0, BG, 2):
                        g = s * SB_GROUPS + b * BG + k
                        slots = slice(k % SLOTS, k % SLOTS + 2)
                        dve.wait_ge(groups_summed, g + 2)
                        for hot_rows, turned, n in ((lane_hot, laneT, P), (code_hot, codeT, CODES)):
                            ins = dve.tensor_tensor(hot_rows[:, slots], iota_code[:, 0:n, :].unsqueeze(1).to_broadcast([P, 2, n, CHUNKS]),
                                                    turned[:, bass.ds(g, 2), :].unsqueeze(2).to_broadcast([P, 2, n, CHUNKS]), ALU.is_equal)
                        ins.then_inc(hot_ready, 2)
                if with_layer:
                    layer(s - 2)

            def grid(ap, f):
                return ap[0:CH, 0:NCH * f].rearrange("p (c f) -> p c f", f=f)

            def wide(ap, f):
                return ap.unsqueeze(2).to_broadcast([CH, NCH, f])

            def every(ap, f):
                return ap.unsqueeze(1).to_broadcast([CH, NCH, f])

            def layer(m, at=None):
                general = at is not None
                at = m if at is None else at
                i = [0]

                def link(ins):
                    i[0] += 1
                    ins.then_inc(layer_dve, 1)
                    dve.wait_ge(layer_dve, m * 4 + i[0])
                dve.wait_ge(uv_ready, m + 1)
                link(dve.tensor_scalar(ctmp[:, :], t_ps[0:CH, SBN:SBN + NCH], 1.0, None, ALU.max))
                link(dve.reciprocal(inv_c[:, :], ctmp[:, :]))
                link(dve.tensor_tensor(ht[:, :, :], grid(u_ps, H), wide(inv_c[:, :], H), ALU.mult))
                dve.tensor_tensor(cnt_all[:, bass.ds(at, 1), :].rearrange("p a c -> p (a c)"), t_ps[0:CH, SBN:SBN + NCH], zero_c[:, :], ALU.add).then_inc(layer_dve, 1)
                if not isinstance(m, int) or m > 0:
                    dve.wait_ge(h_stored, m * 64)
                if general:
                    dve.tensor_tensor(hv[:, :, :], ht[:, :, :], grid(v_ps, H), ALU.add).then_inc(relu_made, 1)
                    dve.wait_ge(relu_made, at + 1)
                    dve.tensor_scalar(hs[:, :, :], hv[:, :, :], 0.0, None, ALU.max).then_inc(h_ready, 1)
                else:
                    dve.tensor_tensor(hs[:, :, :], ht[:, :, :], grid(v_ps, H), ALU.add).then_inc(h_ready, 1)

            dve.wait_ge(consts, 2)
            step(dve.memset(zero_c[:, :], 0.0))
            step(dve.tensor_scalar(code0[:, :], code0[:, :], float(CODES), -1.0, ALU.mult, ALU.add))
            dve.wait_ge(fine_in, 16 * 8)
            find_windows(0, True)
            dve.wait_ge(x1_made, 1)
            x3 = x_rows.rearrange("p (b f) -> p b f", f=F)
            xr = x_rest.rearrange("p (b f) -> p b f", f=F)
            step(dve.tensor_tensor(xr, x3, X12[:, :, 0:F], ALU.subtract))
            step(dve.tensor_copy(X12[:, :, F:2 * F], xr))
            step(dve.tensor_tensor(xr, xr, X12[:, :, F:2 * F], ALU.subtract))
            step(dve.tensor_copy(X3[:, :, 0:F], xr))
            rel_windows(0)
            find_windows(1)
            dve.wait_ge(win_moved, 2)
            superblock(0, False)
            rel_windows(1)
            superblock(1, False)
            with dve.Fori(1, PAIRS) as pair:
                find_windows(pair + 1)
                dve.wait_ge(win_moved, pair * 2 + 2)
                dve.sem_inc(dve_at, 1)
                superblock(pair * 2)
                rel_windows(pair + 1)
                superblock(pair * 2 + 1)
            layer(NSB - 2)
            layer(NSB - 1)

            all_counts = cnt_all[:, :, :].rearrange("p m c -> p (m c)")

            def inverses(i):
                dve.tensor_scalar(inv[:, :, :], cnt_all[:, :, :], 1.0, None, ALU.max).then_inc(inv_made, 1)
                dve.wait_ge(inv_made, 2 * i + 1)
                dve.reciprocal(inv[:, :, :], inv[:, :, :]).then_inc(inv_made, 1)
                dve.wait_ge(inv_made, 2 * i + 2)
            dve.wait_ge(layer_dve, 4 * NSB)
            inverses(0)
            dve.tensor_reduce(chk[0:CH, 0:1], all_counts, AX_X, ALU.add).then_inc(chk_made, 1)
            dve.wait_ge(chk_sum, 1)
            dve.tensor_scalar(flag_i[0:1, 0:1], t2_ps[0:1, 0:1], float(E), None, ALU.not_equal).then_inc(flags, 1)

            dve.wait_ge(w2_in, 16 * 18)
            dve.tensor_scalar(u0b[:, :], shift_b[:, :], 0.0, u0[:, 0:1], ALU.mult, ALU.add).then_inc(wts_made, 1)
            dve.wait_ge(wt_turned, 1)
            dve.tensor_tensor(WbT[:, F:F + 1], v_ps[0:F, 0:1], b1bcol[:, :], ALU.add).then_inc(wts_made, 1)
            dve.wait_ge(wts_ready, 1)
            dve.tensor_tensor(c2[:, :], t2_ps[0:CH, 0:F], b2as[:, :], ALU.add).then_inc(wts_made, 1)
            dve.tensor_copy(Wc[:, :], t2_ps[0:F + 1, 2 * F:3 * F]).then_inc(wts_made, 1)
            dve.tensor_scalar(W2bs[:, :], W2bs[:, :], SCALE, None, ALU.mult).then_inc(wts_made, 1)
            step(dve.tensor_tensor(b2bs[:, :], t2_ps[0:CH, F:2 * F], b2bs[:, :], ALU.add))

            def normalise(link, to, var, std, m):
                link(dve.tensor_reduce(st[:, 0, :], yv[:, :, :], AX_X, ALU.add))
                link(dve.tensor_scalar(st[:, 1, :], st[:, 0, :], -1.0 / F, None, ALU.mult))
                link(dve.tensor_tensor(yd[:, :, :], yv[:, :, :], wide(st[:, 1, :], F), ALU.add))
                link(dve.tensor_tensor(yv[:, :, :], yd[:, :, :], yd[:, :, :], ALU.mult))
                dve.tensor_reduce(st[:, 2, :], yv[:, :, :], AX_X, ALU.add).then_inc(var, 1)
                dve.wait_ge(std, m + 1)
                link(dve.reciprocal(st[:, 0, :], st[:, 3, :]))

            def layer2(m, half, at=None):
                i = [0]
                at = m if at is None else at

                def link(ins):
                    i[0] += 1
                    ins.then_inc(dve2, 1)
                    dve.wait_ge(dve2, m * 11 + i[0])
                dve.wait_ge(u2_ready, m + 1)
                link(dve.tensor_tensor(inv_c[:, :], inv[:, bass.ds(at, 1), :].rearrange("p a c -> p (a c)"), zero_c[:, :], ALU.add))
                link(dve.tensor_tensor(ht[:, :, :], grid(u_ps, H), wide(inv_c[:, :], H), ALU.mult))
                dve.wait_ge(v2_ready, m + 1)
                link(dve.tensor_tensor(hv[:, :, :], grid(v_ps, H), every(bl2s[:, :], H), ALU.add))
                link(dve.tensor_tensor(ht[:, :, :], ht[:, :, :], hv[:, :, :], ALU.add))
                dve.tensor_scalar(hs[:, :, :], ht[:, :, :], 0.0, None, ALU.max).then_inc(h2_ready, 1)
                dve.wait_ge(o_ready, m + 1)
                link(dve.tensor_tensor(yd[:, :, :], grid(cnt_ps[0], F), every(bouts[:, :], F), ALU.add))
                link(dve.tensor_tensor(yv[:, :, :], yd[:, :, :], xm[:, half, :, :], ALU.add))
                normalise(link, None, var_ready, std_ready, m)
                if not isinstance(m, int) or m > 0:
                    dve.wait_ge(x2_kept, m)
                dve.tensor_tensor(x2c[:, :, :], yd[:, :, :], wide(st[:, 0, :], F), ALU.mult).then_inc(x2_ready, 1)
                dve.wait_ge(pq_ready, m + 1)
                pq = grid(agg3_ps, 2 * F)
                dve.tensor_tensor(q2all[:, bass.ds(at, 1), :, :].rearrange("p a c f -> p (a c) f"), pq[:, :, F:2 * F], every(c2[:, :], F), ALU.add)
                if not isinstance(m, int) or m > 0:
                    dve.wait_ge(p_stored, m * 16)
                dve.tensor_tensor(pc[:, :, :], pq[:, :, 0:F], every(b1as[:, :], F), ALU.add).then_inc(p_ready, 1)

            dve.wait_ge(hx_in[0], 32)
            layer2(0, 0, NSB - 2)
            dve.wait_ge(hx_in[1], 48)
            layer2(1, 1, NSB - 1)
            with dve.Fori(1, PAIRS) as j:
                dve.wait_ge(hx_in[0], j * 32 + 32)
                layer2(j * 2, 0, j * 2 - 2)
                dve.wait_ge(hx_in[1], j * 32 + 48)
                layer2(j * 2 + 1, 1, j * 2 - 1)

            def general_sums(rows, i):
                dve.wait_ge(g_set, 2 * i + 2)
                dve.wait_ge(feat_in, 16 * (N // GN) * (i + 1))
                with dve.Fori(0, E // GE) as c:
                    dve.wait_ge(ends_in, c * 32 + 32 * (i * (E // GE) + 1))
                    dve.sem_inc(dve_at, 1)
                    with dve.Fori(0, GE) as e:
                        of = dve.value_load(ends[0:1, 0, bass.ds(e, 1)], min_val=0, max_val=N - 1)
                        to = dve.value_load(ends[0:1, 1, bass.ds(e, 1)], min_val=0, max_val=N - 1)
                        dve.tensor_tensor(sumT[0:rows, bass.ds(to, 1)], sumT[0:rows, bass.ds(to, 1)],
                                          featT[0:rows, bass.ds(of, 1)], ALU.add).then_inc(col_added, 1)
                        dve.wait_ge(col_added, c * GE + (e + (i * E + 1)))
                        dve.sem_inc(dve_at, 1)
                    dve.sem_inc(chunk_added, 1)
                dve.sem_inc(sums_done, 1)

            dve.wait_ge(flags, 1)
            left = dve.value_load(flag_i[0:1, 0:1], min_val=0, max_val=1)
            with dve.If_ne(dve.to_reg(left), 0):
                general_begins(dve)
                dve.memset(xTs[F:F + 1, :], 1.0).then_inc(x_ones, 1)
                dve.sem_inc(chunk_added, 1)
                general_sums(F + 1, 0)
                with dve.Fori(0, NSB) as m:
                    layer(m + NSB, m)
                dve.wait_ge(layer_dve, 2 * 4 * NSB)
                inverses(1)
                general_sums(H, 1)
                with dve.Fori(0, NSB) as m:
                    layer2(m + NSB, 0, m)
                general_ends(dve)

            dve.wait_ge(base_in, 32)
            dve.wait_ge(edges_in, 96)
            dve.tensor_copy(base_f[:, :], base_i[:, :]).then_inc(base_made, 1)
            dve.wait_ge(bases_ready, 1)
            dve.tensor_tensor(drel, dst_e, t2_ps[:, 0:NEG].unsqueeze(2).to_broadcast([P, NEG, EJ]), ALU.subtract).then_inc(drel_made, 1)
            dve.wait_ge(drel_made, 1)
            flat = drel.rearrange("p g j -> p (g j)")
            dve.tensor_scalar(in_window, flat, 0.0, None, ALU.is_ge, ALU.add, accum_out=chk[:, 5:6]).then_inc(chkB_made, 1)
            dve.wait_ge(chkB_made, 1)
            dve.tensor_scalar(in_window, flat, float(WIN), None, ALU.is_ge, ALU.add, accum_out=chk[:, 6:7]).then_inc(chkB_made, 1)
            dve.wait_ge(chkB_made, 2)
            dve.tensor_tensor(chk[:, 7:8], chk[:, 5:6], chk[:, 6:7], ALU.subtract).then_inc(chkB_made, 1)
            dve.wait_ge(chkB_sum, 1)
            dve.tensor_scalar(flag_i[0:1, 1:2], t2_ps[0:1, 0:1], float(E), None, ALU.not_equal).then_inc(flagB, 1)
            dve.wait_ge(acc_zero, 1 + NB)

            dve.wait_ge(x2_kept, NSB)
            step(dve.tensor_tensor(y_all, y_all, b2bs[:, :].unsqueeze(1).to_broadcast([CH, NSB * NCH, F]), ALU.add))

            def edge_group(g, k, z_ps, last=None, r=None, first=False):
                dve.wait_ge(gath_in[k], (g // NB + 1) * (16 * EJ) if isinstance(g, int) else r * (16 * EJ) + 16 * EJ)
                dve.wait_ge(z_ready, g + 1)
                if not first:
                    dve.wait_ge(selu_act, g * 2)
                dve.tensor_tensor(zs, z_ps[:, 0:EJ * F], gath[k], ALU.add).then_inc(z_made, 1)
                if not first:
                    dve.wait_ge(seg_ready, g)
                dve.tensor_tensor(hot[k], iota_w[:, :].unsqueeze(1).to_broadcast([P, EJ, WIN]),
                                  drel[:, bass.ds(g, 1), :].rearrange("p a j -> p (a j)").unsqueeze(2).to_broadcast([P, EJ, WIN]),
                                  ALU.is_equal).then_inc(hot_made, 1)
                if last is not None:
                    last()
                dve.wait_ge(selu_act, g * 2 + 2)
                e3, r3 = (b.rearrange("p (j f) -> p j f", f=F) for b in (ex, rl))
                dve.scalar_tensor_tensor(msg[k][:, :, 0:F], e3, ALPHA, r3, ALU.min, ALU.add).then_inc(msg_made, 1)

            def add_sums(g, s_ps, first=False):
                dve.wait_ge(seg_ready, g + 1)
                if not first:
                    dve.wait_ge(acc_added, g)
                base = dve.value_load(base_i[0:1, bass.ds(g, 1)], min_val=0, max_val=N - 1)
                win_acc = acc[:, bass.ds(base, WIN)]
                dve.tensor_tensor(win_acc, win_acc, s_ps[0:F + 1, 0:WIN], ALU.add).then_inc(acc_added, 1)

            zb, sbk = [cnt_ps[0], cnt_ps[1], agg_ps], [agg3_ps, u_ps, v_ps]
            edge_group(0, 0, zb[0], first=True)
            edge_group(1, 1, zb[1], lambda: add_sums(0, sbk[0], True))
            edge_group(2, 2, zb[2], lambda: add_sums(1, sbk[1]))
            with dve.Fori(1, (NEG - 1) // NB) as r:
                for k in range(NB):
                    edge_group(r * NB + k, k, zb[k], lambda: add_sums(r * NB + (k - 1), sbk[(k - 1) % NB]), r)
            edge_group(NEG - 1, 0, zb[0], lambda: add_sums(NEG - 2, sbk[2]))
            add_sums(NEG - 1, sbk[0])

            dve.wait_ge(flagB, 1)
            left = dve.value_load(flag_i[0:1, 1:2], min_val=0, max_val=1)
            with dve.If_ne(dve.to_reg(left), 0):
                edges_end(dve)
                dve.sem_inc(ge_added, 1)
                dve.wait_ge(ge_zero, 1)

                def general_edges(g, arrived):
                    dve.wait_ge(ge_rows, g * 16 * EJ + 16 * EJ)
                    dve.wait_ge(ge_z, g + 1)
                    dve.tensor_tensor(zs, cnt_ps[0][:, 0:EJ * F], gath[0], ALU.add).then_inc(ge_zs, 1)
                    dve.wait_ge(ge_selu, g * 2 + 2)
                    e3, r3 = (b.rearrange("p (j f) -> p j f", f=F) for b in (ex, rl))
                    dve.scalar_tensor_tensor(msg[0][:, :, 0:F], e3, ALPHA, r3, ALU.min, ALU.add).then_inc(ge_msg, 1)
                    dve.wait_ge(ge_msgT, g + 1)
                    dve.wait_ge(ge_in, arrived)
                    dve.sem_inc(dve_at, 1)
                    with dve.Fori(0, P) as e:
                        for j in range(EJ):
                            to = dve.value_load(dst_row[0:1, bass.ds(e * EJ + j, 1)], min_val=0, max_val=N + WIN - 1)
                            dve.tensor_tensor(acc[:, bass.ds(to, 1)], acc[:, bass.ds(to, 1)],
                                              (u_ps, v_ps)[j // 4][0:F + 1, bass.ds(e + (j % 4) * P, 1)], ALU.add).then_inc(ge_col, 1)
                            dve.wait_ge(ge_col, g * EG + (e * EJ + (j + 1)))
                            dve.sem_inc(dve_at, 1)
                    dve.sem_inc(ge_added, 1)
                with dve.Fori(0, NEG - 1) as g:
                    general_edges(g, g * 32 + 32)
                general_edges(NEG - 1, NEG * 32 + 16)

            def pair4(ap):
                return ap.rearrange("p (c f) -> p c f", f=F)

            def chunks4(ap, j):
                return ap[:, bass.ds(j * (2 * NCH), 2 * NCH), :]

            def first_half(j):
                dve.wait_ge(m_ready, j + 1)
                dve.sem_inc(dve_at, 1)
                inv2 = inv[:, bass.ds(j * 2, 2), :].rearrange("p a c -> p (a c)").unsqueeze(2).to_broadcast([CH, 2 * NCH, F])
                dve.tensor_tensor(pair4(zm4), pair4(u_ps[0:CH, :]), inv2, ALU.mult).then_inc(zm_made, 1)
                dve.wait_ge(zm_made, j + 1)
                dve.tensor_tensor(pair4(yv4), pair4(zm4), chunks4(sq_all, j), ALU.add).then_inc(zq_made, 1)

            def make_msg(j):
                dve.wait_ge(selu4, j * 2 + 2)
                if not isinstance(j, int) or j > 0:
                    dve.wait_ge(msg4_turned, j)
                dve.scalar_tensor_tensor(msg4, ex4, ALPHA, rl4, ALU.min, ALU.add).then_inc(msg4_made, 1)

            def second_half(j):
                dve.wait_ge(y_ready, j + 2)
                dve.tensor_tensor(chunks4(y_all, j), pair4(v_ps[0:CH, :]), chunks4(y_all, j), ALU.add).then_inc(y_kept, 1)

            dve.sem_inc(y_kept, 1)
            first_half(0)
            make_msg(0)
            first_half(1)
            with dve.Fori(0, PAIRS - 2) as j:
                make_msg(j + 1)
                first_half(j + 2)
                second_half(j)
            make_msg(PAIRS - 1)
            second_half(PAIRS - 2)
            second_half(PAIRS - 1)
            dve.wait_ge(y_kept, PAIRS + 1)

            def wide4(ap):
                return ap.unsqueeze(2).to_broadcast([CH, HALF4, F])
            for i, a in enumerate(HALVES4):
                step(dve.tensor_reduce(st4[:, 0, a], y_all[:, a, :], AX_X, ALU.add))
                step(dve.tensor_scalar(st4[:, 1, a], st4[:, 0, a], -1.0 / F, None, ALU.mult))
                dve.tensor_tensor(y_all[:, a, :], y_all[:, a, :], wide4(st4[:, 1, a]), ALU.add).then_inc(centred4, 1)
            for i, a in enumerate(HALVES4):
                dve.wait_ge(centred4, i + 1)
                dve.wait_ge(squared4, i + 1)
                dve.tensor_reduce(st4[:, 1, a], sq_all[:, a, :], AX_X, ALU.add).then_inc(var4, 1)
            for i, a in enumerate(HALVES4):
                dve.wait_ge(std4, i + 1)
                step(dve.reciprocal(st4[:, 0, a], st4[:, 2, a]))
                dve.tensor_tensor(y_all[:, a, :], y_all[:, a, :], wide4(st4[:, 0, a]), ALU.mult).then_inc(row_made, 1)


_INS = ['x', 'src', 'dst', 'edge_attr_64', 'L0_gnn_W_l1', 'L0_gnn_b_l1', 'L0_gnn_W_r1', 'L0_gnn_W_l2', 'L0_gnn_b_l2',
        'L0_gnn_W_r2', 'L0_gnn_W_out', 'L0_gnn_b_out', 'L1_gnn_u', 'L1_gnn_W1a', 'L1_gnn_b1a', 'L1_gnn_W1b',
        'L1_gnn_b1b', 'L1_gnn_W2a', 'L1_gnn_b2a', 'L1_gnn_W2b', 'L1_gnn_b2b']


def kernel(**inputs):
    import numpy as _np
    import concourse.bacc as _bacc
    from concourse import mybir as _mybir
    from concourse.bass_utils import run_bass_kernel_spmd as _run

    nc = _bacc.Bacc("TRN2", target_bir_lowering=False, num_devices=1)
    arrays, args = {}, []
    for name in _INS:
        a = _np.ascontiguousarray(inputs[name])
        arrays[f"in_{name}_dram"] = a
        args.append(nc.dram_tensor(f"in_{name}_dram", a.shape, _mybir.dt.from_np(a.dtype), kind="ExternalInput").ap())
    out = nc.dram_tensor("out_0_dram", (N, F), F32, kind="ExternalOutput").ap()
    build(nc, *args, out)
    r = _run(nc, [arrays], core_ids=[0])
    return r.results[0]["out_0_dram"]
```
